# Optimizing a Trainium2 kernel written in Bass

```python
import numpy as np
import jax
import jax.numpy as jnp

def _softmax(x, axis=-1):
    return jax.nn.softmax(x, axis=axis)
def _gelu(x):
    return jax.nn.gelu(x, approximate=True)
def _silu(x):
    return jax.nn.silu(x)
def _sigmoid(x):
    return jax.nn.sigmoid(x)
def _layernorm(x, axis=-1, eps=1e-5):
    m = jnp.mean(x, axis=axis, keepdims=True)
    v = jnp.var(x, axis=axis, keepdims=True)
    return (x - m) / jnp.sqrt(v + eps)
def _scatter_add(tgt, idx, src, axis=0):
    return tgt.at[idx].add(src)
def _segment_sum(src, seg, n):
    return jax.ops.segment_sum(src, seg, n)

kernel_name = 'mk_adj_ffn_d2_adj_256_ed3f42'

def setup_inputs(seed: int = 0):
    np.random.seed(seed)
    _w = jnp.asarray
    def _rec_inputs():
        import jax
        import jax.numpy as jnp
        _gk = jax.random.key(seed)
        x = -0.0002928 + 1 * jax.random.normal(jax.random.fold_in(_gk, 1), (128, 64, 256), jnp.float32)
        _a = jax.random.bernoulli(jax.random.fold_in(_gk, 2), 0.125, (128, 64, 64))
        _a = jnp.logical_or(_a, jnp.swapaxes(_a, -1, -2))
        _a = jnp.logical_or(_a, jnp.eye(64, dtype=bool))
        _af = _a.astype(jnp.float32)
        _af = _af * jax.random.uniform(jax.random.fold_in(_gk, 3), (128, 64, 64), jnp.float32, 0.05, 1)
        adj = _af
        return x, adj
    x, adj = _rec_inputs()
    def _L0_gnn_setup():
        import jax, jax.numpy as jnp
        import numpy as np
        SPARSITY = 0.01

        def quantize(weight, s):
            pos = (weight > s).astype(weight.dtype)
            neg = (weight < -s).astype(weight.dtype)
            return (pos - neg) * s
        key = jax.random.key(seed)
        k1, k2, k3 = jax.random.split(key, 3)
        B, N, Din, Dout = (8, 2048, 256, 256)
        x = jax.random.normal(k1, (B, N, Din), dtype=jnp.float32)
        adj = jax.random.uniform(k2, (B, N, N), dtype=jnp.float32)
        limit = float(np.sqrt(6.0 / (Din + Dout)))
        weight = jax.random.uniform(k3, (Din, Dout), dtype=jnp.float32, minval=-limit, maxval=limit)
        bias = jnp.zeros((Dout,), dtype=jnp.float32)
        return {'x': x, 'adj': adj, 'weight': weight, 'bias': bias}
    _L0_gnn_all = _L0_gnn_setup()
    _L0_gnn_in = {k: v for k, v in _L0_gnn_all.items() if k in ('weight', 'bias', )}
    del _L0_gnn_all

    def _L0_ffn_setup():
        import jax, jax.numpy as jnp
        import numpy as np
        C = 256
        HID = 1024
        E = 8
        TEMP = 1.0
        key = jax.random.key(seed)
        ks = jax.random.split(key, 7)
        x = jax.random.normal(ks[0], (8, 16384, C), dtype=jnp.float32)
        W1 = jax.random.normal(ks[1], (C, HID), dtype=jnp.float32) * 0.02
        b1 = jnp.zeros((HID,), dtype=jnp.float32)
        Wg = jax.random.normal(ks[2], (HID, E), dtype=jnp.float32) * 0.02
        bg = jnp.zeros((E,), dtype=jnp.float32)
        Wd = jax.random.normal(ks[3], (E, HID, C), dtype=jnp.float32) * 0.02
        bd = jnp.zeros((E, C), dtype=jnp.float32)
        return {'x': x, 'W1': W1, 'b1': b1, 'Wg': Wg, 'bg': bg, 'Wd': Wd, 'bd': bd}
    _L0_ffn_all = _L0_ffn_setup()
    _L0_ffn_in = {k: v for k, v in _L0_ffn_all.items() if k in ('W1', 'b1', 'Wg', 'bg', 'Wd', 'bd', )}
    del _L0_ffn_all

    def _L1_gnn_setup():
        import jax, jax.numpy as jnp
        import numpy as np
        B, N, IN_DIM, OUT_DIM, H = (8, 1024, 256, 256, 4)
        D = OUT_DIM // H
        NEG_INF = -9000000000000000.0
        LRELU_SLOPE = 0.2
        key = jax.random.key(seed)
        k1, k2, k3, k4 = jax.random.split(key, 4)
        x = jax.random.normal(k1, (B, N, IN_DIM), dtype=jnp.float32)
        adj = jax.random.randint(k2, (B, N, N), 0, 2).astype(jnp.float32)
        W = jax.random.normal(k3, (IN_DIM, H * D), dtype=jnp.float32) * jnp.sqrt(2.0 / (IN_DIM + H * D))
        a = jax.random.normal(k4, (H, 2 * D), dtype=jnp.float32) * jnp.sqrt(2.0 / (H + 2 * D))
        return {'x': x, 'adj': adj, 'W': W, 'a': a}
    _L1_gnn_all = _L1_gnn_setup()
    _L1_gnn_in = {k: v for k, v in _L1_gnn_all.items() if k in ('W', 'a', )}
    del _L1_gnn_all

    def _L1_ffn_setup():
        import jax, jax.numpy as jnp
        import numpy as np
        D = 256
        E = 4
        C = 4
        DC = 64
        H = 2
        DH = DC // H
        EPS = 1e-05
        key = jax.random.key(seed)
        ks = jax.random.split(key, 8)
        B, T = (4, 1024)
        s = 0.02
        return {'x': jax.random.normal(ks[0], (B, T, D), dtype=jnp.float32), 'norm_w': jnp.ones((D,), dtype=jnp.float32), 'router_w': jax.random.normal(ks[1], (E, D), dtype=jnp.float32) * s, 'router_b': jnp.zeros((E,), dtype=jnp.float32), 'qkv_w': jax.random.normal(ks[2], (E, 3 * DC, DC), dtype=jnp.float32) * s, 'proj_w': jax.random.normal(ks[3], (E, DC, DC), dtype=jnp.float32) * s, 'proj_b': jnp.zeros((E, DC), dtype=jnp.float32), 'out_w': jax.random.normal(ks[4], (D, D), dtype=jnp.float32) * s}
    _L1_ffn_all = _L1_ffn_setup()
    _L1_ffn_in = {k: v for k, v in _L1_ffn_all.items() if k in ('norm_w', 'router_w', 'router_b', 'qkv_w', 'proj_w', 'proj_b', 'out_w', )}
    del _L1_ffn_all

    return {
        "x": x,
        "adj": adj,
        "L0_gnn_weight": _L0_gnn_in["weight"],
        "L0_gnn_bias": _L0_gnn_in["bias"],
        "L0_ffn_W1": _L0_ffn_in["W1"],
        "L0_ffn_b1": _L0_ffn_in["b1"],
        "L0_ffn_Wg": _L0_ffn_in["Wg"],
        "L0_ffn_bg": _L0_ffn_in["bg"],
        "L0_ffn_Wd": _L0_ffn_in["Wd"],
        "L0_ffn_bd": _L0_ffn_in["bd"],
        "L1_gnn_W": _L1_gnn_in["W"],
        "L1_gnn_a": _L1_gnn_in["a"],
        "L1_ffn_norm_w": _L1_ffn_in["norm_w"],
        "L1_ffn_router_w": _L1_ffn_in["router_w"],
        "L1_ffn_router_b": _L1_ffn_in["router_b"],
        "L1_ffn_qkv_w": _L1_ffn_in["qkv_w"],
        "L1_ffn_proj_w": _L1_ffn_in["proj_w"],
        "L1_ffn_proj_b": _L1_ffn_in["proj_b"],
        "L1_ffn_out_w": _L1_ffn_in["out_w"],
    }

def reference(x, adj, L0_gnn_weight, L0_gnn_bias, L0_ffn_W1, L0_ffn_b1, L0_ffn_Wg, L0_ffn_bg, L0_ffn_Wd, L0_ffn_bd, L1_gnn_W, L1_gnn_a, L1_ffn_norm_w, L1_ffn_router_w, L1_ffn_router_b, L1_ffn_qkv_w, L1_ffn_proj_w, L1_ffn_proj_b, L1_ffn_out_w):
    import jax
    import jax.numpy as jnp
    def _L0_gnn_ref(x, adj, weight, bias):
        import jax, jax.numpy as jnp
        import numpy as np
        SPARSITY = 0.01

        def quantize(weight, s):
            pos = (weight > s).astype(weight.dtype)
            neg = (weight < -s).astype(weight.dtype)
            return (pos - neg) * s
        dw = quantize(weight, SPARSITY)
        support = jnp.einsum('bni,io->bno', x, dw)
        out = jnp.einsum('bnm,bmo->bno', adj, support) + bias
        return jax.nn.relu(out)

    def _L0_ffn_ref(x, W1, b1, Wg, bg, Wd, bd):
        import jax, jax.numpy as jnp
        import numpy as np
        C = 256
        HID = 1024
        E = 8
        TEMP = 1.0
        orig_shape = x.shape
        xf = x.reshape(-1, orig_shape[-1])
        H = jax.nn.gelu(xf @ W1 + b1, approximate=False)
        probs = jax.nn.softmax((H @ Wg + bg) / TEMP, axis=-1)
        assign = jnp.argmax(probs, axis=-1)
        out = jnp.zeros_like(xf)
        for e in range(Wd.shape[0]):
            y = H @ Wd[e] + bd[e]
            sel = (assign == e)[:, None]
            out = out + jnp.where(sel, probs[:, e:e + 1] * y, 0.0)
        return out.reshape(orig_shape)

    def _L1_gnn_ref(x, adj, W, a):
        import jax, jax.numpy as jnp
        import numpy as np
        B, N, IN_DIM, OUT_DIM, H = (8, 1024, 256, 256, 4)
        D = OUT_DIM // H
        NEG_INF = -9000000000000000.0
        LRELU_SLOPE = 0.2
        h = jnp.einsum('bni,io->bno', x, W).reshape(x.shape[0], x.shape[1], H, D)
        h = h.transpose(0, 2, 1, 3)
        a1, a2 = (a[:, :D], a[:, D:])
        e_i = jnp.einsum('bhnd,hd->bhn', h, a1)
        e_j = jnp.einsum('bhmd,hd->bhm', h, a2)
        e = e_i[:, :, :, None] + e_j[:, :, None, :]
        e = jnp.where(e > 0, e, LRELU_SLOPE * e)
        e = jnp.where(adj[:, None, :, :] > 0, e, NEG_INF)
        attn = jax.nn.softmax(e, axis=-1)
        out = jnp.einsum('bhnm,bhmd->bhnd', attn, h)
        out = out.transpose(0, 2, 1, 3).reshape(x.shape[0], x.shape[1], H * D)
        return out

    def _L1_ffn_ref(x, norm_w, router_w, router_b, qkv_w, proj_w, proj_b, out_w):
        import jax, jax.numpy as jnp
        import numpy as np
        D = 256
        E = 4
        C = 4
        DC = 64
        H = 2
        DH = DC // H
        EPS = 1e-05
        B, T, _ = x.shape
        residual = x
        mean = jnp.mean(x, axis=-1, keepdims=True)
        var = jnp.mean((x - mean) ** 2, axis=-1, keepdims=True)
        xn = (x - mean) / jnp.sqrt(var + EPS) * norm_w
        gate = jax.nn.softmax(xn @ router_w.T + router_b, axis=-1)
        xc = xn.reshape(B, T, C, DC)
        qkv = jnp.einsum('btcd,ekd->btcek', xc, qkv_w)
        qkv = qkv.reshape(B, T, C, E, 3, H, DH)
        qkv = qkv.transpose(4, 0, 2, 3, 5, 1, 6)
        q, k, v = (qkv[0], qkv[1], qkv[2])
        scale = 1.0 / np.sqrt(DH).astype(np.float32)
        attn = jnp.einsum('bcehtd,bcehsd->bcehts', q, k) * scale
        attn = jax.nn.softmax(attn, axis=-1)
        y = jnp.einsum('bcehts,bcehsd->bcehtd', attn, v)
        y = y.transpose(0, 4, 1, 2, 3, 5).reshape(B, T, C, E, DC)
        y = jnp.einsum('btced,eod->btceo', y, proj_w) + proj_b[None, None, None, :, :]
        out = jnp.einsum('btceo,bte->btco', y, gate).reshape(B, T, D)
        return residual + out @ out_w.T

    x = x + _L0_gnn_ref(_layernorm(x, axis=-1), adj, L0_gnn_weight, L0_gnn_bias)
    x = x + _L0_ffn_ref(_layernorm(x, axis=-1), L0_ffn_W1, L0_ffn_b1, L0_ffn_Wg, L0_ffn_bg, L0_ffn_Wd, L0_ffn_bd)
    x = x + _L1_gnn_ref(_layernorm(x, axis=-1), adj, L1_gnn_W, L1_gnn_a)
    x = x + _L1_ffn_ref(_layernorm(x, axis=-1), L1_ffn_norm_w, L1_ffn_router_w, L1_ffn_router_b, L1_ffn_qkv_w, L1_ffn_proj_w, L1_ffn_proj_b, L1_ffn_out_w)
    return x


_drawn_inputs = setup_inputs


def setup_inputs(seed=0):
    import zlib

    import numpy as np

    out = dict(_drawn_inputs(seed))
    spreads = {'L0_gnn_bias': (0.0, 0.1),
     'L0_ffn_b1': (0.0, 0.581),
     'L0_ffn_bg': (0.0, 0.396),
     'L0_ffn_bd': (0.0, 0.557),
     'L1_ffn_norm_w': (1.0, 0.6),
     'L1_ffn_router_b': (0.0, 0.8),
     'L1_ffn_proj_b': (0.0, 0.8)}
    factors = {'L0_ffn_W1': 2.717,
     'L0_ffn_Wg': 2.933,
     'L0_ffn_Wd': 3.32,
     'L1_ffn_router_w': 8.0,
     'L1_ffn_qkv_w': 8.0,
     'L1_ffn_proj_w': 8.0,
     'L1_ffn_out_w': 8.0}
    for name, (base, spread) in spreads.items():
        noise = np.random.default_rng([zlib.crc32(name.encode()), seed]).standard_normal(out[name].shape)
        drawn = base * np.exp(spread * noise) if base else spread * noise
        out[name] = jnp.asarray(drawn.astype(out[name].dtype))
    for name, factor in factors.items():
        out[name] = (out[name] * factor).astype(out[name].dtype)
    return out
```

```python
import concourse.bass as bass
from concourse import mybir
from contextlib import ExitStack

F32 = mybir.dt.float32
F32R = mybir.dt.float32r
BF16 = mybir.dt.bfloat16
I32 = mybir.dt.int32
ALU = mybir.AluOpType
ACT = mybir.ActivationFunctionType
AX = mybir.AxisListType

P = 128
EPS = 1e-5
RSQRT_SEED = 1597463007.0


def wait(eng, sem, value):
    if isinstance(value, int) and value <= 0:
        return
    eng.wait_ge(sem, value)


class Steps:

    def __init__(self, eng, sem, base):
        self.eng, self.sem, self.base, self.n = eng, sem, base, 0

    def done(self, instruction):
        self.n += 1
        instruction.then_inc(self.sem, 1)

    def sync(self):
        self.eng.wait_ge(self.sem, self.base + self.n)

    def link(self, instruction):
        self.done(instruction)
        self.sync()


def mm3(pe, out, stat, mov, start=True, stop=True, **kw):
    pe.matmul(out, stat[0], mov[0], start=start, stop=False, **kw)
    pe.matmul(out, stat[0], mov[1], start=False, stop=False, **kw)
    return pe.matmul(out, stat[1], mov[0], start=False, stop=stop, **kw)


RSQRT_LINKS = 12


def rsqrt(dve, steps, arg, y_i, tmp):
    y = y_i.bitcast(F32)
    steps.link(dve.tensor_scalar(y_i, arg.bitcast(I32), 1, None, ALU.arith_shift_right))
    steps.link(dve.tensor_scalar(y_i, y_i, -1.0, RSQRT_SEED, ALU.mult, ALU.add))
    steps.link(dve.tensor_scalar(arg, arg, -0.5, None, ALU.mult))
    for _ in range(3):
        steps.link(dve.tensor_tensor(tmp, y, y, ALU.mult))
        steps.link(dve.tensor_tensor(tmp, tmp, arg, ALU.mult))
        steps.link(dve.scalar_tensor_tensor(y, tmp, 1.5, y, ALU.add, ALU.mult))


def pool_turn(pool, pad, at):
    return pool.tensor_tensor(pad[:, at:at + 1], pad[:, 0:1], pad[:, 0:1], ALU.add)


TILES = 64
GROUP = 4
GROUPS = TILES // GROUP
TOKENS = TILES * P
D = 256
HID = 1024
KH = HID // P
E0 = 8
SLOTS = TILES + E0
TERNARY = 0.01


def setup_shared(nc, sb, sem, w):
    c = {}
    c["ident"] = sb("ident", [P, P])
    c["ident_bf"] = sb("ident_bf", [P, P], BF16)
    c["before"] = sb("before", [P, P], BF16)
    c["ones_bf"] = sb("ones_bf", [P, P], BF16)
    c["iota_i"] = sb("iota_i", [P, P], I32)
    c["iota8"] = sb("iota8", [P, E0])
    c["token_f"] = sb("token_f", [P, GROUP])
    c["running"] = sb("running", [P, E0])
    c["shifted"] = sb("shifted", [P, TILES, E0])
    c["expert"] = sb("expert", [P, TILES])
    c["rank"] = sb("rank", [P, TILES])
    c["prob"] = sb("prob", [P, TILES])
    c["yrow"] = sb("yrow", [P, TILES], I32)
    c["slot_expert"] = sb("slot_expert", [P, SLOTS], I32)
    c["slot_row"] = sb("slot_row", [P, SLOTS], I32)
    c["bd_bc"] = sb("bd_bc", [P, E0 * D])
    c["b1"] = sb("b1", [P, KH])
    c["w1h"] = sb("w1h", [P, 2, HID], F32R)
    c["w1l"] = sb("w1l", [P, 2, HID], F32R)
    return c


def layer0a(nc, c, A, wd_raw):
    x_t = A["x"].rearrange("(t g) m d -> (g m) t d", g=2)
    adj_t = A["adj"].rearrange("(t g) n m -> g n t m", g=2)
    x1_t = A["x1"].rearrange("(t p) d -> p t d", p=P)
    xn_t = A["xn"].rearrange("(t p) d -> p t d", p=P)
    with ExitStack() as ctx:
        def sb(name, shape, dt=F32):
            return ctx.enter_context(nc.sbuf_tensor("a_" + name, shape, dt))

        def ps(name, shape, dt=F32):
            return ctx.enter_context(nc.psum_tensor("a_" + name, shape, dt))

        def sem(name):
            return ctx.enter_context(nc.semaphore("a_" + name))

        ident, w1h, w1l = c["ident"], c["w1h"], c["w1l"]
        w0_raw = sb("w0_raw", [P, 2, D])
        w0_neg = sb("w0_neg", [P, 2, D])
        w0 = sb("w0", [P, 2, D], F32R)
        w1_raw = sb("w1_raw", [P, 2, HID])
        wg_raw = sb("wg_raw", [P, KH, E0])
        wgh = sb("wgh", [P, KH, E0], F32R)
        wgl = sb("wgl", [P, KH, E0], F32R)
        bias0 = sb("bias0", [P, D])
        bg = sb("bg", [P, E0])
        zero_i = sb("zero_i", [P, 512], I32)

        dve_pad = sb("dve_pad", [P, 1])
        pool_pad = sb("pool_pad", [P, 3])
        xin = [sb(f"xin{u}", [P, GROUP, D]) for u in range(2)]
        adjd = [sb(f"adjd{u}", [P, GROUP, P]) for u in range(2)]
        stats = sb("stats", [P, GROUP, 6])
        mv = sb("mv", [P, GROUP, 2])
        seed_i = sb("seed_i", [P, GROUP], I32)
        rs_tmp = sb("rs_tmp", [P, GROUP])
        rstd = sb("rstd", [P, GROUP])
        xln = sb("xln", [P, GROUP, D])
        xlnh = sb("xlnh", [P, GROUP, D], F32R)
        xlnl = sb("xlnl", [P, GROUP, D], F32R)
        adjTh = sb("adjTh", [P, GROUP, P], F32R)
        adjTl = sb("adjTl", [P, GROUP, P], F32R)
        zh = sb("zh", [P, 2, GROUP * P], F32R)
        zl = sb("zl", [P, 2, GROUP * P], F32R)
        conv = sb("conv", [P, GROUP, D])
        x1 = [sb(f"x1{u}", [P, GROUP, D]) for u in range(2)]
        xn = [sb(f"xn{u}", [P, GROUP, D]) for u in range(2)]
        stats2 = sb("stats2", [P, GROUP, 6])
        mv2 = sb("mv2", [P, GROUP, 2])
        rstd2 = sb("rstd2", [P, GROUP])
        xTh = [sb(f"xTh{u}", [P, 2, GROUP * P], F32R) for u in range(2)]
        xTl = [sb(f"xTl{u}", [P, 2, GROUP * P], F32R) for u in range(2)]
        gel = [sb(f"gel{u}", [P, GROUP * P]) for u in range(2)]
        Hh = [sb(f"Hh{u}", [P, GROUP * P], F32R) for u in range(4)]
        Hl = [sb(f"Hl{u}", [P, GROUP * P], F32R) for u in range(4)]
        logit = sb("logit", [P, GROUP, E0])
        top = sb("top", [P, GROUP])
        shifted = sb("shiftedg", [P, GROUP, E0])
        cand = sb("cand", [P, GROUP, E0])
        eidx = [sb(f"eidx{u}", [P, GROUP]) for u in range(2)]
        onehot = [sb(f"onehot{u}", [P, GROUP, E0], BF16) for u in range(2)]
        base = sb("base", [P, GROUP + 1, E0])
        counts = sb("counts", [P, GROUP, E0])
        within = sb("within", [P, GROUP, E0])
        rank = sb("rankg", [P, GROUP])
        place_f = sb("place_f", [P, GROUP])
        place = [sb(f"place{u}", [P, GROUP], I32) for u in range(2)]
        token = [sb(f"token{u}", [P, GROUP], I32) for u in range(2)]

        front_a = ps("front_a", [P, 2, 512])
        front_b = ps("front_b", [P, 2, 512])
        hid = [ps(f"hid{i}", [P, 512]) for i in range(3)]
        gate = ps("gate", [P, 512])
        lg = gate[:, 0:GROUP * E0].rearrange("p (t e) -> p t e", e=E0)
        prefix = gate[:, 64:64 + GROUP * E0].rearrange("p (t e) -> p t e", e=E0)
        total = gate[:, 128:128 + GROUP * E0].rearrange("p (t e) -> p t e", e=E0)

        weights_in = sem("weights_in")
        table_zeroed = sem("table_zeroed")
        wd_in = sem("wd_in")
        const_step = sem("const_step")
        adjd_zeroed = sem("adjd_zeroed")
        weights_split = sem("weights_split")
        x_in = [sem(f"x_in{u}") for u in range(2)]
        adj_in = [sem(f"adj_in{u}") for u in range(2)]
        x1_out = [sem(f"x1_out{u}") for u in range(2)]
        adj_turned = sem("adj_turned")
        adjh_done = sem("adjh_done")
        adj_split = sem("adj_split")
        xln_ready = sem("xln_ready")
        z_done = sem("z_done")
        zh_done = sem("zh_done")
        z_split = sem("z_split")
        conv_done = sem("conv_done")
        x1_ready = sem("x1_ready")
        xn_ready = sem("xn_ready")
        xn_turned = sem("xn_turned")
        xTh_done = sem("xTh_done")
        xT_split = sem("xT_split")
        hid_done = sem("hid_done")
        gelu_done = sem("gelu_done")
        gelu_hi = sem("gelu_hi")
        h_split = sem("h_split")
        logits_part = sem("logits_part")
        onehot_ready = sem("onehot_ready")
        ranks_counted = sem("ranks_counted")
        ranks_read = sem("ranks_read")
        place_ready = sem("place_ready")
        scatter_turn = sem("scatter_turn")
        scattered = [sem(f"scattered{u}") for u in range(2)]
        stage_step = sem("stage_step")
        norm_step = sem("norm_step")
        gate_step = sem("gate_step")
        rank_step = sem("rank_step")

        block = ctx.enter_context(nc.Block())

        def schedule(eng, step):
            for s in range(4):
                step(s, s // 2, s % 2)
            with eng.Fori(2, 7) as j:
                step(2 * j, j, 0)
                step(2 * j + 1, j, 1)
            for s in range(14, GROUPS + 2):
                step(s, s // 2, s % 2)

        def has(s, first, last):
            return not isinstance(s, int) or first <= s <= last

        @block.sync
        def _(sp):
            for n, (dst, src) in enumerate((
                    (w0_raw[:], A["w0"].rearrange("(c p) o -> p c o", p=P)),
                    (w1_raw[:], A["w1"].rearrange("(c p) o -> p c o", p=P)),
                    (wg_raw[:], A["wg"].rearrange("(k p) e -> p k e", p=P)),
                    (c["b1"][:], A["b1"].rearrange("(k p) -> p k", p=P)),
                    (bias0[:], A["bias0"].partition_broadcast(P)),
                    (bg[:], A["bg"].partition_broadcast(P)),
                    (c["bd_bc"][:], A["bd"].rearrange("e o -> (e o)").partition_broadcast(P)))):
                sp.dma_start(dst, src, allow_slow_non_contiguous=(n == 3)).then_inc(weights_in, 16)

            def load(n, h, u):
                wait(sp, x1_ready, n - 1)
                sp.dma_start(xin[u][:], x_t[:, bass.ds(GROUP * n, GROUP), :]).then_inc(x_in[u], 16)
                if isinstance(n, int) and n < 2:
                    sp.wait_ge(adjd_zeroed, 2)
                for g in range(2):
                    r = slice(64 * g, 64 * g + 64)
                    sp.dma_start(adjd[u][r, :, r],
                                 adj_t[g, :, bass.ds(GROUP * n, GROUP), :]).then_inc(adj_in[u], 16)

            def step(s, j, u):
                if has(s, 0, GROUPS - 2):
                    load(s + 1, j + u, 1 - u)
                if has(s, 0, GROUPS - 1):
                    sp.wait_ge(x1_ready, s + 1)
                    sp.dma_start(x1_t[:, bass.ds(GROUP * s, GROUP), :], x1[u][:]).then_inc(x1_out[u], 16)
                    sp.wait_ge(xn_ready, s + 1)
                    sp.dma_start(xn_t[:, bass.ds(GROUP * s, GROUP), :], xn[u][:]).then_inc(x1_out[u], 16)

            load(0, 0, 0)
            schedule(sp, step)
            for u in range(2):
                sp.wait_ge(x1_out[u], 32 * (GROUPS // 2))
            sp.wait_ge(wd_in, 16 * E0)

        @block.gpsimd
        def _(pool):
            n = 0

            def link(ins, count=True):
                nonlocal n
                n += 1
                ins.then_inc(const_step, 1)
                pool.wait_ge(const_step, n)

            for u in range(2):
                pool.memset(adjd[u][:], 0.0).then_inc(adjd_zeroed, 1)
            link(pool.memset(ident[:], 0.0))
            link(pool.affine_select(out=ident[:], in_=ident[:], compare_op=ALU.not_equal, fill=1.0, base=0,
                                    pattern=[[-1, P]], channel_multiplier=1))
            link(pool.tensor_copy(c["ident_bf"][:], ident[:]))
            link(pool.memset(c["ones_bf"][:], 1.0))
            link(pool.affine_select(out=c["before"][:], in_=c["ones_bf"][:], compare_op=ALU.is_gt, fill=0.0,
                                    base=0, pattern=[[1, P]], channel_multiplier=-1))
            link(pool.iota(c["iota_i"][:], pattern=[[1, P]], base=0, channel_multiplier=0))
            link(pool.tensor_copy(c["iota8"][:], c["iota_i"][:, 0:E0]))
            link(pool.iota(c["iota_i"][:, 0:GROUP], pattern=[[P, GROUP]], base=0, channel_multiplier=1))
            link(pool.tensor_copy(c["token_f"][:], c["iota_i"][:, 0:GROUP]))
            link(pool.memset(c["running"][:], 0.0))
            link(pool.memset(pool_pad[:], 0.0))
            link(pool.memset(zero_i[:], 0))
            pool.dma_start(A["table"].rearrange("(p n) a -> p (n a)", p=P), zero_i[:]).then_inc(table_zeroed, 16)
            pool.wait_ge(table_zeroed, 16)
            wd_v = A["wd"].rearrange("e (k p) o -> p e k o", p=P)
            raw_v = wd_raw[:].rearrange("p k (e o) -> p e k o", e=E0)
            for e in range(E0):
                pool.dma_start(raw_v[:, e], wd_v[:, e]).then_inc(wd_in, 16)

            def step(s, j, u):
                if has(s, 2, GROUPS + 1):
                    pool.wait_ge(place_ready, s - 1)
                    pool_turn(pool, pool_pad, 1 + u).then_inc(scatter_turn, 1)
                    for t in range(GROUP):
                        pool.indirect_dma_start(
                            A["table"], bass.IndirectOffsetOnAxis(ap=place[u][:, t:t + 1], axis=0),
                            token[u][:, t:t + 1], None).then_inc(scattered[u], 16)

            schedule(pool, step)
            for u in range(2):
                pool.wait_ge(scattered[u], 16 * GROUP * (GROUPS // 2))

        BANK = [0, 1, 2, 0, 1, 2, 0, 1]
        BANK_BEFORE = [-2, -1, -3, 0, 1, 2, 3, 4]

        @block.tensor
        def _(pe):
            pe.wait_ge(const_step, 12)
            pe.wait_ge(weights_split, 5)

            def turn_adj(n, h, u):
                pe.wait_ge(adj_in[u], 32 * (h + 1))
                wait(pe, x1_ready, n)
                for t in range(GROUP):
                    ins = pe.transpose(front_a[:, 0, t * P:(t + 1) * P], adjd[u][:, t, :], ident[:])
                ins.then_inc(adj_turned, 1)

            def mix_nodes(n):
                pe.wait_ge(xln_ready, n + 1)
                pe.wait_ge(adj_split, n + 1)
                wait(pe, xT_split, 2 * n)
                for ic in range(2):
                    for t in range(GROUP):
                        cols = slice(ic * P, ic * P + P)
                        ins = mm3(pe, front_b[:, ic, t * P:(t + 1) * P],
                                  (xlnh[:, t, cols], xlnl[:, t, cols]), (adjTh[:, t, :], adjTl[:, t, :]))
                    ins.then_inc(z_done, 1)

            def mix_channels(n):
                pe.wait_ge(z_split, 2 * n + 2)
                for t in range(GROUP):
                    out = front_a[:, t // 2, (t % 2) * D:(t % 2) * D + D]
                    for ic in range(2):
                        cols = slice(t * P, t * P + P)
                        pe.matmul(out, zh[:, ic, cols], w0[:, ic, :], start=(ic == 0), stop=False)
                        ins = pe.matmul(out, zl[:, ic, cols], w0[:, ic, :], start=False, stop=(ic == 1))
                    if t % 2:
                        ins.then_inc(conv_done, 1)

            def turn_xn(n, u):
                pe.wait_ge(xn_ready, n + 1)
                for ic in range(2):
                    for t in range(GROUP):
                        ins = pe.transpose(front_b[:, ic, t * P:(t + 1) * P],
                                           xn[u][:, t, ic * P:ic * P + P], ident[:])
                    ins.then_inc(xn_turned, 1)

            def hidden(n, k, u):
                if k == 0:
                    pe.wait_ge(xT_split, 2 * n + 2)
                wait(pe, gelu_hi, KH * n + BANK_BEFORE[k] + 1)
                out = hid[BANK[k]]
                cols = slice(k * P, k * P + P)
                for ic in range(2):
                    ins = mm3(pe, out[:], (w1h[:, ic, cols], w1l[:, ic, cols]), (xTh[u][:, ic, :], xTl[u][:, ic, :]),
                              start=(ic == 0), stop=(ic == 1))
                ins.then_inc(hid_done, 1)

            def logits(n, k):
                pe.wait_ge(h_split, KH * n + k + 1)
                if k == 0:
                    wait(pe, ranks_read, n)
                for t in range(GROUP):
                    cols = slice(t * P, t * P + P)
                    ins = mm3(pe, lg[:, t, :], (Hh[k % 4][:, cols], Hl[k % 4][:, cols]),
                              (wgh[:, k, :], wgl[:, k, :]), start=(k == 0 and t == 0), stop=(k == KH - 1),
                              skip_group_check=True)
                ins.then_inc(logits_part, 1)

            def count_ranks(n, u):
                pe.wait_ge(onehot_ready, n + 1)
                pe.matmul(prefix, c["before"][:], onehot[u][:], start=True, stop=True)
                pe.matmul(total, c["ones_bf"][:], onehot[u][:], start=True, stop=True).then_inc(ranks_counted, 1)

            def step(s, j, u):
                front, back, ranks = has(s, 0, GROUPS - 1), has(s, 1, GROUPS), has(s, 2, GROUPS + 1)
                v = 1 - u
                if front:
                    turn_adj(s, j, u)
                if back:
                    hidden(s - 1, 0, v)
                    hidden(s - 1, 1, v)
                if ranks:
                    count_ranks(s - 2, u)
                if front:
                    mix_nodes(s)
                if back:
                    hidden(s - 1, 2, v)
                    logits(s - 1, 0)
                    hidden(s - 1, 3, v)
                    logits(s - 1, 1)
                if front:
                    mix_channels(s)
                if back:
                    hidden(s - 1, 4, v)
                    logits(s - 1, 2)
                    hidden(s - 1, 5, v)
                    logits(s - 1, 3)
                    hidden(s - 1, 6, v)
                    logits(s - 1, 4)
                if front:
                    turn_xn(s, u)
                if back:
                    hidden(s - 1, 7, v)
                    for k in range(5, KH):
                        logits(s - 1, k)

            schedule(pe, step)

        @block.scalar
        def _(act):
            act.wait_ge(weights_in, 16 * 7)

            def gelu(n, k):
                act.wait_ge(hid_done, KH * n + k + 1)
                wait(act, h_split, KH * n + k - 1)
                act.activation(gel[k % 2][:], hid[BANK[k]][:], ACT.Gelu, bias=c["b1"][:, k:k + 1]).then_inc(gelu_done, 1)
                wait(act, logits_part, KH * n + k - 3)
                act.activation(Hh[k % 4][:], hid[BANK[k]][:], ACT.Gelu, bias=c["b1"][:, k:k + 1]).then_inc(gelu_hi, 1)

            def step(s, j, u):
                front, back = has(s, 0, GROUPS - 1), has(s, 1, GROUPS)
                if front:
                    act.wait_ge(adj_turned, s + 1)
                    wait(act, z_done, 2 * s)
                    act.activation(adjTh[:], front_a[:, 0, :].rearrange("p (t n) -> p t n", n=P), ACT.Copy).then_inc(adjh_done, 1)
                if back:
                    gelu(s - 1, 0)
                    gelu(s - 1, 1)
                if front:
                    for ic in range(2):
                        act.wait_ge(z_done, 2 * s + ic + 1)
                        if ic == 0:
                            wait(act, conv_done, 2 * s)
                        act.activation(zh[:, ic, :], front_b[:, ic, :], ACT.Copy).then_inc(zh_done, 1)
                if back:
                    for k in range(2, 7):
                        gelu(s - 1, k)
                if front:
                    for ic in range(2):
                        act.wait_ge(xn_turned, 2 * s + ic + 1)
                        if ic == 0:
                            wait(act, hid_done, KH * (s - 1))
                        act.activation(xTh[u][:, ic, :], front_b[:, ic, :], ACT.Copy).then_inc(xTh_done, 1)
                if back:
                    gelu(s - 1, 7)

            schedule(act, step)

        @block.vector
        def _(dve):
            dve.wait_ge(weights_in, 16 * 7)
            dve.tensor_scalar(w0_neg[:], w0_raw[:], -TERNARY, None, ALU.is_lt).then_inc(weights_split, 1)
            dve.tensor_copy(w1h[:], w1_raw[:]).then_inc(weights_split, 1)
            dve.tensor_copy(wgh[:], wg_raw[:]).then_inc(weights_split, 1)
            dve.wait_ge(weights_split, 3)
            dve.scalar_tensor_tensor(w0[:], w0_raw[:], TERNARY, w0_neg[:], ALU.is_gt, ALU.subtract)
            dve.tensor_tensor(w1l[:], w1_raw[:], w1h[:].bitcast(F32), ALU.subtract).then_inc(weights_split, 1)
            dve.tensor_tensor(wgl[:], wg_raw[:], wgh[:].bitcast(F32), ALU.subtract).then_inc(weights_split, 1)

            STAGE_LINKS = 4 + RSQRT_LINKS

            def stage_x(n, h, u):
                st = Steps(dve, stage_step, STAGE_LINKS * n)
                dve.wait_ge(x_in[u], 16 * (h + 1))
                for t in range(GROUP):
                    ins = dve.bn_stats(stats[:, t, :], xin[u][:, t, :])
                st.link(ins)
                dve.memset(dve_pad[:], 0.0)
                for t in range(GROUP):
                    ins = dve.bn_aggr(mv[:, t, :], stats[:, t, :])
                st.link(ins)
                rsqrt_into(st, rstd, mv)
                for t in range(GROUP):
                    ins = dve.tensor_scalar(xln[:, t, :], xin[u][:, t, :], mv[:, t, 0:1], rstd_y(t), ALU.subtract, ALU.mult)
                st.link(ins)
                wait(dve, z_done, 2 * n)
                dve.tensor_copy(xlnh[:], xln[:]).then_inc(xln_hi, 1)
                dve.wait_ge(xln_hi, n + 1)
                dve.tensor_tensor(xlnl[:], xln[:], xlnh[:].bitcast(F32), ALU.subtract).then_inc(xln_ready, 1)
                assert st.n == STAGE_LINKS

            def rsqrt_into(st, half, moments):
                st.link(dve.tensor_scalar(half[:], moments[:, :, 1], EPS, None, ALU.add))
                rsqrt(dve, st, half[:], seed_i[:], rs_tmp[:])

            def rstd_y(t):
                return seed_i[:, t:t + 1].bitcast(F32)

            def split_adj(n):
                dve.wait_ge(adjh_done, n + 1)
                dve.tensor_tensor(adjTl[:], front_a[:, 0, :].rearrange("p (t n) -> p t n", n=P),
                                  adjTh[:].bitcast(F32), ALU.subtract).then_inc(adj_split, 1)

            def split_z(n):
                for ic in range(2):
                    dve.wait_ge(zh_done, 2 * n + ic + 1)
                    dve.tensor_tensor(zl[:, ic, :], front_b[:, ic, :], zh[:, ic, :].bitcast(F32),
                                      ALU.subtract).then_inc(z_split, 1)

            def split_xT(n, u):
                for ic in range(2):
                    dve.wait_ge(xTh_done, 2 * n + ic + 1)
                    dve.tensor_tensor(xTl[u][:, ic, :], front_b[:, ic, :], xTh[u][:, ic, :].bitcast(F32),
                                      ALU.subtract).then_inc(xT_split, 1)

            def split_h(n, k):
                dve.wait_ge(gelu_hi, KH * n + k + 1)
                wait(dve, logits_part, KH * n + k - 3)
                dve.tensor_tensor(Hl[k % 4][:], gel[k % 2][:], Hh[k % 4][:].bitcast(F32), ALU.subtract).then_inc(h_split, 1)

            NORM_LINKS = 4 + RSQRT_LINKS

            def residual_norm(n, h, u):
                st = Steps(dve, norm_step, NORM_LINKS * n)
                wait(dve, x1_out[u], 32 * h)
                for b in range(2):
                    dve.wait_ge(conv_done, 2 * n + b + 1)
                    ins = dve.scalar_tensor_tensor(
                        conv[:, 2 * b:2 * b + 2, :], front_a[:, b, :].rearrange("p (t o) -> p t o", o=D), TERNARY,
                        bias0[:].unsqueeze(1).to_broadcast([P, 2, D]), ALU.mult, ALU.add)
                st.link(ins)
                dve.scalar_tensor_tensor(x1[u][:], conv[:], 0.0, xin[u][:], ALU.max, ALU.add).then_inc(x1_ready, 1)
                dve.wait_ge(x1_ready, n + 1)
                for t in range(GROUP):
                    ins = dve.bn_stats(stats2[:, t, :], x1[u][:, t, :])
                st.link(ins)
                dve.memset(dve_pad[:], 0.0)
                for t in range(GROUP):
                    ins = dve.bn_aggr(mv2[:, t, :], stats2[:, t, :])
                st.link(ins)
                rsqrt_into(st, rstd2, mv2)
                for t in range(GROUP):
                    ins = dve.tensor_scalar(xn[u][:, t, :], x1[u][:, t, :], mv2[:, t, 0:1], rstd_y(t), ALU.subtract, ALU.mult)
                ins.then_inc(xn_ready, 1)
                assert st.n == NORM_LINKS

            GATE_LINKS = 6

            def choose(n, u):
                st = Steps(dve, gate_step, GATE_LINKS * n)
                bc = lambda ap: ap.unsqueeze(2).to_broadcast([P, GROUP, E0])
                i8 = c["iota8"][:].unsqueeze(1).to_broadcast([P, GROUP, E0])
                dve.wait_ge(logits_part, KH * n + KH)
                st.link(dve.tensor_tensor(logit[:], lg, bg[:].unsqueeze(1).to_broadcast([P, GROUP, E0]), ALU.add))
                st.link(dve.tensor_reduce(top[:], logit[:], AX.X, ALU.max))
                st.link(dve.tensor_tensor(shifted[:], logit[:], bc(top[:]), ALU.subtract))
                dve.tensor_copy(c["shifted"][:, bass.ds(GROUP * n, GROUP), :], shifted[:])
                st.link(dve.tensor_scalar(cand[:], shifted[:], 0.0, float(E0), ALU.is_lt, ALU.mult))
                st.link(dve.tensor_tensor(cand[:], cand[:], i8, ALU.add))
                st.link(dve.tensor_reduce(eidx[u][:], cand[:], AX.X, ALU.min))
                dve.tensor_copy(c["expert"][:, bass.ds(GROUP * n, GROUP)], eidx[u][:])
                dve.tensor_tensor(onehot[u][:], i8, bc(eidx[u][:]), ALU.is_equal).then_inc(onehot_ready, 1)
                assert st.n == GATE_LINKS

            RANK_LINKS = 12

            def number(n, h, u):
                st = Steps(dve, rank_step, RANK_LINKS * n)
                dve.wait_ge(ranks_counted, n + 1)
                dve.tensor_copy(counts[:], total)
                st.link(dve.tensor_copy(within[:], prefix))
                st.link(dve.tensor_copy(base[:, 0, :], c["running"][:]))
                for t in range(GROUP):
                    st.link(dve.tensor_tensor(base[:, t + 1, :], base[:, t, :], counts[:, t, :], ALU.add))
                dve.tensor_copy(c["running"][:], base[:, GROUP, :]).then_inc(ranks_read, 1)
                st.link(dve.tensor_tensor(within[:], within[:], base[:, 0:GROUP, :], ALU.add))
                st.link(dve.tensor_tensor(within[:], within[:], onehot[u][:], ALU.mult))
                st.link(dve.tensor_reduce(rank[:], within[:], AX.X, ALU.add))
                dve.tensor_copy(c["rank"][:, bass.ds(GROUP * n, GROUP)], rank[:])
                st.link(dve.scalar_tensor_tensor(place_f[:], eidx[u][:], float(TOKENS), rank[:], ALU.mult, ALU.add))
                wait(dve, scattered[u], 16 * GROUP * h)
                wait(dve, scatter_turn, 2 * h)
                st.link(dve.tensor_copy(token[u][:], c["token_f"][:]))
                dve.tensor_copy(place[u][:], place_f[:]).then_inc(place_ready, 1)
                st.link(dve.tensor_scalar(c["token_f"][:], c["token_f"][:], float(GROUP * P), None, ALU.add))
                assert st.n == RANK_LINKS

            def step(s, j, u):
                front, back, ranks = has(s, 0, GROUPS - 1), has(s, 1, GROUPS), has(s, 2, GROUPS + 1)
                if front:
                    split_adj(s)
                if back:
                    split_h(s - 1, 0)
                    split_h(s - 1, 1)
                if front:
                    split_z(s)
                if ranks:
                    number(s - 2, j - 1, u)
                if back:
                    split_h(s - 1, 2)
                    split_h(s - 1, 3)
                if front:
                    residual_norm(s, j, u)
                if back:
                    split_h(s - 1, 4)
                    split_h(s - 1, 5)
                    split_h(s - 1, 6)
                if front:
                    split_xT(s, u)
                if has(s, 0, GROUPS - 2):
                    stage_x(s + 1, j + u, 1 - u)
                if back:
                    split_h(s - 1, 7)
                    choose(s - 1, 1 - u)

            xln_hi = sem("xln_hi")
            dve.wait_ge(const_step, 12)
            stage_x(0, 0, 0)
            schedule(dve, step)


def plan_slots(nc, c):
    with ExitStack() as ctx:
        def sb(name, shape, dt=F32):
            return ctx.enter_context(nc.sbuf_tensor("p_" + name, shape, dt))

        tiles_i = sb("tiles_i", [P, E0], I32)
        tiles = sb("tiles", [P, E0])
        ends = sb("ends", [P, E0 + 1])
        slot_f = sb("slot_f", [P, SLOTS])
        slot_i = sb("slot_i", [P, SLOTS], I32)
        past = sb("past", [P, SLOTS, E0])
        part = sb("part", [P, SLOTS, E0])
        expert_f = sb("expert_f", [P, SLOTS])
        before = sb("before_slot", [P, SLOTS])
        row_f = sb("row_f", [P, SLOTS])
        pick = sb("pick", [P, TILES, E0])
        first = sb("first", [P, TILES])
        yrow_f = sb("yrow_f", [P, TILES])
        expd = sb("expd", [P, TILES, E0])
        sums = sb("sums", [P, TILES])
        slots_counted = ctx.enter_context(nc.semaphore("slots_counted"))
        exp_done = ctx.enter_context(nc.semaphore("exp_done"))
        plan_step = ctx.enter_context(nc.semaphore("plan_step"))
        block = ctx.enter_context(nc.Block())

        @block.gpsimd
        def _(pool):
            pool.iota(slot_i[:], pattern=[[1, SLOTS]], base=0, channel_multiplier=0).then_inc(slots_counted, 1)

        @block.scalar
        def _(act):
            act.activation(expd[:], c["shifted"][:], ACT.Exp).then_inc(exp_done, 1)

        @block.vector
        def _(dve):
            st = Steps(dve, plan_step, 0)
            st.link(dve.tensor_scalar(tiles[:], c["running"][:], float(P - 1), None, ALU.add))
            st.link(dve.tensor_copy(tiles_i[:], tiles[:]))
            st.link(dve.tensor_scalar(tiles_i[:], tiles_i[:], 7, None, ALU.arith_shift_right))
            st.link(dve.tensor_copy(tiles[:], tiles_i[:]))
            st.link(dve.memset(ends[:, 0:1], 0.0))
            for e in range(E0):
                st.link(dve.tensor_tensor(ends[:, e + 1:e + 2], ends[:, e:e + 1], tiles[:, e:e + 1], ALU.add))
            dve.wait_ge(slots_counted, 1)
            st.link(dve.tensor_copy(slot_f[:], slot_i[:]))
            over_slots = lambda ap: ap.unsqueeze(1).to_broadcast([P, SLOTS, E0])
            over_tiles = lambda ap: ap.unsqueeze(1).to_broadcast([P, TILES, E0])
            st.link(dve.tensor_tensor(past[:], slot_f[:].unsqueeze(2).to_broadcast([P, SLOTS, E0]),
                                      over_slots(ends[:, 1:]), ALU.is_ge))
            st.link(dve.tensor_reduce(expert_f[:], past[:], AX.X, ALU.add))
            st.link(dve.tensor_scalar(expert_f[:], expert_f[:], float(E0 - 1), None, ALU.min))
            st.link(dve.tensor_tensor(part[:], past[:], over_slots(tiles[:]), ALU.mult))
            st.link(dve.tensor_reduce(before[:], part[:], AX.X, ALU.add))
            st.link(dve.tensor_tensor(row_f[:], slot_f[:], before[:], ALU.subtract))
            st.link(dve.tensor_scalar(row_f[:], row_f[:], float(P), None, ALU.mult))
            st.link(dve.scalar_tensor_tensor(row_f[:], expert_f[:], float(TOKENS), row_f[:], ALU.mult, ALU.add))
            st.link(dve.tensor_copy(c["slot_row"][:], row_f[:]))
            st.link(dve.tensor_scalar(expert_f[:], expert_f[:], float(D), None, ALU.mult))
            st.link(dve.tensor_copy(c["slot_expert"][:], expert_f[:]))
            i8 = c["iota8"][:].unsqueeze(1).to_broadcast([P, TILES, E0])
            st.link(dve.tensor_tensor(pick[:], c["expert"][:].unsqueeze(2).to_broadcast([P, TILES, E0]), i8,
                                      ALU.is_equal))
            st.link(dve.tensor_tensor(pick[:], pick[:], over_tiles(ends[:, 0:E0]), ALU.mult))
            st.link(dve.tensor_reduce(first[:], pick[:], AX.X, ALU.add))
            st.link(dve.scalar_tensor_tensor(yrow_f[:], first[:], float(P), c["rank"][:], ALU.mult, ALU.add))
            st.link(dve.tensor_copy(c["yrow"][:], yrow_f[:]))
            dve.wait_ge(exp_done, 1)
            st.link(dve.tensor_reduce(sums[:], expd[:], AX.X, ALU.add))
            st.link(dve.reciprocal(c["prob"][:], sums[:]))


def layer0b(nc, c, A, wd_raw):
    SG = SLOTS // GROUP
    y_t = A["y"].rearrange("(t p) d -> p t d", p=P)
    with ExitStack() as ctx:
        def sb(name, shape, dt=F32):
            return ctx.enter_context(nc.sbuf_tensor("b_" + name, shape, dt))

        def ps(name, shape, dt=F32):
            return ctx.enter_context(nc.psum_tensor("b_" + name, shape, dt))

        def sem(name):
            return ctx.enter_context(nc.semaphore("b_" + name))

        ident, w1h, w1l = c["ident"], c["w1h"], c["w1l"]
        wdl = nc.alloc_sbuf_tensor_at("b_wdl", [P, KH, E0 * D], F32R, offset=c["wd_offset"])
        wdh = sb("wdh", [P, KH, E0 * D], F32R)
        slot_token = [sb(f"slot_token{u}", [P, GROUP], I32) for u in range(2)]
        pool_pad = sb("pool_pad", [P, 3])
        xg = [sb(f"xg{u}", [P, GROUP, D]) for u in range(1)] * 2
        xTh = [sb(f"xTh{u}", [P, 2, GROUP * P], F32R) for u in range(1)] * 2
        xTl = [sb(f"xTl{u}", [P, 2, GROUP * P], F32R) for u in range(1)] * 2
        gel = [sb(f"gel{u}", [P, GROUP * P]) for u in range(2)]
        Hh = [sb(f"Hh{u}", [P, GROUP * P], F32R) for u in range(3)]
        Hl = [sb(f"Hl{u}", [P, GROUP * P], F32R) for u in range(3)]
        yout = sb("yout", [P, GROUP, D])
        turned = ps("turned", [P, 512])
        hid = [ps(f"hid{i}", [P, 512]) for i in range(3)]
        yps = [ps(f"yps{t}", [P, 512]) for t in range(GROUP)]

        pad_set = sem("pad_set")
        wd_hi = sem("wd_hi")
        wd_split = sem("wd_split")
        tokens_in = [sem(f"tokens_in{u}") for u in range(2)]
        gather_turn = sem("gather_turn")
        gathered = [sem(f"gathered{u}") for u in range(2)]
        x_turned = sem("x_turned")
        xTh_done = sem("xTh_done")
        xT_split = sem("xT_split")
        hid_done = sem("hid_done")
        gelu_done = sem("gelu_done")
        gelu_hi = sem("gelu_hi")
        h_split = sem("h_split")
        chunk_used = sem("chunk_used")
        y_done = sem("y_done")
        y_ready = sem("y_ready")
        y_out = sem("y_out")
        block = ctx.enter_context(nc.Block())

        def schedule(eng, step):
            for s in range(4):
                step(s, s // 2, s % 2)
            with eng.Fori(2, SG // 2) as j:
                step(2 * j, j, 0)
                step(2 * j + 1, j, 1)
            step(SG, SG // 2, 0)

        def has(s, first, last):
            return not isinstance(s, int) or first <= s <= last

        @block.sync
        def _(sp):
            def tokens(n, u):
                wait(sp, x_turned, 2 * (n - 1))
                for t in range(GROUP):
                    row = sp.value_load(c["slot_row"][0:1, bass.ds(GROUP * n + t, 1)], min_val=0,
                                        max_val=E0 * TOKENS - P)
                    sp.dma_start(slot_token[u][:, t:t + 1], A["table"][bass.ds(row, P), :]).then_inc(tokens_in[u], 16)

            def step(s, j, u):
                if has(s, 0, SG - 2):
                    tokens(s + 1, 1 - u)
                if has(s, 1, SG):
                    sp.wait_ge(y_ready, GROUP * s)
                    sp.dma_start(y_t[:, bass.ds(GROUP * s - GROUP, GROUP), :], yout[:]).then_inc(y_out, 16)

            tokens(0, 0)
            for s in range(4):
                step(s, s // 2, s % 2)
            with sp.Fori(2, SG // 2 - 1) as j:
                step(2 * j, j, 0)
                step(2 * j + 1, j, 1)
            for s in range(SG - 2, SG + 1):
                step(s, s // 2, s % 2)
            sp.wait_ge(y_out, 16 * SG)

        @block.gpsimd
        def _(pool):
            pool.memset(pool_pad[:], 0.0).then_inc(pad_set, 1)
            pool.wait_ge(pad_set, 1)

            def step(s, j, u):
                if has(s, 0, SG - 1):
                    wait(pool, x_turned, 2 * s)
                    wait(pool, tokens_in[u], 16 * GROUP * (j + 1))
                    wait(pool, gather_turn, s)
                    pool_turn(pool, pool_pad, 1).then_inc(gather_turn, 1)
                    for t in range(GROUP):
                        pool.indirect_dma_start(
                            xg[u][:, t, :], None, A["xn"],
                            bass.IndirectOffsetOnAxis(ap=slot_token[u][:, t:t + 1], axis=0)).then_inc(gathered[u], 16)

            schedule(pool, step)

        BANK = [0, 1, 2, 0, 1, 2, 0, 1]
        BANK_BEFORE = [-2, -1, -3, 0, 1, 2, 3, 4]

        def used(eng, n, k):
            before = BANK_BEFORE[k]
            if before == -1:
                wait(eng, y_done, GROUP * n)
            elif before < 0:
                wait(eng, chunk_used, (KH - 1) * n + before + 2)
            else:
                wait(eng, chunk_used, (KH - 1) * n + before + 1)

        @block.tensor
        def _(pe):
            def turn_x(n, h, u):
                pe.wait_ge(gathered[u], 16 * GROUP * (h + 1))
                for ic in range(2):
                    wait(pe, xT_split, 2 * n + ic)
                    for t in range(GROUP):
                        ins = pe.transpose(turned[:, t * P:(t + 1) * P], xg[u][:, t, ic * P:ic * P + P], ident[:])
                    ins.then_inc(x_turned, 1)

            def hidden(n, k, u):
                if k == 0:
                    pe.wait_ge(xT_split, 2 * n + 2)
                wait(pe, gelu_hi, KH * n + BANK_BEFORE[k] + 1)
                cols = slice(k * P, k * P + P)
                for ic in range(2):
                    ins = mm3(pe, hid[BANK[k]][:], (w1h[:, ic, cols], w1l[:, ic, cols]),
                              (xTh[u][:, ic, :], xTl[u][:, ic, :]), start=(ic == 0), stop=(ic == 1))
                ins.then_inc(hid_done, 1)

            def experts(n, k, at):
                pe.wait_ge(h_split, KH * n + k + 1)
                if k == 0:
                    wait(pe, y_ready, GROUP * n)
                    if isinstance(n, int) and n == 0:
                        pe.wait_ge(wd_split, E0)
                b = BANK[k]
                for t in range(GROUP):
                    cols = slice(t * P, t * P + P)
                    w = bass.ds(at[t], D)
                    ins = mm3(pe, yps[t][:, 0:D], (Hh[b][:, cols], Hl[b][:, cols]), (wdh[:, k, w], wdl[:, k, w]),
                              start=(k == 0), stop=(k == KH - 1))
                    if k == KH - 1:
                        ins.then_inc(y_done, 1)
                    elif t == GROUP - 1:
                        ins.then_inc(chunk_used, 1)

            def step(s, j, u):
                front, back = has(s, 0, SG - 1), has(s, 1, SG)
                n, v = s - 1, 1 - u
                if back:
                    at = [pe.value_load(c["slot_expert"][0:1, bass.ds(GROUP * n + t, 1)], min_val=0,
                                        max_val=(E0 - 1) * D) for t in range(GROUP)]
                    hidden(n, 0, v)
                    hidden(n, 1, v)
                    for k in range(2, KH):
                        hidden(n, k, v)
                        experts(n, k - 2, at)
                    if front:
                        turn_x(s, j, u)
                    experts(n, KH - 2, at)
                    experts(n, KH - 1, at)
                elif front:
                    turn_x(s, j, u)

            schedule(pe, step)

        @block.scalar
        def _(act):
            raw = wd_raw[:].rearrange("p k (e o) -> p e k o", e=E0)
            high = wdh[:].rearrange("p k (e o) -> p e k o", e=E0)
            for e in range(E0):
                act.activation(high[:, e], raw[:, e], ACT.Copy).then_inc(wd_hi, 1)

            def gelu(n, k):
                act.wait_ge(hid_done, KH * n + k + 1)
                wait(act, h_split, KH * n + k - 1)
                act.activation(gel[k % 2][:], hid[BANK[k]][:], ACT.Gelu, bias=c["b1"][:, k:k + 1]).then_inc(gelu_done, 1)
                used(act, n, k)
                act.activation(Hh[BANK[k]][:], hid[BANK[k]][:], ACT.Gelu, bias=c["b1"][:, k:k + 1]).then_inc(gelu_hi, 1)

            def step(s, j, u):
                front, back = has(s, 0, SG - 1), has(s, 1, SG)
                if back:
                    for k in range(KH):
                        gelu(s - 1, k)
                if front:
                    for ic in range(2):
                        act.wait_ge(x_turned, 2 * s + ic + 1)
                        if ic == 0:
                            wait(act, hid_done, KH * s)
                        act.activation(xTh[u][:, ic, :], turned[:], ACT.Copy).then_inc(xTh_done, 1)

            schedule(act, step)

        @block.vector
        def _(dve):
            raw = wd_raw[:].rearrange("p k (e o) -> p e k o", e=E0)
            high = wdh[:].rearrange("p k (e o) -> p e k o", e=E0)
            raw_low = wdl[:].rearrange("p k (e o) -> p e k o", e=E0)
            for e in range(E0):
                dve.wait_ge(wd_hi, e + 1)
                dve.tensor_tensor(raw_low[:, e], raw[:, e], high[:, e].bitcast(F32), ALU.subtract).then_inc(wd_split, 1)

            def step(s, j, u):
                front, back = has(s, 0, SG - 1), has(s, 1, SG)
                n = s - 1
                if back:
                    for k in range(KH):
                        dve.wait_ge(gelu_hi, KH * n + k + 1)
                        used(dve, n, k)
                        dve.tensor_tensor(Hl[BANK[k]][:], gel[k % 2][:], Hh[BANK[k]][:].bitcast(F32),
                                          ALU.subtract).then_inc(h_split, 1)
                if front:
                    for ic in range(2):
                        dve.wait_ge(xTh_done, 2 * s + ic + 1)
                        dve.tensor_tensor(xTl[u][:, ic, :], turned[:], xTh[u][:, ic, :].bitcast(F32),
                                          ALU.subtract).then_inc(xT_split, 1)
                if back:
                    at = [dve.value_load(c["slot_expert"][0:1, bass.ds(GROUP * n + t, 1)], min_val=0,
                                         max_val=(E0 - 1) * D) for t in range(GROUP)]
                    wait(dve, y_out, 16 * n)
                    for t in range(GROUP):
                        dve.wait_ge(y_done, GROUP * n + t + 1)
                        dve.tensor_tensor(yout[:, t, :], yps[t][:, 0:D], c["bd_bc"][:, bass.ds(at[t], D)],
                                          ALU.add).then_inc(y_ready, 1)

            schedule(dve, step)


HEADS = 4
NODES = 64
C1 = 4
E1 = 4
DC = 64
DH = 32
EH = 8
V1 = DH + 1
NEG = -9e15
SLOPE = 0.2
SCALE = 1.0 / (DH ** 0.5)


def setup_layer1(nc, c, A, sb):
    w = {
        "gat_w": sb("gat_w", [P, 2, D + 2 * HEADS]),
        "norm_w": sb("norm_w", [P, C1]),
        "att_h": sb("att_h", [P, EH, P], F32R),
        "att_l": sb("att_l", [P, EH, P], F32R),
        "val_w": sb("val_w", [P, E1 * DC]),
        "router_w": sb("router_w", [P, C1, E1]),
        "router_b": sb("router_b", [P, E1]),
        "proj_w": sb("proj_w", [P, 2, DC]),
        "proj_b": sb("proj_b", [P, E1, DC]),
        "out_w": sb("out_w", [P, 2, D]),
        "same_graph": sb("same_graph", [P, P]),
        "node": sb("node", [P, NODES]),
        "spread": sb("spread", [48, 2, EH, NODES], BF16),
        "zero": sb("zero", [P, 1]),
    }
    with ExitStack() as ctx:
        def sb2(name, shape, dt=F32):
            return ctx.enter_context(nc.sbuf_tensor("s_" + name, shape, dt))

        def sem(name):
            return ctx.enter_context(nc.semaphore("s_" + name))

        a_bc = sb2("a_bc", [P, 2, HEADS, DC])
        gat_a = sb2("gat_a", [P, 2, 2, D])
        qk = sb2("qk", [DH, 2, E1, 2, 2, DC])
        val = sb2("val", [DC, E1, 2, DC])
        proj = sb2("proj", [DC, E1, DC])
        outw = sb2("outw", [P, 2, D])
        att = sb2("att", [P, EH, DC])
        banks = [ctx.enter_context(nc.psum_tensor(f"s_bank{i}", [P, 512], F32)) for i in range(5)]
        loaded = sem("loaded")
        made = sem("made")
        turned = sem("turned")
        step = sem("step")
        LOADS = 3 + 2 * (1 + C1 + 4 + 2) + 4
        block = ctx.enter_context(nc.Block())

        @block.sync
        def _(sp):
            q4 = A["qkv_w"].rearrange("e (q h r) d -> q h r e d", q=3, h=2)
            n = 0

            def load(dst, src, slow=False):
                nonlocal n
                sp.dma_start(dst, src, allow_slow_non_contiguous=slow).then_inc(loaded, 16)
                n += 1

            load(w["gat_w"][:, :, 0:D], A["gat_w"].rearrange("(c p) o -> p c o", p=P))
            for k in range(2):
                load(a_bc[:, k], A["gat_a"].rearrange("h (k d) -> k h d", k=2)[k].partition_broadcast(P))
            for copy in range(2):
                r = slice(64 * copy, 64 * copy + 64)
                load(w["norm_w"][r, :], A["norm_w"].rearrange("(c d) -> d c", c=C1), True)
                for ch in range(C1):
                    load(w["router_w"][r, ch, :], A["router_w"].rearrange("e (c d) -> c d e", c=C1)[ch], True)
                for q in range(2):
                    for h in range(2):
                        load(qk[:, q, :, h, copy, :], q4[q, h])
                for h in range(2):
                    load(val[DH * h:DH * h + DH, :, copy, :], q4[2, h])
            load(w["router_b"][:], A["router_b"].partition_broadcast(P))
            load(proj[:], A["proj_w"].rearrange("e o d -> o e d"))
            load(w["proj_b"][:], A["proj_b"].partition_broadcast(P))
            load(outw[:], A["out_w"].rearrange("(b p) o -> p b o", p=P))
            assert n == LOADS

        @block.gpsimd
        def _(pool):
            n = 0

            def link(ins):
                nonlocal n
                n += 1
                ins.then_inc(made, 1)
                pool.wait_ge(made, n)

            link(pool.memset(w["same_graph"][:], 0.0))
            for g in range(2):
                r = slice(64 * g, 64 * g + 64)
                link(pool.memset(w["same_graph"][r, r], 1.0))
            link(pool.tensor_tensor(w["node"][:], c["ident"][:, 0:64], c["ident"][:, 64:128], ALU.add))
            link(pool.memset(w["spread"][:], 0.0))
            for part in range(3):
                v = w["spread"][:].rearrange("r c e s -> r (c e) s")
                link(pool.affine_select(out=v, in_=v, compare_op=ALU.not_equal, fill=1.0, base=-16 * part,
                                        pattern=[[-1, 16], [0, NODES]], channel_multiplier=1))
            link(pool.memset(w["zero"][:], 0.0))

        @block.tensor
        def _(pe):
            pe.wait_ge(loaded, 16 * LOADS)
            for e in range(E1):
                for h in range(2):
                    pe.matmul(banks[0][:, (2 * e + h) * DC:(2 * e + h + 1) * DC],
                              qk[:, 1, e, h, :, :].rearrange("r a d -> r (a d)"), qk[:, 0, e, h, 0, :],
                              start=True, stop=True)
            for e in range(E1):
                pe.transpose(banks[1][:, e * DC:(e + 1) * DC], val[:, e, :, :].rearrange("r a d -> r (a d)"),
                             c["ident"][0:DC, 0:DC])
            for b in range(2):
                pe.transpose(banks[2][:, b * DC:(b + 1) * DC],
                             proj[:, 2 * b:2 * b + 2, :].rearrange("o e d -> o (e d)"), c["ident"][0:DC, 0:DC])
            for b in range(2):
                for k in range(2):
                    ins = pe.transpose(banks[3 + k][:, b * P:(b + 1) * P], outw[:, b, k * P:(k + 1) * P], c["ident"][:])
            ins.then_inc(turned, 1)

        @block.vector
        def _(dve):
            st = Steps(dve, step, 0)
            dve.wait_ge(loaded, 16 * LOADS)
            for k in range(2):
                for ic in range(2):
                    ins = dve.tensor_tensor(gat_a[:, k, ic, :], w["gat_w"][:, ic, 0:D],
                                            a_bc[:, k].rearrange("p h d -> p (h d)"), ALU.mult)
            st.link(ins)
            for k in range(2):
                for ic in range(2):
                    dve.tensor_reduce(w["gat_w"][:, ic, D + HEADS * k:D + HEADS * k + HEADS],
                                      gat_a[:, k, ic, :].rearrange("p (h d) -> p h d", h=HEADS), AX.X, ALU.add)
            dve.memset(w["att_h"][:].bitcast(F32), 0.0)
            st.link(dve.memset(w["att_l"][:].bitcast(F32), 0.0))
            dve.wait_ge(turned, 1)
            st.link(dve.tensor_scalar(att[:], banks[0][:].rearrange("p (e d) -> p e d", e=EH), SCALE, None, ALU.mult))
            for g in range(2):
                r = slice(64 * g, 64 * g + 64)
                ins = dve.tensor_copy(w["att_h"][r, :, r], att[r])
            st.link(ins)
            for g in range(2):
                r = slice(64 * g, 64 * g + 64)
                dve.tensor_tensor(w["att_l"][r, :, r], att[r], w["att_h"][r, :, r].bitcast(F32), ALU.subtract)
            dve.tensor_copy(w["val_w"][:], banks[1][:, 0:E1 * DC])
            dve.tensor_copy(w["proj_w"][:], banks[2][:, 0:2 * DC].rearrange("p (b o) -> p b o", b=2))
            for k in range(2):
                dve.tensor_copy(w["out_w"][:, k, :], banks[3 + k][:, 0:D])
    return w


def layer1(nc, c, w, A):
    x1_t = A["x1"].rearrange("(t p) d -> p t d", p=P)
    out_t = A["out"].rearrange("(t g) m d -> (g m) t d", g=2)
    adj_t = A["adj"].rearrange("(t g) n m -> (g n) t m", g=2)
    with ExitStack() as ctx:
        def sb(name, shape, dt=F32):
            return ctx.enter_context(nc.sbuf_tensor("l_" + name, shape, dt))

        def ps(name, shape, dt=F32):
            return ctx.enter_context(nc.psum_tensor("l_" + name, shape, dt))

        def sem(name):
            return ctx.enter_context(nc.semaphore("l_" + name))

        ident, ident_bf = c["ident"], c["ident_bf"]
        yrow = [sb(f"yrow{u}", [P, 1], I32) for u in range(2)]
        prob = [sb(f"prob{u}", [P, 1]) for u in range(2)]
        pool_pad = sb("pool_pad", [P, 3])
        dve_pad = sb("dve_pad", [P, 1])
        x1 = [sb(f"x1{u}", [P, D]) for u in range(2)]
        yin = [sb(f"yin{u}", [P, D]) for u in range(2)]
        adj = [sb(f"adj{u}", [P, NODES]) for u in range(2)]
        x2 = [sb(f"x2{u}", [P, D]) for u in range(2)]
        stats = sb("stats", [P, 6])
        mv = sb("mv", [P, 2])
        seed_i = sb("seed_i", [P, 2], I32)
        rs_tmp = sb("rs_tmp", [P, 2])
        rs_var = sb("rs_var", [P, 2])
        res_scale = sb("res_scale", [P, 2])
        x3n = sb("x3n", [P, D])
        xa = sb("xa", [P, D])
        xaT = sb("xaT", [P, 2, P])
        hx = sb("hx", [P, HEADS, DC + 2])
        e8 = sb("e8", [P, 2, HEADS])
        ediag = sb("ediag", [P, HEADS, NODES])
        edge = sb("edge", [P, NODES])
        noedge = sb("noedge", [P, NODES])
        score = sb("score", [P, HEADS, NODES])
        leaky = sb("leaky", [P, HEADS, NODES])
        masked = sb("masked", [P, HEADS, NODES])
        masked2 = sb("masked2", [P, HEADS, NODES])
        gmax = sb("gmax", [P, HEADS])
        gshift = sb("gshift", [P, HEADS, NODES])
        gprob = sb("gprob", [P, HEADS, P])
        gprobT = sb("gprobT", [P, HEADS, P])
        gsum = sb("gsum", [P, HEADS])
        gout = sb("gout", [P, HEADS, DC])
        x3 = [sb(f"x3{u}", [P, D]) for u in range(2)]
        xpad = sb("xpad", [P, C1, P])
        xbd = sb("xbd", [P, C1, P])
        xmh = sb("xmh", [P, C1, NODES], F32R)
        xml = sb("xml", [P, C1, NODES], F32R)
        wk = sb("wk", [P, C1, EH, NODES])
        vd = sb("vd", [P, 2, C1, E1, 2 * V1])
        rlog = sb("rlog", [P, E1])
        rmax = sb("rmax", [P, 1])
        rexp = sb("rexp", [P, E1])
        rsum = sb("rsum", [P, 1])
        gate = sb("gate", [P, E1])
        gbias = sb("gbias", [P, DC])
        nmax = sb("nmax", [P, 2 * EH])
        nrest = sb("nrest", [P, 2 * EH])
        nparts = sb("nparts", [P, 8, 2 * EH], BF16)
        nmaxT = sb("nmaxT", [48, P], BF16)
        pex = [sb(f"pex{i}", [P, E1, P]) for i in range(2)]
        pT = [sb(f"pT{i}", [P, E1, P]) for i in range(2)]
        den = sb("den", [P, E1, 2])
        fac = sb("fac", [P, E1, 2])
        yh = sb("yh", [P, C1, E1, 2, DH])
        yT = sb("yT", [P, 2, 512])
        oc = sb("oc", [P, C1, DC])
        oT = sb("oT", [P, 2, P])
        final = [sb(f"final{u}", [P, D]) for u in range(2)]

        W0 = ps("W0", [P, 512])
        W1 = ps("W1", [P, 512])
        W2 = ps("W2", [P, 512])
        S = ps("S", [P, 3, 512])
        Y = [ps(f"Y{i}", [P, 512]) for i in range(2)]
        SBANK = [2, 0, 1, 2]

        names = """zeroed picked gather_turn x2_ready xa_ready edges_ready gT_done xaT_ready gH_done
            hx_ready ediag_ready gB_done leaky_ready masked_ready gshift_ready gexp_done gP_done gprobT_ready gV_done
            x3_ready xpad_ready res_ready T4_done xbd_ready xm_ready V_done vd_ready yT_done yT0_ready yT1_ready w_done
            we_ready wo_ready proj_done oc_ready router_done rlog_read rshift_ready rexp_done S_done oT_done oT_ready
            nparts_ready nT_done nmaxT_ready A_done exp_done out_done final_ready PT_done pTa_ready pTb_ready
            PV_done yh_ready a_step n_step r_step m_step m2_step gmax_step y_step  hi_step x_step""".split()
        s_ = {n: sem(n) for n in names}
        x1_in = [sem(f"x1_in{u}") for u in range(2)]
        adj_in = [sem(f"adj_in{u}") for u in range(2)]
        y_in = [sem(f"y_in{u}") for u in range(2)]
        out_out = [sem(f"out_out{u}") for u in range(2)]
        block = ctx.enter_context(nc.Block())

        def upto(tile, per=1, part=None):
            part = per if part is None else part
            if isinstance(tile, int):
                return 0 if tile < 0 else per * TILES if tile >= TILES else per * tile + part
            return per * tile + part

        def schedule(eng, step):
            for s in range(4):
                step(s, s // 2, s % 2)
            with eng.Fori(2, 31) as j:
                step(2 * j, j, 0)
                step(2 * j + 1, j, 1)
            for s in range(62, TILES + 2):
                step(s, s // 2, s % 2)

        def runs(s, lag):
            return not isinstance(s, int) or 0 <= s - lag < TILES

        @block.sync
        def _(sp):
            def load(n, u):
                wait(sp, s_["x2_ready"], upto(n - 2))
                wait(sp, s_["edges_ready"], upto(n - 2))
                sp.dma_start(x1[u][:], x1_t[:, bass.ds(n, 1), :]).then_inc(x1_in[u], 16)
                sp.dma_start(adj[u][:], adj_t[:, bass.ds(n, 1), :]).then_inc(adj_in[u], 16)

            def step(s, j, u):
                if runs(s, -2):
                    load(s + 2, u)
                if runs(s, 2):
                    sp.wait_ge(s_["final_ready"], upto(s - 2))
                    sp.dma_start(out_t[:, bass.ds(s - 2, 1), :], final[u][:]).then_inc(out_out[u], 16)

            load(0, 0)
            load(1, 1)
            schedule(sp, step)
            for u in range(2):
                sp.wait_ge(out_out[u], 16 * (TILES // 2))

        @block.gpsimd
        def _(pool):
            n = 0
            for buf, value in ((pool_pad, 0.0), (gprob, 0.0), (xpad, 0.0), (hx, 1.0), (vd, 0.0), (nparts, 0.0)):
                pool.memset(buf[:], value).then_inc(s_["zeroed"], 1)
            pool.wait_ge(s_["zeroed"], 6)
            for h in range(2):
                r = slice(64 * h, 64 * h + 64)
                v = vd[:].rearrange("p g c e k -> p (g c e) k")
                pool.memset(v[r, :, V1 * h + DH:V1 * h + DH + 1], 1.0).then_inc(s_["zeroed"], 1)
            pool.wait_ge(s_["zeroed"], 8)

            def gather(n, u):
                wait(pool, s_["picked"], upto(n))
                pool_turn(pool, pool_pad, 1 + u).then_inc(s_["gather_turn"], 1)
                pool.indirect_dma_start(yin[u][:], None, A["y"],
                                        bass.IndirectOffsetOnAxis(ap=yrow[u][:], axis=0)).then_inc(y_in[u], 16)

            def spread_ej(n):
                pool.wait_ge(s_["hx_ready"], upto(n, 2))
                wait(pool, s_["gB_done"], upto(n - 1))
                pool.tensor_tensor(ediag[:], e8[:, 1, :].unsqueeze(2).to_broadcast([P, HEADS, NODES]),
                                   w["node"][:].unsqueeze(1).to_broadcast([P, HEADS, NODES]),
                                   ALU.mult).then_inc(s_["ediag_ready"], 1)
                pool.wait_ge(s_["ediag_ready"], upto(n))

            def mask(n):
                pool.wait_ge(s_["leaky_ready"], upto(n))
                pool.wait_ge(s_["edges_ready"], upto(n))
                wait(pool, s_["gshift_ready"], upto(n - 1))
                pool.tensor_tensor(masked[:], leaky[:], edge[:].unsqueeze(1).to_broadcast([P, HEADS, NODES]),
                                   ALU.mult).then_inc(s_["m_step"], 1)
                pool.wait_ge(s_["m_step"], upto(n))
                pool.tensor_tensor(masked2[:], masked[:], noedge[:].unsqueeze(1).to_broadcast([P, HEADS, NODES]),
                                   ALU.add).then_inc(s_["masked_ready"], 1)
                pool.wait_ge(s_["masked_ready"], upto(n))

            def moving_x(n):
                pool.wait_ge(s_["xbd_ready"], upto(n))
                wait(pool, s_["w_done"], upto(n - 1, 4))
                for g in range(2):
                    r = slice(64 * g, 64 * g + 64)
                    ins = pool.tensor_tensor(xmh[r], xbd[r, :, 64 * g:64 * g + 64],
                                             w["zero"][r].unsqueeze(2).to_broadcast([64, C1, NODES]), ALU.add)
                    ins.then_inc(s_["hi_step"], 1)
                    pool.wait_ge(s_["hi_step"], upto(n, 2, g + 1))
                for g in range(2):
                    r = slice(64 * g, 64 * g + 64)
                    ins = pool.tensor_tensor(xml[r], xbd[r, :, 64 * g:64 * g + 64], xmh[r].bitcast(F32), ALU.subtract)
                    ins.then_inc(s_["xm_ready"], 1)
                    pool.wait_ge(s_["xm_ready"], upto(n, 2, g + 1))

            def step(s, j, u):
                if runs(s, 1):
                    moving_x(s - 1)
                if runs(s, -1):
                    gather(s + 1, 1 - u)
                if runs(s, 0):
                    spread_ej(s)
                    mask(s)

            gather(0, 0)
            schedule(pool, step)

        @block.tensor
        def _(pe):
            def free(name, tile, per=1, part=None):
                wait(pe, s_[name], upto(tile, per, part))

            def need(name, tile, per=1, part=None):
                wait(pe, s_[name], upto(tile, per, part))

            pe.wait_ge(s_["zeroed"], 8)

            def turn_xpad(f):
                need("xpad_ready", f)
                free("pTa_ready", f - 1, 3, 2)
                for ch in range(C1):
                    ins = pe.transpose(W0[:, ch * P:(ch + 1) * P], xpad[:, ch, :], ident[:])
                ins.then_inc(s_["T4_done"], 1)

            def turn_xa(g):
                need("xa_ready", g)
                free("pTa_ready", g - 2, 3)
                for ic in range(2):
                    ins = pe.transpose(W1[:, ic * P:(ic + 1) * P], xa[:, ic * P:(ic + 1) * P], ident[:])
                ins.then_inc(s_["gT_done"], 1)

            def values(f):
                need("xbd_ready", f)
                free("exp_done", f - 1, 4, 3)
                for ch in range(C1):
                    ins = pe.matmul(S[:, ch // 2, (ch % 2) * D:(ch % 2) * D + D], xbd[:, ch, :], w["val_w"][:],
                                    start=True, stop=True)
                ins.then_inc(s_["V_done"], 1)

            def turn_y(r):
                need("yh_ready", r, 4)
                free("xbd_ready", r + 1)
                free("xaT_ready", r + 2)
                for half, bank in enumerate((W0, W1)):
                    for q in range(4):
                        ch, k = 2 * half + q // 2, q % 2
                        ins = pe.transpose(bank[:, q * P:(q + 1) * P],
                                           yh[:, ch, 2 * k:2 * k + 2].rearrange("p e h d -> p (e h d)"), ident[:])
                    ins.then_inc(s_["yT_done"], 1)

            def att_keys(f, k):
                if k == 0:
                    need("xm_ready", f, 2)
                    free("yT0_ready", f - 1)
                elif k == 1:
                    free("yT1_ready", f - 1)
                    free("xaT_ready", f + 1)
                elif k == 2:
                    free("we_ready", f, 2, 1)
                else:
                    free("wo_ready", f, 2, 1)
                bank = (W0, W1)[k % 2]
                for e in range(2):
                    ins = mm3(pe, bank[:, e * 256:(e + 1) * 256],
                              (w["att_h"][:, 2 * k + e, :], w["att_l"][:, 2 * k + e, :]),
                              (xmh[:].rearrange("p c m -> p (c m)"), xml[:].rearrange("p c m -> p (c m)")))
                ins.then_inc(s_["w_done"], 1)

            def project(r):
                need("yT0_ready", r)
                need("yT1_ready", r)
                free("x3_ready", r + 1)
                for ch in range(C1):
                    for k in range(2):
                        q = 2 * (ch % 2) + k
                        ins = pe.matmul(W2[:, ch * DC:(ch + 1) * DC], yT[:, ch // 2, q * P:(q + 1) * P],
                                        w["proj_w"][:, k, :], start=(k == 0), stop=(k == 1))
                ins.then_inc(s_["proj_done"], 1)

            def route(f):
                free("yh_ready", f - 1, 4)
                for ch in range(C1):
                    ins = pe.matmul(Y[1][:, 0:E1], xbd[:, ch, :], w["router_w"][:, ch, :], start=(ch == 0),
                                    stop=(ch == C1 - 1))
                ins.then_inc(s_["router_done"], 1)

            def scores(f, ch):
                if ch == 0:
                    need("we_ready", f, 2)
                    need("wo_ready", f, 2)
                    free("exp_done", f - 1, 4)
                elif ch < 3:
                    free("vd_ready", f)
                else:
                    free("exp_done", f, 4, 1)
                pe.matmul(S[:, SBANK[ch], :], xbd[:, ch, :], wk[:, ch].rearrange("p e m -> p (e m)"),
                          start=True, stop=False, skip_group_check=True).then_inc(s_["S_done"], 1)

            def turn_oc(r):
                need("oc_ready", r)
                free("we_ready", r + 1, 2)
                for k in range(2):
                    ins = pe.transpose(W0[:, k * P:(k + 1) * P],
                                       oc[:].rearrange("p c o -> p (c o)")[:, k * P:(k + 1) * P], ident[:])
                ins.then_inc(s_["oT_done"], 1)

            def graph_h(g):
                need("xaT_ready", g)
                free("wo_ready", g - 1, 2)
                for ic in range(2):
                    ins = pe.matmul(W1[:, 0:D + 2 * HEADS], xaT[:, ic, :], w["gat_w"][:, ic, :], start=(ic == 0),
                                    stop=(ic == 1))
                ins.then_inc(s_["gH_done"], 1)

            def turn_max(f, half):
                need("nparts_ready", f, 2, half + 1)
                if half == 0:
                    free("oc_ready", f - 1)
                    free("x3_ready", f)
                else:
                    free("leaky_ready", f + 1)
                    free("nmaxT_ready", f, 2, 1)
                pe.transpose(W2[:, 0:64].bitcast(BF16), nparts[:].rearrange("p k m -> p (k m)"),
                             ident_bf[:]).then_inc(s_["nT_done"], 1)

            def subtract_max(f, half):
                need("nmaxT_ready", f, 2, half + 1)
                for k in range(2):
                    pe.matmul(S[:, SBANK[2 * half + k], :], nmaxT[:], w["spread"][:, k].rearrange("r e m -> r (e m)"),
                              start=False, stop=True, skip_group_check=True).then_inc(s_["A_done"], 1)

            def out_project(r):
                need("oT_ready", r)
                free("yh_ready", r, 4, 3)
                for k in range(2):
                    ins = pe.matmul(Y[0][:, 0:D], oT[:, k, :], w["out_w"][:, k, :], start=(k == 0), stop=(k == 1))
                ins.then_inc(s_["out_done"], 1)

            def graph_ej(g):
                need("ediag_ready", g)
                free("nmaxT_ready", g - 1, 2, 1)
                free("x3_ready", g - 1)
                pe.matmul(W2[:, 0:HEADS * NODES], w["same_graph"][:], ediag[:].rearrange("p h m -> p (h m)"),
                          start=True, stop=True).then_inc(s_["gB_done"], 1)

            def turn_probs(f, ch):
                need("exp_done", f, 4, ch + 1)
                if ch == 0:
                    free("oT_ready", f - 1)
                elif ch == 1:
                    free("hx_ready", f + 1, 2)
                elif ch == 2:
                    free("pTa_ready", f, 3, 1)
                else:
                    free("pTb_ready", f)
                for e in range(E1):
                    ins = pe.transpose((W0, W1)[ch % 2][:, e * P:(e + 1) * P], pex[ch % 2][:, e, :], ident[:])
                ins.then_inc(s_["PT_done"], 1)

            def head_out(f, ch):
                if ch == 1:
                    need("pTb_ready", f)
                    free("rlog_read", f)
                else:
                    need("pTa_ready", f, 3, max(ch, 1))
                    if ch == 0:
                        free("final_ready", f - 1)
                        free("yh_ready", f - 1, 4, 3)
                    else:
                        free("yh_ready", f, 4, ch - 1)
                for e in range(E1):
                    for g in range(2):
                        r = slice(64 * g, 64 * g + 64)
                        ins = pe.matmul(Y[ch % 2][r, e * 2 * V1:(e + 1) * 2 * V1], pT[ch % 2][:, e, r],
                                        vd[:, g, ch, e, :], start=True, stop=True)
                ins.then_inc(s_["PV_done"], 1)

            def turn_graph_prob(g):
                need("gexp_done", g)
                free("nmaxT_ready", g - 1, 2)
                for h in range(HEADS):
                    ins = pe.transpose(W2[:, h * P:(h + 1) * P], gprob[:, h, :], ident[:])
                ins.then_inc(s_["gP_done"], 1)

            def graph_out(g):
                need("gprobT_ready", g)
                for h in range(HEADS):
                    ins = pe.matmul(W2[:, h * (DC + 2):(h + 1) * (DC + 2)], gprobT[:, h, :], hx[:, h, :],
                                    start=True, stop=True)
                ins.then_inc(s_["gV_done"], 1)

            def step(s, j, u):
                graph, head, out = runs(s, 0), runs(s, 1), runs(s, 2)
                g, f, r = s, s - 1, s - 2
                if head:
                    turn_xpad(f)
                if graph:
                    turn_xa(g)
                if head:
                    values(f)
                if out:
                    turn_y(r)
                if head:
                    for k in range(4):
                        att_keys(f, k)
                if out:
                    project(r)
                if head:
                    route(f)
                    for ch in range(3):
                        scores(f, ch)
                if out:
                    turn_oc(r)
                if graph:
                    graph_h(g)
                if head:
                    turn_max(f, 0)
                    subtract_max(f, 0)
                if out:
                    out_project(r)
                if graph:
                    graph_ej(g)
                if head:
                    scores(f, 3)
                    turn_probs(f, 0)
                    head_out(f, 0)
                    turn_max(f, 1)
                    turn_probs(f, 1)
                    head_out(f, 1)
                    subtract_max(f, 1)
                if graph:
                    turn_graph_prob(g)
                if head:
                    turn_probs(f, 2)
                    head_out(f, 2)
                if graph:
                    graph_out(g)
                if head:
                    turn_probs(f, 3)
                    head_out(f, 3)

            schedule(pe, step)

        @block.scalar
        def _(act):
            def need(name, tile, per=1, part=None):
                wait(act, s_[name], upto(tile, per, part))

            free = need
            act.wait_ge(s_["zeroed"], 8)

            def copy_xaT(g):
                need("gT_done", g)
                free("gH_done", g - 1)
                act.activation(xaT[:], W1[:, 0:D].rearrange("p (c m) -> p c m", c=2), ACT.Copy).then_inc(s_["xaT_ready"], 1)

            def place_values(f):
                need("V_done", f)
                free("PV_done", f - 1, 4)
                src = S[:, 0:2, :].rearrange("p b (c e h k) -> p (b c e) h k", c=2, e=E1, h=2)
                for g in range(2):
                    for h in range(2):
                        dst = vd[64 * h:64 * h + 64, g].rearrange("p c e k -> p (c e) k")[:, :, V1 * h:V1 * h + DH]
                        ins = act.activation(dst, src[64 * g:64 * g + 64, :, h, :], ACT.Copy)
                ins.then_inc(s_["vd_ready"], 1)

            def copy_yT(r):
                need("yT_done", r, 2, 1)
                free("proj_done", r - 1)
                act.activation(yT[:, 0, :], W0[:], ACT.Copy).then_inc(s_["yT0_ready"], 1)

            def copy_keys(f, k):
                need("w_done", f, 4, k + 1)
                free("S_done", f - 1, 4)
                act.activation(wk[:, :, 2 * k:2 * k + 2, :].rearrange("p c e m -> p e c m"),
                               W0[:].rearrange("p (e c m) -> p e c m", e=2, c=C1), ACT.Copy).then_inc(s_["we_ready"], 1)

            def route_exp(f):
                need("rshift_ready", f)
                act.activation(rexp[:], rlog[:], ACT.Exp).then_inc(s_["rexp_done"], 1)

            def copy_oT(r):
                need("oT_done", r)
                free("out_done", r - 1)
                act.activation(oT[:], W0[:, 0:D].rearrange("p (c m) -> p c m", c=2), ACT.Copy).then_inc(s_["oT_ready"], 1)

            def copy_h(g):
                need("gH_done", g)
                free("gV_done", g - 1)
                free("ediag_ready", g - 1)
                free("leaky_ready", g - 1)
                act.activation(hx[:, :, 0:DC], W1[:, 0:D].rearrange("p (h d) -> p h d", h=HEADS), ACT.Copy).then_inc(s_["hx_ready"], 1)
                act.activation(e8[:], W1[:, D:D + 2 * HEADS].rearrange("p (k h) -> p k h", k=2), ACT.Copy).then_inc(s_["hx_ready"], 1)

            def copy_max(f, half):
                need("nT_done", f, 2, half + 1)
                if half:
                    free("A_done", f, 4, 2)
                else:
                    free("A_done", f - 1, 4)
                act.activation(nmaxT[:], W2[0:48, 0:64].bitcast(BF16), ACT.Copy).then_inc(s_["nmaxT_ready"], 1)

            def head_exp(f, ch):
                need("A_done", f, 4, ch + 1)
                if ch < 2:
                    free("PT_done", f - 1, 4, ch + 3)
                else:
                    free("PT_done", f, 4, ch - 1)
                act.activation(pex[ch % 2][:], S[:, SBANK[ch], :].rearrange("p (e m) -> p e m", e=E1), ACT.Exp)\
                   .then_inc(s_["exp_done"], 1)

            def copy_pT(f, ch):
                need("PT_done", f, 4, ch + 1)
                if ch < 2:
                    free("PV_done", f - 1, 4, ch + 3)
                else:
                    free("PV_done", f, 4, ch - 1)
                act.activation(pT[ch % 2][:], (W0, W1)[ch % 2][:].rearrange("p (e m) -> p e m", e=E1), ACT.Copy)\
                   .then_inc(s_["pTa_ready"], 1)

            def graph_exp(g):
                need("gshift_ready", g)
                free("gP_done", g - 1)
                for k in range(2):
                    r = slice(64 * k, 64 * k + 64)
                    ins = act.activation(gprob[r, :, r], gshift[r], ACT.Exp)
                ins.then_inc(s_["gexp_done"], 1)

            def copy_graph_probT(g):
                need("gP_done", g)
                free("gV_done", g - 1)
                act.activation(gprobT[:], W2[:].rearrange("p (h m) -> p h m", h=HEADS), ACT.Copy).then_inc(s_["gprobT_ready"], 1)

            def step(s, j, u):
                graph, head, out = runs(s, 0), runs(s, 1), runs(s, 2)
                g, f, r = s, s - 1, s - 2
                if graph:
                    copy_xaT(g)
                if head:
                    place_values(f)
                if out:
                    copy_yT(r)
                if head:
                    copy_keys(f, 0)
                    copy_keys(f, 2)
                    route_exp(f)
                if out:
                    copy_oT(r)
                if graph:
                    copy_h(g)
                if head:
                    copy_max(f, 0)
                    head_exp(f, 0)
                    head_exp(f, 1)
                    copy_pT(f, 0)
                if graph:
                    graph_exp(g)
                if head:
                    copy_max(f, 1)
                    head_exp(f, 2)
                    head_exp(f, 3)
                if graph:
                    copy_graph_probT(g)
                if head:
                    copy_pT(f, 2)
                    copy_pT(f, 3)

            schedule(act, step)

        @block.vector
        def _(dve):
            def need(name, tile, per=1, part=None):
                wait(dve, s_[name], upto(tile, per, part))

            free = need
            dve.wait_ge(s_["zeroed"], 8)

            def pick(n, u):
                free("x2_ready", n - 2)
                free("gather_turn", n - 2)
                dve.tensor_copy(prob[u][:], c["prob"][:, bass.ds(n, 1)])
                dve.tensor_copy(yrow[u][:], c["yrow"][:, bass.ds(n, 1)]).then_inc(s_["picked"], 1)

            def moments(st, x):
                st.link(dve.bn_stats(stats[:], x))
                dve.memset(dve_pad[:], 0.0)
                st.link(dve.bn_aggr(mv[:], stats[:]))

            N_LINKS = 3 + RSQRT_LINKS

            def expert_sum(n, h, u):
                st = Steps(dve, s_["a_step"], N_LINKS * n)
                dve.wait_ge(x1_in[u], 16 * (h + 1))
                dve.wait_ge(y_in[u], 16 * (h + 1))
                dve.scalar_tensor_tensor(x2[u][:], yin[u][:], prob[u][:], x1[u][:], ALU.mult, ALU.add).then_inc(s_["x2_ready"], 1)
                need("x2_ready", n)
                moments(st, x2[u][:])
                st.link(dve.tensor_scalar(rs_var[:, 0:1], mv[:, 1:2], EPS, None, ALU.add))
                rsqrt(dve, st, rs_var[:, 0:1], seed_i[:, 0:1], rs_tmp[:, 0:1])
                free("gT_done", n - 1)
                dve.tensor_scalar(xa[:], x2[u][:], mv[:, 0:1], seed_i[:, 0:1].bitcast(F32), ALU.subtract, ALU.mult).then_inc(s_["xa_ready"], 1)
                assert st.n == N_LINKS

            def copy_x(f):
                need("T4_done", f)
                free("S_done", f - 1, 4)
                dve.tensor_tensor(xbd[:], W0[:].rearrange("p (c m) -> p c m", c=C1),
                                  w["norm_w"][:].unsqueeze(2).to_broadcast([P, C1, P]), ALU.mult).then_inc(s_["xbd_ready"], 1)

            def copy_yT(r):
                need("yT_done", r, 2)
                free("proj_done", r - 1)
                dve.tensor_copy(yT[:, 1, :], W1[:]).then_inc(s_["yT1_ready"], 1)

            def copy_keys(f, k):
                need("w_done", f, 4, k + 1)
                free("S_done", f - 1, 4)
                dve.tensor_copy(wk[:, :, 2 * k:2 * k + 2, :].rearrange("p c e m -> p e c m"),
                                W1[:].rearrange("p (e c m) -> p e c m", e=2, c=C1)).then_inc(s_["wo_ready"], 1)

            def add_bias(r):
                need("proj_done", r)
                free("oT_done", r - 1)
                dve.tensor_tensor(oc[:], W2[:, 0:D].rearrange("p (c o) -> p c o", c=C1),
                                  gbias[:].unsqueeze(1).to_broadcast([P, C1, DC]), ALU.add).then_inc(s_["oc_ready"], 1)

            R_LINKS = 8

            def route_shift(f):
                st = Steps(dve, s_["r_step"], R_LINKS * f)
                need("router_done", f)
                dve.tensor_tensor(rlog[:], Y[1][:, 0:E1], w["router_b"][:], ALU.add).then_inc(s_["rlog_read"], 1)
                need("rlog_read", f)
                st.link(dve.tensor_reduce(rmax[:], rlog[:], AX.X, ALU.max))
                dve.tensor_scalar(rlog[:], rlog[:], rmax[:], None, ALU.subtract).then_inc(s_["rshift_ready"], 1)
                return st

            def route_gate(f, st):
                need("rexp_done", f)
                st.link(dve.tensor_reduce(rsum[:], rexp[:], AX.X, ALU.add))
                st.link(dve.reciprocal(rsum[:], rsum[:]))
                st.link(dve.tensor_scalar(gate[:], rexp[:], rsum[:], None, ALU.mult))
                st.link(dve.tensor_scalar(gbias[:], w["proj_b"][:, 0, :], gate[:, 0:1], None, ALU.mult))
                for e in range(1, E1):
                    ins = dve.scalar_tensor_tensor(gbias[:], w["proj_b"][:, e, :], gate[:, e:e + 1], gbias[:],
                                                   ALU.mult, ALU.add)
                    if e < E1 - 1:
                        st.link(ins)
                    else:
                        st.done(ins)
                assert st.n == R_LINKS

            def head_max(f, ch):
                need("S_done", f, 4, ch + 1)
                return dve.tensor_reduce(nmax[:, (ch % 2) * EH:(ch % 2) * EH + EH],
                                         S[:, SBANK[ch], :].rearrange("p (e m) -> p e m", e=EH), AX.X, ALU.max)

            M_LINKS = 5

            def max_parts(f, half):
                st = Steps(dve, s_["m2_step"], 2 * M_LINKS * f + M_LINKS * half)
                head_max(f, 2 * half)
                st.link(head_max(f, 2 * half + 1))
                if half:
                    free("nT_done", f, 2, 1)
                else:
                    free("nT_done", f - 1, 2)
                st.link(dve.tensor_scalar(nparts[:, 0, :], nmax[:], -1.0, None, ALU.mult))
                st.link(dve.scalar_tensor_tensor(nrest[:], nmax[:], -1.0, nparts[:, 0, :], ALU.mult, ALU.subtract))
                st.link(dve.tensor_copy(nparts[:, 1, :], nrest[:]))
                st.link(dve.tensor_tensor(nrest[:], nrest[:], nparts[:, 1, :], ALU.subtract))
                dve.tensor_copy(nparts[:, 2, :], nrest[:]).then_inc(s_["nparts_ready"], 1)
                assert st.n == M_LINKS

            def finish(r, h, u):
                need("out_done", r)
                need("res_ready", r)
                wait(dve, out_out[u], 16 * h)
                dve.tensor_tensor(final[u][:], Y[0][:, 0:D], x3[u][:], ALU.add).then_inc(s_["final_ready"], 1)

            def edges(g, h, u):
                dve.wait_ge(adj_in[u], 16 * (h + 1))
                free("masked_ready", g - 1)
                dve.tensor_scalar(edge[:], adj[u][:], 0.0, None, ALU.is_gt)
                dve.tensor_scalar(noedge[:], adj[u][:], 0.0, NEG, ALU.is_le, ALU.mult).then_inc(s_["edges_ready"], 1)

            def graph_scores(g):
                need("gB_done", g)
                free("masked_ready", g - 1)
                dve.tensor_tensor(score[:], W2[:, 0:HEADS * NODES].rearrange("p (h m) -> p h m", h=HEADS),
                                  e8[:, 0, :].unsqueeze(2).to_broadcast([P, HEADS, NODES]), ALU.add).then_inc(s_["n_step"], 1)
                need("n_step", g)
                dve.scalar_tensor_tensor(leaky[:], score[:], SLOPE, score[:], ALU.mult, ALU.max).then_inc(s_["leaky_ready"], 1)

            def graph_shift(g):
                need("masked_ready", g)
                dve.tensor_reduce(gmax[:], masked2[:], AX.X, ALU.max).then_inc(s_["gmax_step"], 1)
                need("gmax_step", g)
                free("gexp_done", g - 1)
                dve.tensor_tensor(gshift[:], masked2[:], gmax[:].unsqueeze(2).to_broadcast([P, HEADS, NODES]),
                                  ALU.subtract).then_inc(s_["gshift_ready"], 1)

            def copy_pT(f):
                need("PT_done", f, 4, 2)
                free("PV_done", f - 1, 4)
                dve.tensor_copy(pT[1][:], W1[:].rearrange("p (e m) -> p e m", e=E1)).then_inc(s_["pTb_ready"], 1)

            def scale_heads(f, ch):
                st = Steps(dve, s_["y_step"], 8 * f + 2 * ch)
                need("PV_done", f, 4, ch + 1)
                if ch == 0:
                    free("yT_done", f - 1, 2)
                v = Y[ch % 2][:, 0:E1 * 2 * V1].rearrange("p (e h k) -> p e h k", e=E1, h=2)
                st.link(dve.reciprocal(den[:].unsqueeze(3), v[:, :, :, DH:V1]))
                st.link(dve.tensor_tensor(fac[:], den[:], gate[:].unsqueeze(2).to_broadcast([P, E1, 2]), ALU.mult))
                dve.tensor_tensor(yh[:, ch], v[:, :, :, 0:DH], fac[:].unsqueeze(3).to_broadcast([P, E1, 2, DH]),
                                  ALU.mult).then_inc(s_["yh_ready"], 1)

            X_LINKS = 6 + RSQRT_LINKS

            def graph_sum(g, u):
                st = Steps(dve, s_["x_step"], X_LINKS * g)
                need("gV_done", g)
                v = W2[:, 0:HEADS * (DC + 2)].rearrange("p (h k) -> p h k", h=HEADS)
                st.link(dve.reciprocal(gsum[:].unsqueeze(2), v[:, :, DC:DC + 1]))
                dve.tensor_tensor(gout[:], v[:, :, 0:DC], gsum[:].unsqueeze(2).to_broadcast([P, HEADS, DC]),
                                  ALU.mult).then_inc(s_["x3_ready"], 1)
                need("x3_ready", g)
                st.link(dve.tensor_tensor(x3n[:], gout[:].rearrange("p h d -> p (h d)"), x2[u][:], ALU.add))
                moments(st, x3n[:])
                dve.tensor_scalar(rs_var[:, 0:1], mv[:, 1:2], EPS, None, ALU.add)
                st.link(dve.tensor_scalar(rs_var[:, 1:2], mv[:, 1:2], 1.0 + EPS, EPS * EPS, ALU.mult, ALU.add))
                rsqrt(dve, st, rs_var[:], seed_i[:], rs_tmp[:])
                free("T4_done", g - 1)
                for k in range(2):
                    r = slice(64 * k, 64 * k + 64)
                    ins = dve.tensor_scalar(xpad[r, :, r], x3n[r, :].rearrange("p (c d) -> p c d", c=C1),
                                            mv[r, 0:1], seed_i[r, 1:2].bitcast(F32), ALU.subtract, ALU.mult)
                ins.then_inc(s_["xpad_ready"], 1)
                dve.tensor_scalar(res_scale[:, 0:1], seed_i[:, 0:1].bitcast(F32), 1.0, None, ALU.add)
                st.link(dve.tensor_tensor(res_scale[:, 1:2], seed_i[:, 0:1].bitcast(F32), mv[:, 0:1], ALU.mult))
                dve.tensor_scalar(x3[u][:], x3n[:], res_scale[:, 0:1], res_scale[:, 1:2], ALU.mult, ALU.subtract).then_inc(s_["res_ready"], 1)
                assert st.n == X_LINKS

            def step(s, j, u):
                graph, head, out = runs(s, 0), runs(s, 1), runs(s, 2)
                g, f, r = s, s - 1, s - 2
                if runs(s, -2):
                    pick(s + 2, u)
                if head:
                    copy_x(f)
                if out:
                    copy_yT(r)
                if head:
                    copy_keys(f, 1)
                if out:
                    add_bias(r)
                if head:
                    copy_keys(f, 3)
                    st = route_shift(f)
                    max_parts(f, 0)
                    route_gate(f, st)
                if out:
                    finish(r, j - 1, u)
                if graph:
                    edges(g, j, u)
                    graph_scores(g)
                if head:
                    max_parts(f, 1)
                    copy_pT(f)
                if graph:
                    graph_shift(g)
                if head:
                    scale_heads(f, 0)
                    scale_heads(f, 1)
                    scale_heads(f, 2)
                if graph:
                    graph_sum(g, u)
                if runs(s, -1):
                    expert_sum(s + 1, j + u, 1 - u)
                if head:
                    scale_heads(f, 3)

            pick(0, 0)
            pick(1, 1)
            expert_sum(0, 0, 0)
            schedule(dve, step)


_INS = ["x", "adj", "L0_gnn_weight", "L0_gnn_bias", "L0_ffn_W1", "L0_ffn_b1", "L0_ffn_Wg", "L0_ffn_bg", "L0_ffn_Wd",
        "L0_ffn_bd", "L1_gnn_W", "L1_gnn_a", "L1_ffn_norm_w", "L1_ffn_router_w", "L1_ffn_router_b", "L1_ffn_qkv_w",
        "L1_ffn_proj_w", "L1_ffn_proj_b", "L1_ffn_out_w"]
_SHORT = ["x", "adj", "w0", "bias0", "w1", "b1", "wg", "bg", "wd", "bd", "gat_w", "gat_a", "norm_w", "router_w",
          "router_b", "qkv_w", "proj_w", "proj_b", "out_w"]


def program(nc, A):
    with ExitStack() as ctx:
        def sb(name, shape, dt=F32):
            return ctx.enter_context(nc.sbuf_tensor(name, shape, dt))

        def sem(name):
            return ctx.enter_context(nc.semaphore(name))

        c = {}
        with ExitStack() as layer0:
            c = setup_shared(nc, sb, sem, A)
            wd_offset = (nc.sbuf_base + 31) // 32 * 32
            wd_raw = layer0.enter_context(nc.sbuf_tensor("wd_raw", [P, KH, E0 * D], F32))
            c["wd_offset"] = wd_offset
            layer0a(nc, c, A, wd_raw)
            plan_slots(nc, c)
            layer0b(nc, c, A, wd_raw)
        w = setup_layer1(nc, c, A, sb)
        layer1(nc, c, w, A)


def kernel(**inputs):
    import numpy as _np
    import concourse.bacc as _bacc
    from concourse import mybir as _mybir
    from concourse.bass_utils import run_bass_kernel_spmd as _run

    nc = _bacc.Bacc("TRN2", target_bir_lowering=False, num_devices=1)
    arrays, A = {}, {}
    for name, short in zip(_INS, _SHORT):
        a = _np.ascontiguousarray(inputs[name])
        arrays[f"in_{name}"] = a
        A[short] = nc.dram_tensor(f"in_{name}", a.shape, _mybir.dt.from_np(a.dtype), kind="ExternalInput").ap()
    A["out"] = nc.dram_tensor("out_0", (2 * TILES, NODES, D), F32, kind="ExternalOutput").ap()
    for name, shape, dt in (("x1", (TOKENS, D), F32), ("xn", (TOKENS, D), F32), ("table", (E0 * TOKENS, 1), I32),
                            ("y", (SLOTS * P, D), F32)):
        A[name] = nc.dram_tensor("scratch_" + name, shape, dt, kind="Internal").ap()
    program(nc, A)
    r = _run(nc, [arrays], core_ids=[0])
    return r.results[0]["out_0"]
```

```python
import concourse.bass as bass
from concourse import mybir
from contextlib import ExitStack

F32 = mybir.dt.float32
F32R = mybir.dt.float32r
BF16 = mybir.dt.bfloat16
I32 = mybir.dt.int32
ALU = mybir.AluOpType
ACT = mybir.ActivationFunctionType
AX = mybir.AxisListType

P = 128
EPS = 1e-5
RSQRT_SEED = 1597463007.0


def wait(eng, sem, value):
    if isinstance(value, int) and value <= 0:
        return
    eng.wait_ge(sem, value)


class Steps:

    def __init__(self, eng, sem, base):
        self.eng, self.sem, self.base, self.n = eng, sem, base, 0

    def done(self, instruction):
        self.n += 1
        instruction.then_inc(self.sem, 1)

    def sync(self):
        self.eng.wait_ge(self.sem, self.base + self.n)

    def link(self, instruction):
        self.done(instruction)
        self.sync()


def mm3(pe, out, stat, mov, start=True, stop=True, **kw):
    pe.matmul(out, stat[0], mov[0], start=start, stop=False, **kw)
    pe.matmul(out, stat[0], mov[1], start=False, stop=False, **kw)
    return pe.matmul(out, stat[1], mov[0], start=False, stop=stop, **kw)


RSQRT_LINKS = 11


def rsqrt_seed(dve, steps, arg, y_i):
    steps.link(dve.tensor_scalar(y_i, arg.bitcast(I32), 1, None, ALU.arith_shift_right))
    dve.tensor_scalar(arg, arg, -0.5, None, ALU.mult)
    steps.link(dve.tensor_scalar(y_i, y_i, -1.0, RSQRT_SEED, ALU.mult, ALU.add))


def rsqrt_newton(dve, steps, arg, y_i, tmp):
    y = y_i.bitcast(F32)
    steps.link(dve.tensor_tensor(tmp, y, y, ALU.mult))
    steps.link(dve.tensor_tensor(tmp, tmp, arg, ALU.mult))
    steps.link(dve.scalar_tensor_tensor(y, tmp, 1.5, y, ALU.add, ALU.mult))


def rsqrt(dve, steps, arg, y_i, tmp):
    rsqrt_seed(dve, steps, arg, y_i)
    for _ in range(3):
        rsqrt_newton(dve, steps, arg, y_i, tmp)


def pool_turn(pool, pad, at):
    return pool.tensor_tensor(pad[:, at:at + 1], pad[:, 0:1], pad[:, 0:1], ALU.add)


TILES = 64
GROUP = 4
GROUPS = TILES // GROUP
TOKENS = TILES * P
D = 256
HID = 1024
KH = HID // P
E0 = 8
SLOTS = TILES + E0
TERNARY = 0.01


def place_shared(sb):
    c = {}
    c["ident"] = sb("ident", [P, P])
    c["ident_bf"] = sb("ident_bf", [P, P], BF16)
    c["before"] = sb("before", [P, P], BF16)
    c["ones_bf"] = sb("ones_bf", [P, P], BF16)
    c["iota_i"] = sb("iota_i", [P, P], I32)
    c["iota8"] = sb("iota8", [P, E0])
    c["token_f"] = sb("token_f", [P, GROUP])
    c["running"] = sb("running", [P, E0])
    c["shifted"] = sb("shifted", [P, TILES, E0])
    c["expert"] = sb("expert", [P, TILES])
    c["rank"] = sb("rank", [P, TILES])
    c["prob"] = sb("prob", [P, TILES])
    c["yrow"] = sb("yrow", [P, TILES], I32)
    c["slot_expert"] = sb("slot_expert", [P, SLOTS], I32)
    c["slot_row"] = sb("slot_row", [P, SLOTS], I32)
    c["bd_bc"] = sb("bd_bc", [P, E0 * D])
    c["b1"] = sb("b1", [P, KH])
    c["w1h"] = sb("w1h", [P, 2, HID], F32R)
    c["w1l"] = sb("w1l", [P, 2, HID], F32R)
    return c


def layer0a(nc, c, A, wd_raw):
    x_t = A["x"].rearrange("(t g) m d -> (g m) t d", g=2)
    adj_t = A["adj"].rearrange("(t g) n m -> g n t m", g=2)
    x1_t = A["x1"].rearrange("(t p) d -> p t d", p=P)
    xn_t = A["xn"].rearrange("(t p) d -> p t d", p=P)
    with ExitStack() as ctx:
        def sb(name, shape, dt=F32):
            return ctx.enter_context(nc.sbuf_tensor("a_" + name, shape, dt))

        def ps(name, shape, dt=F32):
            return ctx.enter_context(nc.psum_tensor("a_" + name, shape, dt))

        def sem(name):
            return ctx.enter_context(nc.semaphore("a_" + name))

        ident, w1h, w1l = c["ident"], c["w1h"], c["w1l"]
        w0 = sb("w0", [P, 2, D], F32R)
        wg_raw = sb("wg_raw", [P, KH, E0])
        wgh = sb("wgh", [P, KH, P], F32R)
        wgl = sb("wgl", [P, KH, P], F32R)
        bias0 = sb("bias0", [P, D])
        bg = sb("bg", [P, E0])
        zero_i = sb("zero_i", [P, 512], I32)

        dve_pad = sb("dve_pad", [P, 1])
        pool_pad = sb("pool_pad", [P, 3])
        xin = [sb(f"xin{u}", [P, GROUP, D]) for u in range(2)]
        adjd = [sb(f"adjd{u}", [P, GROUP, P]) for u in range(2)]
        stats = sb("stats", [P, 2, GROUP, 6])
        mv = sb("mv", [P, 2, GROUP, 2])
        factor = sb("factor", [P, 2, GROUP], I32)
        offset = sb("offset", [P, 2, GROUP])
        rs_var = sb("rs_var", [P, 2, GROUP])
        rs_tmp = sb("rs_tmp", [P, 2, GROUP])
        xln = sb("xln", [P, GROUP, D])
        xlnh = sb("xlnh", [P, GROUP, D], F32R)
        xlnl = sb("xlnl", [P, GROUP, D], F32R)
        adjTh = sb("adjTh", [P, GROUP, P], F32R)
        adjTl = sb("adjTl", [P, GROUP, P], F32R)
        zh = sb("zh", [P, 2, GROUP * P], F32R)
        zl = sb("zl", [P, 2, GROUP * P], F32R)
        x1 = [sb(f"x1{u}", [P, GROUP, D]) for u in range(2)]
        xn = [sb(f"xn{u}", [P, GROUP, D]) for u in range(2)]
        w1_raw = [b[:].rearrange("p t d -> p (t d)") for b in (x1[1], xn[0])]
        w0_raw, w0_neg = xn[1][:, 0:2, :], xn[1][:, 2:4, :]
        xTh = [sb(f"xTh{u}", [P, 2, GROUP * P], F32R) for u in range(2)]
        xTl = [sb(f"xTl{u}", [P, 2, GROUP * P], F32R) for u in range(2)]
        gel = [sb(f"gel{u}", [P, GROUP * P]) for u in range(2)]
        Hh = [sb(f"Hh{u}", [P, GROUP * P], F32R) for u in range(4)]
        Hl = [sb(f"Hl{u}", [P, GROUP * P], F32R) for u in range(4)]
        lgT = sb("lgT", [P, GROUP * P])
        logit = sb("logit", [P, GROUP, E0])
        top = sb("top", [P, GROUP])
        shifted = sb("shiftedg", [P, GROUP, E0])
        cand = sb("cand", [P, GROUP, E0])
        eidx = [sb(f"eidx{u}", [P, GROUP]) for u in range(2)]
        onehot = [sb(f"onehot{u}", [P, GROUP, E0], BF16) for u in range(2)]
        base = sb("base", [P, GROUP + 1, E0])
        counts = sb("counts", [P, GROUP, E0])
        within = sb("within", [P, GROUP, E0])
        rank = sb("rankg", [P, GROUP])
        place_f = sb("place_f", [P, GROUP])
        place = [sb(f"place{u}", [P, GROUP], I32) for u in range(2)]
        token = [sb(f"token{u}", [P, GROUP], I32) for u in range(2)]

        front_a = ps("front_a", [P, 2, 512])
        front_b = ps("front_b", [P, 2, 512])
        hid = [ps(f"hid{i}", [P, 512]) for i in range(3)]
        gate = ps("gate", [P, 512])
        lg = gate[:].rearrange("p (t e) -> p t e", t=GROUP)[:, :, 0:E0]
        prefix = gate[:, 64:64 + GROUP * E0].rearrange("p (t e) -> p t e", e=E0)
        total = gate[:, 128:128 + GROUP * E0].rearrange("p (t e) -> p t e", e=E0)

        weights_in = sem("weights_in")
        table_zeroed = sem("table_zeroed")
        wd_in = sem("wd_in")
        const_step = sem("const_step")
        adjd_zeroed = sem("adjd_zeroed")
        weights_split = sem("weights_split")
        x_in = [sem(f"x_in{u}") for u in range(2)]
        adj_in = [sem(f"adj_in{u}") for u in range(2)]
        x1_out = [sem(f"x1_out{u}") for u in range(2)]
        xn_out = [sem(f"xn_out{u}") for u in range(2)]
        rows_ready = sem("rows_ready")
        stats_ready = sem("stats_ready")
        conv_read = sem("conv_read")
        adj_turned = sem("adj_turned")
        adjh_done = sem("adjh_done")
        adj_split = sem("adj_split")
        moments_ready = sem("moments_ready")
        xln_full = sem("xln_full")
        xlnh_ready = sem("xlnh_ready")
        xln_ready = sem("xln_ready")
        z_done = sem("z_done")
        zh_done = sem("zh_done")
        z_split = sem("z_split")
        conv_done = sem("conv_done")
        x1_ready = sem("x1_ready")
        xn_ready = sem("xn_ready")
        xn_turned = sem("xn_turned")
        xTh_done = sem("xTh_done")
        xT_split = sem("xT_split")
        hid_done = sem("hid_done")
        gelu_done = sem("gelu_done")
        gelu_hi = sem("gelu_hi")
        h_split = [sem(f"h_split{i}") for i in range(2)]
        logits_part = sem("logits_part")
        lgT_ready = sem("lgT_ready")
        logits_turned = sem("logits_turned")
        onehot_ready = sem("onehot_ready")
        ranks_counted = sem("ranks_counted")
        ranks_read = sem("ranks_read")
        place_ready = sem("place_ready")
        scatter_turn = sem("scatter_turn")
        scattered = [sem(f"scattered{u}") for u in range(2)]
        first_step = sem("first_step")
        norm_step = sem("norm_step")
        gate_step = sem("gate_step")
        rank_step = sem("rank_step")

        block = ctx.enter_context(nc.Block())

        def schedule(eng, step):
            for s in range(5):
                step(s, s // 2, s % 2)
            with eng.Fori(2, 7) as j:
                for q in (1, 2):
                    step(2 * j + q, j, q)
            for s in range(15, GROUPS + 3):
                step(s, s // 2, s % 2)

        def has(s, lag):
            return not isinstance(s, int) or 0 <= s - lag < GROUPS

        def half(j, q, lag):
            return j + (q - lag) // 2

        @block.sync
        def _(sp):
            def weight(dst, src, slow=False):
                sp.dma_start(dst, src, allow_slow_non_contiguous=slow).then_inc(weights_in, 16)

            def load_x(n, u):
                sp.dma_start(xin[u][:], x_t[:, bass.ds(GROUP * n, GROUP), :]).then_inc(x_in[u], 16)

            def load_adj(n, u):
                for g in range(2):
                    r = slice(64 * g, 64 * g + 64)
                    sp.dma_start(adjd[u][r, :, r],
                                 adj_t[g, :, bass.ds(GROUP * n, GROUP), :]).then_inc(adj_in[u], 16)

            def load(n, u):
                wait(sp, x1_ready, n - 1)
                load_x(n, u)
                load_adj(n, u)

            def zero_table():
                sp.wait_ge(const_step, 12)
                sp.dma_start(A["table"].rearrange("(p n) a -> p (n a)", p=P), zero_i[:]).then_inc(table_zeroed, 16)

            def load_experts(first):
                wd_v = A["wd"].rearrange("e (k p) o -> p e k o", p=P)
                raw_v = wd_raw[:].rearrange("p k (e o) -> p e k o", e=E0)
                for e in (first, first + 1):
                    sp.dma_start(raw_v[:, e], wd_v[:, e]).then_inc(wd_in, 16)

            def step(s, j, q):
                u = q % 2
                if has(s, -1):
                    load(s + 1, 1 - u)
                if isinstance(s, int) and s == 0:
                    zero_table()
                if isinstance(s, int) and 1 <= s <= 4:
                    load_experts(2 * s - 2)
                if has(s, 1):
                    sp.wait_ge(xn_ready, s)
                    sp.dma_start(xn_t[:, bass.ds(GROUP * (s - 1), GROUP), :], xn[1 - u][:]).then_inc(xn_out[1 - u], 16)
                if has(s, 0):
                    sp.wait_ge(x1_ready, s + 1)
                    sp.dma_start(x1_t[:, bass.ds(GROUP * s, GROUP), :], x1[u][:]).then_inc(x1_out[u], 16)

            load_x(0, 0)
            for ic in range(2):
                weight(w1_raw[ic], A["w1"][ic * P:ic * P + P, :])
            weight(w0_raw, A["w0"].rearrange("(c p) o -> p c o", p=P))
            weight(wg_raw[:], A["wg"].rearrange("(k p) e -> p k e", p=P))
            sp.wait_ge(adjd_zeroed, 2)
            load_adj(0, 0)
            weight(bias0[:], A["bias0"].partition_broadcast(P))
            weight(c["b1"][:], A["b1"].rearrange("(k p) -> p k", p=P), True)
            weight(bg[:], A["bg"].partition_broadcast(P))
            weight(c["bd_bc"][:], A["bd"].rearrange("e o -> (e o)").partition_broadcast(P))
            schedule(sp, step)
            for u in range(2):
                sp.wait_ge(x1_out[u], 16 * (GROUPS // 2))
                sp.wait_ge(xn_out[u], 16 * (GROUPS // 2))
            sp.wait_ge(wd_in, 16 * E0)

        @block.gpsimd
        def _(pool):
            n = 0

            def link(ins, count=True):
                nonlocal n
                n += 1
                ins.then_inc(const_step, 1)
                pool.wait_ge(const_step, n)

            for u in range(2):
                pool.memset(adjd[u][:], 0.0).then_inc(adjd_zeroed, 1)
            link(pool.memset(ident[:], 0.0))
            link(pool.affine_select(out=ident[:], in_=ident[:], compare_op=ALU.not_equal, fill=1.0, base=0,
                                    pattern=[[-1, P]], channel_multiplier=1))
            link(pool.tensor_copy(c["ident_bf"][:], ident[:]))
            link(pool.memset(c["ones_bf"][:], 1.0))
            link(pool.affine_select(out=c["before"][:], in_=c["ones_bf"][:], compare_op=ALU.is_gt, fill=0.0,
                                    base=0, pattern=[[1, P]], channel_multiplier=-1))
            link(pool.iota(c["iota_i"][:], pattern=[[1, P]], base=0, channel_multiplier=0))
            link(pool.tensor_copy(c["iota8"][:], c["iota_i"][:, 0:E0]))
            link(pool.iota(c["iota_i"][:, 0:GROUP], pattern=[[P, GROUP]], base=0, channel_multiplier=1))
            link(pool.tensor_copy(c["token_f"][:], c["iota_i"][:, 0:GROUP]))
            link(pool.memset(c["running"][:], 0.0))
            link(pool.memset(pool_pad[:], 0.0))
            link(pool.memset(zero_i[:], 0))

            def split_h(n, k):
                pool.wait_ge(gelu_hi, KH * n + k + 1)
                wait(pool, logits_part, KH * n + k - 3)
                pool.tensor_tensor(Hl[k % 4][:], gel[1][:], Hh[k % 4][:].bitcast(F32), ALU.subtract).then_inc(h_split[1], 1)
                pool.wait_ge(h_split[1], KH // 2 * n + k // 2 + 1)

            def split_xln(n):
                pool.wait_ge(xlnh_ready, n + 1)
                wait(pool, z_done, 2 * n)
                pool.tensor_tensor(xlnl[:], xln[:], xlnh[:].bitcast(F32), ALU.subtract).then_inc(xln_ready, 1)
                pool.wait_ge(xln_ready, n + 1)

            def scatter(n, h, u):
                pool.wait_ge(place_ready, n + 1)
                if isinstance(n, int) and n == 0:
                    pool.wait_ge(table_zeroed, 16)
                pool_turn(pool, pool_pad, 1 + u).then_inc(scatter_turn, 1)
                for t in range(GROUP):
                    pool.indirect_dma_start(
                        A["table"], bass.IndirectOffsetOnAxis(ap=place[u][:, t:t + 1], axis=0),
                        token[u][:, t:t + 1], None).then_inc(scattered[u], 16)
                pool.wait_ge(scattered[u], 16 * GROUP * (h + 1))

            def step(s, j, q):
                if has(s, 2):
                    split_h(s - 2, 1)
                    split_h(s - 2, 3)
                if has(s, -1):
                    split_xln(s + 1)
                if has(s, 2):
                    split_h(s - 2, 5)
                    split_h(s - 2, 7)
                if has(s, 3):
                    scatter(s - 3, half(j, q, 3), (q - 3) % 2)

            split_xln(0)
            schedule(pool, step)
            for u in range(2):
                pool.wait_ge(scattered[u], 16 * GROUP * (GROUPS // 2))

        BANK = [0, 1, 2, 0, 1, 2, 0, 1]
        BANK_BEFORE = [-2, -1, -3, 0, 1, 2, 3, 4]

        @block.tensor
        def _(pe):
            pe.wait_ge(const_step, 12)

            def turn_adj(n, h, u):
                pe.wait_ge(adj_in[u], 32 * (h + 1))
                wait(pe, x1_ready, n)
                for t in range(GROUP):
                    ins = pe.transpose(front_a[:, 0, t * P:(t + 1) * P], adjd[u][:, t, :], ident[:])
                ins.then_inc(adj_turned, 1)

            def mix_nodes(n):
                pe.wait_ge(xln_ready, n + 1)
                pe.wait_ge(adj_split, n + 1)
                wait(pe, xT_split, 2 * n - 2)
                for ic in range(2):
                    for t in range(GROUP):
                        cols = slice(ic * P, ic * P + P)
                        ins = mm3(pe, front_b[:, ic, t * P:(t + 1) * P],
                                  (xlnh[:, t, cols], xlnl[:, t, cols]), (adjTh[:, t, :], adjTl[:, t, :]))
                    ins.then_inc(z_done, 1)

            def mix_channels(n):
                pe.wait_ge(z_split, 2 * n + 2)
                if isinstance(n, int) and n == 0:
                    pe.wait_ge(weights_split, 2)
                for t in range(GROUP):
                    out = front_a[:, t // 2, (t % 2) * D:(t % 2) * D + D]
                    for ic in range(2):
                        cols = slice(t * P, t * P + P)
                        pe.matmul(out, zh[:, ic, cols], w0[:, ic, :], start=(ic == 0), stop=False)
                        ins = pe.matmul(out, zl[:, ic, cols], w0[:, ic, :], start=False, stop=(ic == 1))
                    if t % 2:
                        ins.then_inc(conv_done, 1)

            def turn_xn(n, u):
                pe.wait_ge(xn_ready, n + 1)
                pe.wait_ge(z_split, min(2 * n + 4, 2 * GROUPS) if isinstance(n, int) else 2 * n + 4)
                for ic in range(2):
                    for t in range(GROUP):
                        ins = pe.transpose(front_b[:, ic, t * P:(t + 1) * P],
                                           xn[u][:, t, ic * P:ic * P + P], ident[:])
                    ins.then_inc(xn_turned, 1)

            def hidden(n, k, u):
                if k == 0:
                    pe.wait_ge(xT_split, 2 * n + 2)
                    if isinstance(n, int) and n == 0:
                        pe.wait_ge(weights_split, 6)
                wait(pe, gelu_hi, KH * n + BANK_BEFORE[k] + 1)
                out = hid[BANK[k]]
                cols = slice(k * P, k * P + P)
                for ic in range(2):
                    ins = mm3(pe, out[:], (w1h[:, ic, cols], w1l[:, ic, cols]), (xTh[u][:, ic, :], xTl[u][:, ic, :]),
                              start=(ic == 0), stop=(ic == 1))
                ins.then_inc(hid_done, 1)

            def logits(n, k):
                pe.wait_ge(h_split[k % 2], KH // 2 * n + k // 2 + 1)
                if k == 0:
                    wait(pe, ranks_read, n)
                mm3(pe, gate[:], (wgh[:, k, :], wgl[:, k, :]), (Hh[k % 4][:], Hl[k % 4][:]), start=(k == 0),
                    stop=(k == KH - 1)).then_inc(logits_part, 1)

            def turn_logits(n):
                pe.wait_ge(lgT_ready, n + 1)
                for t in range(GROUP):
                    ins = pe.transpose(gate[:, t * P:(t + 1) * P], lgT[:, t * P:(t + 1) * P], ident[:])
                ins.then_inc(logits_turned, 1)

            def count_ranks(n, u):
                pe.wait_ge(onehot_ready, n + 1)
                pe.matmul(prefix, c["before"][:], onehot[u][:], start=True, stop=True)
                pe.matmul(total, c["ones_bf"][:], onehot[u][:], start=True, stop=True).then_inc(ranks_counted, 1)

            def step(s, j, q):
                front, turn, back, ranks = has(s, 0), has(s, 1), has(s, 2), has(s, 3)
                u, v = q % 2, (q - 1) % 2
                if front:
                    turn_adj(s, half(j, q, 0), u)
                if ranks:
                    logits(s - 3, KH - 2)
                if back:
                    hidden(s - 2, 0, u)
                if ranks:
                    logits(s - 3, KH - 1)
                if back:
                    hidden(s - 2, 1, u)
                if ranks:
                    turn_logits(s - 3)
                if front:
                    mix_nodes(s)
                if back:
                    hidden(s - 2, 2, u)
                    hidden(s - 2, 3, u)
                if ranks:
                    count_ranks(s - 3, v)
                if front:
                    mix_channels(s)
                if back:
                    logits(s - 2, 0)
                    logits(s - 2, 1)
                    hidden(s - 2, 4, u)
                    logits(s - 2, 2)
                    hidden(s - 2, 5, u)
                    logits(s - 2, 3)
                if turn:
                    turn_xn(s - 1, v)
                if back:
                    hidden(s - 2, 6, u)
                    logits(s - 2, 4)
                    hidden(s - 2, 7, u)
                    logits(s - 2, 5)

            schedule(pe, step)

        @block.scalar
        def _(act):
            act.wait_ge(weights_in, 16 * 8)

            def gelu(n, k):
                act.wait_ge(hid_done, KH * n + k + 1)
                wait(act, h_split[k % 2], KH // 2 * n + k // 2)
                act.activation(gel[k % 2][:], hid[BANK[k]][:], ACT.Gelu, bias=c["b1"][:, k:k + 1]).then_inc(gelu_done, 1)
                wait(act, logits_part, KH * n + k - 3)
                act.activation(Hh[k % 4][:], hid[BANK[k]][:], ACT.Gelu, bias=c["b1"][:, k:k + 1]).then_inc(gelu_hi, 1)

            def norm_rows(n, u):
                act.wait_ge(moments_ready, n + 1)
                wait(act, xln_ready, n)
                for t in range(GROUP):
                    ins = act.activation(xln[:, t, :], xin[u][:, t, :], ACT.Identity, bias=offset[:, 0, t:t + 1],
                                         scale=factor[:, 0, t:t + 1].bitcast(F32))
                ins.then_inc(xln_full, 1)
                act.wait_ge(xln_full, n + 1)
                wait(act, z_done, 2 * n)
                act.activation(xlnh[:], xln[:], ACT.Copy).then_inc(xlnh_ready, 1)

            def norm_x1(n, h, u):
                wait(act, xn_out[u], 16 * h)
                wait(act, xn_turned, 2 * n - 2)
                act.wait_ge(moments_ready, n + 3)
                for t in range(GROUP):
                    ins = act.activation(xn[u][:, t, :], x1[u][:, t, :], ACT.Identity, bias=offset[:, 1, t:t + 1],
                                         scale=factor[:, 1, t:t + 1].bitcast(F32))
                ins.then_inc(xn_ready, 1)

            def copy_z(n, ic):
                act.wait_ge(z_done, 2 * n + ic + 1)
                wait(act, conv_done, 2 * n)
                act.activation(zh[:, ic, :], front_b[:, ic, :], ACT.Copy).then_inc(zh_done, 1)

            def copy_xT(n, ic, u):
                act.wait_ge(xn_turned, 2 * n + ic + 1)
                wait(act, hid_done, KH * (n - 1))
                act.activation(xTh[u][:, ic, :], front_b[:, ic, :], ACT.Copy).then_inc(xTh_done, 1)

            def copy_logits(n):
                act.wait_ge(logits_part, KH * (n + 1))
                wait(act, logits_turned, n)
                act.activation(lgT[:], gate[:], ACT.Copy).then_inc(lgT_ready, 1)

            def step(s, j, q):
                front, turn, back, ranks = has(s, 0), has(s, 1), has(s, 2), has(s, 3)
                u, v = q % 2, (q - 1) % 2
                if front:
                    act.wait_ge(adj_turned, s + 1)
                    wait(act, z_done, 2 * s)
                    act.activation(adjTh[:], front_a[:, 0, :].rearrange("p (t n) -> p t n", n=P), ACT.Copy).then_inc(adjh_done, 1)
                if back:
                    gelu(s - 2, 0)
                if ranks:
                    copy_logits(s - 3)
                if back:
                    gelu(s - 2, 1)
                if front:
                    copy_z(s, 0)
                    copy_z(s, 1)
                if back:
                    gelu(s - 2, 2)
                if turn:
                    norm_x1(s - 1, half(j, q, 1), v)
                if back:
                    gelu(s - 2, 3)
                if has(s, -1):
                    norm_rows(s + 1, v)
                if back:
                    gelu(s - 2, 4)
                    gelu(s - 2, 5)
                if turn:
                    copy_xT(s - 1, 0, v)
                    copy_xT(s - 1, 1, v)
                if back:
                    gelu(s - 2, 6)
                    gelu(s - 2, 7)

            norm_rows(0, 0)
            schedule(act, step)

        @block.vector
        def _(dve):
            def split_weights():
                for ic in range(2):
                    dve.tensor_copy(w1h[:, ic, :], w1_raw[ic])
                dve.memset(wgh[:].bitcast(F32), 0.0)
                dve.memset(wgl[:].bitcast(F32), 0.0).then_inc(weights_split, 1)
                dve.wait_ge(weights_split, 3)
                dve.tensor_copy(wgh[:, :, 0:E0], wg_raw[:]).then_inc(weights_split, 1)
                dve.wait_ge(weights_split, 4)
                for ic in range(2):
                    ins = dve.tensor_tensor(w1l[:, ic, :], w1_raw[ic], w1h[:, ic, :].bitcast(F32), ALU.subtract)
                ins.then_inc(weights_split, 1)
                dve.tensor_tensor(wgl[:, :, 0:E0], wg_raw[:], wgh[:, :, 0:E0].bitcast(F32),
                                  ALU.subtract).then_inc(weights_split, 1)

            def row_stats(n, h, u):
                dve.wait_ge(x_in[u], 16 * (h + 1))
                for t in range(GROUP):
                    ins = dve.bn_stats(stats[:, 0, t, :], xin[u][:, t, :])
                return ins

            def offsets(k):
                return dve.scalar_tensor_tensor(offset[:, k, :], mv[:, k, :, 0], -1.0, factor[:, k, :].bitcast(F32),
                                                ALU.mult, ALU.mult)

            def first_moments():
                st = Steps(dve, first_step, 0)
                st.link(row_stats(0, 0, 0))
                dve.memset(dve_pad[:], 0.0)
                for t in range(GROUP):
                    ins = dve.bn_aggr(mv[:, 0, t, :], stats[:, 0, t, :])
                st.link(ins)
                st.link(dve.tensor_scalar(rs_var[:, 0, :], mv[:, 0, :, 1], EPS, None, ALU.add))
                rsqrt(dve, st, rs_var[:, 0, :], factor[:, 0, :], rs_tmp[:, 0, :])
                offsets(0).then_inc(moments_ready, 1)

            def split_adj(n):
                dve.wait_ge(adjh_done, n + 1)
                dve.tensor_tensor(adjTl[:], front_a[:, 0, :].rearrange("p (t n) -> p t n", n=P),
                                  adjTh[:].bitcast(F32), ALU.subtract).then_inc(adj_split, 1)

            def split_z(n):
                for ic in range(2):
                    dve.wait_ge(zh_done, 2 * n + ic + 1)
                    dve.tensor_tensor(zl[:, ic, :], front_b[:, ic, :], zh[:, ic, :].bitcast(F32),
                                      ALU.subtract).then_inc(z_split, 1)

            def split_xT(n, ic, u):
                dve.wait_ge(xTh_done, 2 * n + ic + 1)
                dve.tensor_tensor(xTl[u][:, ic, :], front_b[:, ic, :], xTh[u][:, ic, :].bitcast(F32),
                                  ALU.subtract).then_inc(xT_split, 1)

            def split_h(n, k):
                dve.wait_ge(gelu_hi, KH * n + k + 1)
                wait(dve, logits_part, KH * n + k - 3)
                dve.tensor_tensor(Hl[k % 4][:], gel[0][:], Hh[k % 4][:].bitcast(F32), ALU.subtract).then_inc(h_split[0], 1)

            NORM_LINKS = 2 + RSQRT_LINKS

            def residual(n, h, u):
                wait(dve, x1_out[u], 16 * h)
                wait(dve, xn_ready, n - 1)
                for b in range(2):
                    dve.wait_ge(conv_done, 2 * n + b + 1)
                    ins = dve.scalar_tensor_tensor(
                        x1[u][:, 2 * b:2 * b + 2, :], front_a[:, b, :].rearrange("p (t o) -> p t o", o=D), TERNARY,
                        bias0[:].unsqueeze(1).to_broadcast([P, 2, D]), ALU.mult, ALU.add)
                ins.then_inc(conv_read, 1)
                dve.wait_ge(conv_read, n + 1)
                dve.scalar_tensor_tensor(x1[u][:], x1[u][:], 0.0, xin[u][:], ALU.max, ALU.add).then_inc(x1_ready, 1)
                dve.wait_ge(x1_ready, n + 1)
                for t in range(GROUP):
                    ins = dve.bn_stats(stats[:, 1, t, :], x1[u][:, t, :])
                ins.then_inc(stats_ready, 1)

            def moments(s, st, ks):
                dve.memset(dve_pad[:], 0.0)
                for k in ks:
                    for t in range(GROUP):
                        ins = dve.bn_aggr(mv[:, k, t, :], stats[:, k, t, :])
                st.link(ins)
                wait(dve, xn_ready, min(s - 1, GROUPS) if isinstance(s, int) else s - 1)
                wait(dve, xln_full, min(s + 1, GROUPS) if isinstance(s, int) else s + 1)
                cols = slice(ks[0], ks[-1] + 1)
                st.link(dve.tensor_scalar(rs_var[:, cols, :], mv[:, cols, :, 1], EPS, None, ALU.add))

            GATE_LINKS = 6

            def choose(n, u):
                st = Steps(dve, gate_step, GATE_LINKS * n)
                bc = lambda ap: ap.unsqueeze(2).to_broadcast([P, GROUP, E0])
                i8 = c["iota8"][:].unsqueeze(1).to_broadcast([P, GROUP, E0])
                dve.wait_ge(logits_turned, n + 1)
                st.link(dve.tensor_tensor(logit[:], lg, bg[:].unsqueeze(1).to_broadcast([P, GROUP, E0]), ALU.add))
                st.link(dve.tensor_reduce(top[:], logit[:], AX.X, ALU.max))
                st.link(dve.tensor_tensor(shifted[:], logit[:], bc(top[:]), ALU.subtract))
                dve.tensor_copy(c["shifted"][:, bass.ds(GROUP * n, GROUP), :], shifted[:])
                st.link(dve.tensor_scalar(cand[:], shifted[:], 0.0, float(E0), ALU.is_lt, ALU.mult))
                st.link(dve.tensor_tensor(cand[:], cand[:], i8, ALU.add))
                st.link(dve.tensor_reduce(eidx[u][:], cand[:], AX.X, ALU.min))
                dve.tensor_copy(c["expert"][:, bass.ds(GROUP * n, GROUP)], eidx[u][:])
                dve.tensor_tensor(onehot[u][:], i8, bc(eidx[u][:]), ALU.is_equal).then_inc(onehot_ready, 1)
                assert st.n == GATE_LINKS

            RANK_LINKS = 12

            def number(n, h, u):
                st = Steps(dve, rank_step, RANK_LINKS * n)
                dve.wait_ge(ranks_counted, n + 1)
                dve.tensor_copy(counts[:], total)
                st.link(dve.tensor_copy(within[:], prefix))
                st.link(dve.tensor_copy(base[:, 0, :], c["running"][:]))
                for t in range(GROUP):
                    st.link(dve.tensor_tensor(base[:, t + 1, :], base[:, t, :], counts[:, t, :], ALU.add))
                dve.tensor_copy(c["running"][:], base[:, GROUP, :]).then_inc(ranks_read, 1)
                st.link(dve.tensor_tensor(within[:], within[:], base[:, 0:GROUP, :], ALU.add))
                st.link(dve.tensor_tensor(within[:], within[:], onehot[u][:], ALU.mult))
                st.link(dve.tensor_reduce(rank[:], within[:], AX.X, ALU.add))
                dve.tensor_copy(c["rank"][:, bass.ds(GROUP * n, GROUP)], rank[:])
                st.link(dve.scalar_tensor_tensor(place_f[:], eidx[u][:], float(TOKENS), rank[:], ALU.mult, ALU.add))
                wait(dve, scattered[u], 16 * GROUP * h)
                wait(dve, scatter_turn, 2 * h)
                st.link(dve.tensor_copy(token[u][:], c["token_f"][:]))
                dve.tensor_copy(place[u][:], place_f[:]).then_inc(place_ready, 1)
                st.link(dve.tensor_scalar(c["token_f"][:], c["token_f"][:], float(GROUP * P), None, ALU.add))
                assert st.n == RANK_LINKS

            def step(s, j, q):
                front, turn, back, ranks = has(s, 0), has(s, 1), has(s, 2), has(s, 3)
                ahead = has(s, -1)
                u, v = q % 2, (q - 1) % 2
                if front:
                    split_adj(s)
                if ahead or turn:
                    st = Steps(dve, norm_step, NORM_LINKS * s)
                    ks = [0] * bool(ahead) + [1] * bool(turn)
                    cols = slice(ks[0], ks[-1] + 1)
                    newton = (dve, st, rs_var[:, cols, :], factor[:, cols, :], rs_tmp[:, cols, :])
                    if ahead:
                        row_stats(s + 1, half(j, q, -1), v).then_inc(rows_ready, 1)
                        dve.wait_ge(rows_ready, s + 1)
                    if turn:
                        dve.wait_ge(stats_ready, s)
                    moments(s, st, ks)
                    rsqrt_seed(*newton[:4])
                if back:
                    split_h(s - 2, 0)
                if ahead or turn:
                    for _ in range(3):
                        rsqrt_newton(*newton)
                    for k in ks:
                        ins = offsets(k)
                    ins.then_inc(moments_ready, 1)
                    assert st.n == NORM_LINKS
                if ranks:
                    choose(s - 3, v)
                if front:
                    split_z(s)
                if ranks:
                    number(s - 3, half(j, q, 3), v)
                if back:
                    split_h(s - 2, 2)
                if front:
                    residual(s, half(j, q, 0), u)
                if isinstance(s, int) and s == 0:
                    split_weights()
                if back:
                    split_h(s - 2, 4)
                if turn:
                    split_xT(s - 1, 0, v)
                    split_xT(s - 1, 1, v)
                if back:
                    split_h(s - 2, 6)

            dve.wait_ge(const_step, 12)
            first_moments()
            dve.wait_ge(weights_in, 16 * 8)
            dve.tensor_scalar(w0_neg, w0_raw, -TERNARY, None, ALU.is_lt).then_inc(weights_split, 1)
            dve.wait_ge(weights_split, 1)
            dve.scalar_tensor_tensor(w0[:], w0_raw, TERNARY, w0_neg, ALU.is_gt, ALU.subtract).then_inc(weights_split, 1)
            schedule(dve, step)


def plan_slots(nc, c):
    with ExitStack() as ctx:
        def sb(name, shape, dt=F32):
            return ctx.enter_context(nc.sbuf_tensor("p_" + name, shape, dt))

        tiles_i = sb("tiles_i", [P, E0], I32)
        tiles = sb("tiles", [P, E0])
        ends = sb("ends", [P, E0 + 1])
        slot_f = sb("slot_f", [P, SLOTS])
        slot_i = sb("slot_i", [P, SLOTS], I32)
        past = sb("past", [P, SLOTS, E0])
        part = sb("part", [P, SLOTS, E0])
        expert_f = sb("expert_f", [P, SLOTS])
        before = sb("before_slot", [P, SLOTS])
        row_f = sb("row_f", [P, SLOTS])
        pick = sb("pick", [P, TILES, E0])
        first = sb("first", [P, TILES])
        yrow_f = sb("yrow_f", [P, TILES])
        expd = sb("expd", [P, TILES, E0])
        sums = sb("sums", [P, TILES])
        slots_counted = ctx.enter_context(nc.semaphore("slots_counted"))
        exp_done = ctx.enter_context(nc.semaphore("exp_done"))
        plan_step = ctx.enter_context(nc.semaphore("plan_step"))
        block = ctx.enter_context(nc.Block())

        @block.gpsimd
        def _(pool):
            pool.iota(slot_i[:], pattern=[[1, SLOTS]], base=0, channel_multiplier=0).then_inc(slots_counted, 1)

        @block.scalar
        def _(act):
            act.activation(expd[:], c["shifted"][:], ACT.Exp).then_inc(exp_done, 1)

        @block.vector
        def _(dve):
            st = Steps(dve, plan_step, 0)
            st.link(dve.tensor_scalar(tiles[:], c["running"][:], float(P - 1), None, ALU.add))
            st.link(dve.tensor_copy(tiles_i[:], tiles[:]))
            st.link(dve.tensor_scalar(tiles_i[:], tiles_i[:], 7, None, ALU.arith_shift_right))
            st.link(dve.tensor_copy(tiles[:], tiles_i[:]))
            st.link(dve.memset(ends[:, 0:1], 0.0))
            for e in range(E0):
                st.link(dve.tensor_tensor(ends[:, e + 1:e + 2], ends[:, e:e + 1], tiles[:, e:e + 1], ALU.add))
            dve.wait_ge(slots_counted, 1)
            st.link(dve.tensor_copy(slot_f[:], slot_i[:]))
            over_slots = lambda ap: ap.unsqueeze(1).to_broadcast([P, SLOTS, E0])
            over_tiles = lambda ap: ap.unsqueeze(1).to_broadcast([P, TILES, E0])
            st.link(dve.tensor_tensor(past[:], slot_f[:].unsqueeze(2).to_broadcast([P, SLOTS, E0]),
                                      over_slots(ends[:, 1:]), ALU.is_ge))
            st.link(dve.tensor_reduce(expert_f[:], past[:], AX.X, ALU.add))
            st.link(dve.tensor_scalar(expert_f[:], expert_f[:], float(E0 - 1), None, ALU.min))
            st.link(dve.tensor_tensor(part[:], past[:], over_slots(tiles[:]), ALU.mult))
            st.link(dve.tensor_reduce(before[:], part[:], AX.X, ALU.add))
            st.link(dve.tensor_tensor(row_f[:], slot_f[:], before[:], ALU.subtract))
            st.link(dve.tensor_scalar(row_f[:], row_f[:], float(P), None, ALU.mult))
            st.link(dve.scalar_tensor_tensor(row_f[:], expert_f[:], float(TOKENS), row_f[:], ALU.mult, ALU.add))
            st.link(dve.tensor_copy(c["slot_row"][:], row_f[:]))
            st.link(dve.tensor_scalar(expert_f[:], expert_f[:], float(D), None, ALU.mult))
            st.link(dve.tensor_copy(c["slot_expert"][:], expert_f[:]))
            i8 = c["iota8"][:].unsqueeze(1).to_broadcast([P, TILES, E0])
            st.link(dve.tensor_tensor(pick[:], c["expert"][:].unsqueeze(2).to_broadcast([P, TILES, E0]), i8,
                                      ALU.is_equal))
            st.link(dve.tensor_tensor(pick[:], pick[:], over_tiles(ends[:, 0:E0]), ALU.mult))
            st.link(dve.tensor_reduce(first[:], pick[:], AX.X, ALU.add))
            st.link(dve.scalar_tensor_tensor(yrow_f[:], first[:], float(P), c["rank"][:], ALU.mult, ALU.add))
            st.link(dve.tensor_copy(c["yrow"][:], yrow_f[:]))
            dve.wait_ge(exp_done, 1)
            st.link(dve.tensor_reduce(sums[:], expd[:], AX.X, ALU.add))
            st.link(dve.reciprocal(c["prob"][:], sums[:]))


def layer0b(nc, c, A, wd_raw, raw1):
    SG = SLOTS // GROUP
    y_t = A["y"].rearrange("(t p) d -> p t d", p=P)
    with ExitStack() as ctx:
        def sb(name, shape, dt=F32):
            return ctx.enter_context(nc.sbuf_tensor("b_" + name, shape, dt))

        def ps(name, shape, dt=F32):
            return ctx.enter_context(nc.psum_tensor("b_" + name, shape, dt))

        def sem(name):
            return ctx.enter_context(nc.semaphore("b_" + name))

        ident, w1h, w1l = c["ident"], c["w1h"], c["w1l"]
        wdl = nc.alloc_sbuf_tensor_at("b_wdl", [P, KH, E0 * D], F32R, offset=c["wd_offset"])
        wdh = sb("wdh", [P, KH, E0 * D], F32R)
        slot_token = [sb(f"slot_token{u}", [P, GROUP], I32) for u in range(2)]
        pool_pad = sb("pool_pad", [P, 3])
        xg = sb("xg", [P, GROUP, D])
        xTh = sb("xTh", [P, 2, GROUP * P], F32R)
        xTl = sb("xTl", [P, 2, GROUP * P], F32R)
        gel = [sb(f"gel{u}", [P, GROUP * P]) for u in range(2)]
        Hh = [sb(f"Hh{u}", [P, GROUP * P], F32R) for u in range(3)]
        Hl = [sb(f"Hl{u}", [P, GROUP * P], F32R) for u in range(3)]
        yout = sb("yout", [P, GROUP, D])
        turned = [ps(f"turned{ic}", [P, 512]) for ic in range(2)]
        hid = [ps(f"hid{i}", [P, 512]) for i in range(3)]
        ybank = [ps(f"ybank{i}", [P, 512]) for i in range(2)]
        yps = [ybank[t // 2][:, (t % 2) * D:(t % 2) * D + D] for t in range(GROUP)]

        pad_set = sem("pad_set")
        wd_hi = sem("wd_hi")
        wd_split = sem("wd_split")
        tokens_in = [sem(f"tokens_in{u}") for u in range(2)]
        gather_turn = sem("gather_turn")
        gathered = [sem(f"gathered{u}") for u in range(2)]
        x_turned = sem("x_turned")
        xTh_done = sem("xTh_done")
        xT_split = sem("xT_split")
        hid_done = sem("hid_done")
        gelu_done = sem("gelu_done")
        gelu_hi = sem("gelu_hi")
        h_split = sem("h_split")
        chunk_used = sem("chunk_used")
        y_done = sem("y_done")
        y_ready = sem("y_ready")
        y_out = sem("y_out")
        assert nc.sbuf_base <= raw1.offset, (nc.sbuf_base, raw1.offset)
        block = ctx.enter_context(nc.Block())

        def schedule(eng, step):
            for s in range(4):
                step(s, s // 2, s % 2)
            with eng.Fori(2, SG // 2) as j:
                step(2 * j, j, 0)
                step(2 * j + 1, j, 1)
            step(SG, SG // 2, 0)

        def has(s, first, last):
            return not isinstance(s, int) or first <= s <= last

        @block.sync
        def _(sp):
            def tokens(n, u):
                wait(sp, x_turned, 2 * (n - 1))
                for t in range(GROUP):
                    row = sp.value_load(c["slot_row"][0:1, bass.ds(GROUP * n + t, 1)], min_val=0,
                                        max_val=E0 * TOKENS - P)
                    sp.dma_start(slot_token[u][:, t:t + 1], A["table"][bass.ds(row, P), :]).then_inc(tokens_in[u], 16)

            def step(s, j, u):
                if has(s, 0, SG - 2):
                    tokens(s + 1, 1 - u)
                if has(s, 1, SG):
                    sp.wait_ge(y_ready, GROUP * s)
                    sp.dma_start(y_t[:, bass.ds(GROUP * s - GROUP, GROUP), :], yout[:]).then_inc(y_out, 16)

            tokens(0, 0)
            for s in range(4):
                step(s, s // 2, s % 2)
            raw1.load(sp, A)
            with sp.Fori(2, SG // 2 - 1) as j:
                step(2 * j, j, 0)
                step(2 * j + 1, j, 1)
            for s in range(SG - 2, SG + 1):
                step(s, s // 2, s % 2)
            sp.wait_ge(y_out, 16 * SG)

        @block.gpsimd
        def _(pool):
            pool.memset(pool_pad[:], 0.0).then_inc(pad_set, 1)
            pool.wait_ge(pad_set, 1)

            def step(s, j, u):
                if has(s, 0, SG - 1):
                    wait(pool, x_turned, 2 * s)
                    wait(pool, tokens_in[u], 16 * GROUP * (j + 1))
                    wait(pool, gather_turn, s)
                    pool_turn(pool, pool_pad, 1).then_inc(gather_turn, 1)
                    for t in range(GROUP):
                        pool.indirect_dma_start(
                            xg[:, t, :], None, A["xn"],
                            bass.IndirectOffsetOnAxis(ap=slot_token[u][:, t:t + 1], axis=0)).then_inc(gathered[u], 16)

            schedule(pool, step)

        BANK = [0, 1, 2, 0, 1, 2, 0, 1]
        BANK_BEFORE = [-2, -1, -3, 0, 1, 2, 3, 4]

        def used(eng, n, k):
            before = BANK_BEFORE[k]
            if before == -1:
                wait(eng, y_done, GROUP * n)
            elif before < 0:
                wait(eng, chunk_used, (KH - 1) * n + before + 2)
            else:
                wait(eng, chunk_used, (KH - 1) * n + before + 1)

        @block.tensor
        def _(pe):
            def turn_x(n, h, u):
                pe.wait_ge(gathered[u], 16 * GROUP * (h + 1))
                for ic in range(2):
                    wait(pe, xT_split, 2 * n - 1 + ic)
                    for t in range(GROUP):
                        ins = pe.transpose(turned[ic][:, t * P:(t + 1) * P], xg[:, t, ic * P:ic * P + P], ident[:])
                    ins.then_inc(x_turned, 1)

            def hidden(n, k, u):
                if k == 0:
                    pe.wait_ge(xT_split, 2 * n + 2)
                wait(pe, gelu_hi, KH * n + BANK_BEFORE[k] + 1)
                cols = slice(k * P, k * P + P)
                for ic in range(2):
                    ins = mm3(pe, hid[BANK[k]][:], (w1h[:, ic, cols], w1l[:, ic, cols]),
                              (xTh[:, ic, :], xTl[:, ic, :]), start=(ic == 0), stop=(ic == 1))
                ins.then_inc(hid_done, 1)

            def experts(n, k, at):
                pe.wait_ge(h_split, KH * n + k + 1)
                if k == 0:
                    wait(pe, y_ready, GROUP * n)
                if isinstance(n, int) and n == 0:
                    pe.wait_ge(wd_split, k + 1)
                b = BANK[k]
                for t in range(GROUP):
                    cols = slice(t * P, t * P + P)
                    w = bass.ds(at[t], D)
                    ins = mm3(pe, yps[t], (Hh[b][:, cols], Hl[b][:, cols]), (wdh[:, k, w], wdl[:, k, w]),
                              start=(k == 0 and t % 2 == 0), stop=(k == KH - 1), skip_group_check=True)
                    if k == KH - 1:
                        ins.then_inc(y_done, 1)
                    elif t == GROUP - 1:
                        ins.then_inc(chunk_used, 1)

            def step(s, j, u):
                front, back = has(s, 0, SG - 1), has(s, 1, SG)
                n, v = s - 1, 1 - u
                if back:
                    hidden(n, 0, v)
                    hidden(n, 1, v)
                    at = [pe.value_load(c["slot_expert"][0:1, bass.ds(GROUP * n + t, 1)], min_val=0,
                                        max_val=(E0 - 1) * D) for t in range(GROUP)]
                    for k in range(2, KH):
                        hidden(n, k, v)
                        experts(n, k - 2, at)
                    if front:
                        turn_x(s, j, u)
                    experts(n, KH - 2, at)
                    experts(n, KH - 1, at)
                elif front:
                    turn_x(s, j, u)

            schedule(pe, step)

        @block.scalar
        def _(act):
            def round_weights(k):
                act.activation(wdh[:, k], wd_raw[:, k], ACT.Copy).then_inc(wd_hi, 1)

            def gelu(n, k):
                act.wait_ge(hid_done, KH * n + k + 1)
                wait(act, h_split, KH * n + k - 1)
                act.activation(gel[k % 2][:], hid[BANK[k]][:], ACT.Gelu, bias=c["b1"][:, k:k + 1]).then_inc(gelu_done, 1)
                used(act, n, k)
                act.activation(Hh[BANK[k]][:], hid[BANK[k]][:], ACT.Gelu, bias=c["b1"][:, k:k + 1]).then_inc(gelu_hi, 1)

            def step(s, j, u):
                front, back = has(s, 0, SG - 1), has(s, 1, SG)
                if back:
                    for k in range(KH):
                        if isinstance(s, int) and s == 1 and 2 <= k + 1 < KH:
                            round_weights(k + 1)
                        gelu(s - 1, k)
                if front:
                    for ic in range(2):
                        act.wait_ge(x_turned, 2 * s + ic + 1)
                        if ic == 0:
                            wait(act, hid_done, KH * s)
                        act.activation(xTh[:, ic, :], turned[ic][:], ACT.Copy).then_inc(xTh_done, 1)

            round_weights(0)
            round_weights(1)
            schedule(act, step)

        @block.vector
        def _(dve):
            def split_weights(k):
                dve.wait_ge(wd_hi, k + 1)
                dve.tensor_tensor(wdl[:, k], wd_raw[:, k], wdh[:, k].bitcast(F32), ALU.subtract).then_inc(wd_split, 1)

            def step(s, j, u):
                front, back = has(s, 0, SG - 1), has(s, 1, SG)
                n = s - 1
                if back:
                    at = [dve.value_load(c["slot_expert"][0:1, bass.ds(GROUP * n + t, 1)], min_val=0,
                                         max_val=(E0 - 1) * D) for t in range(GROUP)]
                    for k in range(KH):
                        if isinstance(s, int) and s == 1 and 2 <= k + 1 < KH:
                            split_weights(k + 1)
                        dve.wait_ge(gelu_hi, KH * n + k + 1)
                        used(dve, n, k)
                        dve.tensor_tensor(Hl[BANK[k]][:], gel[k % 2][:], Hh[BANK[k]][:].bitcast(F32),
                                          ALU.subtract).then_inc(h_split, 1)
                if front:
                    for ic in range(2):
                        dve.wait_ge(xTh_done, 2 * s + ic + 1)
                        dve.tensor_tensor(xTl[:, ic, :], turned[ic][:], xTh[:, ic, :].bitcast(F32),
                                          ALU.subtract).then_inc(xT_split, 1)
                if back:
                    wait(dve, y_out, 16 * n)
                    for t in range(GROUP):
                        dve.wait_ge(y_done, GROUP * n + 2 * (t // 2) + 2)
                        dve.tensor_tensor(yout[:, t, :], yps[t], c["bd_bc"][:, bass.ds(at[t], D)],
                                          ALU.add).then_inc(y_ready, 1)

            split_weights(0)
            split_weights(1)
            schedule(dve, step)


HEADS = 4
NODES = 64
C1 = 4
E1 = 4
DC = 64
DH = 32
EH = 8
V1 = DH + 1
NEG = -9e15
SLOPE = 0.2
SCALE = 1.0 / (DH ** 0.5)


SBUF_BYTES = 229344


class RawWeights:

    LOADS = 3 + 2 * (1 + C1 + 4 + 2) + 4

    def __init__(self, nc, loaded):
        self.nc, self.loaded = nc, loaded
        self.offset = self.end = SBUF_BYTES - 18624
        self.gat_w = self.place("gat_w", [P, 2, D + 2 * HEADS])
        self.norm_w = self.place("norm_w", [P, C1])
        self.router_w = self.place("router_w", [P, C1, E1])
        self.router_b = self.place("router_b", [P, E1])
        self.proj_b = self.place("proj_b", [P, E1, DC])
        self.a_bc = self.place("a_bc", [P, 2, HEADS, DC])
        self.qk = self.place("qk", [DH, 2, E1, 2, 2, DC])
        self.val = self.place("val", [DC, E1, 2, DC])
        self.proj = self.place("proj", [DC, E1, DC])
        self.outw = self.place("outw", [P, 2, D])
        assert self.end == SBUF_BYTES

    def place(self, name, shape):
        size = 4
        for n in shape[1:]:
            size *= n
        t = self.nc.alloc_sbuf_tensor_at("r_" + name, shape, F32, offset=self.end)
        self.end += (size + 31) // 32 * 32
        return t

    def load(self, sp, A):
        q4 = A["qkv_w"].rearrange("e (q h r) d -> q h r e d", q=3, h=2)
        n = 0

        def load(dst, src, slow=False):
            nonlocal n
            sp.dma_start(dst, src, allow_slow_non_contiguous=slow).then_inc(self.loaded, 16)
            n += 1

        load(self.gat_w[:, :, 0:D], A["gat_w"].rearrange("(c p) o -> p c o", p=P))
        for k in range(2):
            load(self.a_bc[:, k], A["gat_a"].rearrange("h (k d) -> k h d", k=2)[k].partition_broadcast(P))
        for copy in range(2):
            r = slice(64 * copy, 64 * copy + 64)
            load(self.norm_w[r, :], A["norm_w"].rearrange("(c d) -> d c", c=C1), True)
            for ch in range(C1):
                load(self.router_w[r, ch, :], A["router_w"].rearrange("e (c d) -> c d e", c=C1)[ch], True)
            for q in range(2):
                for h in range(2):
                    load(self.qk[:, q, :, h, copy, :], q4[q, h])
            for h in range(2):
                load(self.val[DH * h:DH * h + DH, :, copy, :], q4[2, h])
        load(self.router_b[:], A["router_b"].partition_broadcast(P))
        load(self.proj[:], A["proj_w"].rearrange("e o d -> o e d"))
        load(self.proj_b[:], A["proj_b"].partition_broadcast(P))
        load(self.outw[:], A["out_w"].rearrange("(b p) o -> p b o", p=P))
        assert n == self.LOADS


def place_layer1(raw1, sb, sem):
    w = {
        "gat_w": raw1.gat_w, "norm_w": raw1.norm_w, "router_w": raw1.router_w, "router_b": raw1.router_b,
        "proj_b": raw1.proj_b,
        "att_h": sb("att_h", [P, EH, P], F32R),
        "att_l": sb("att_l", [P, EH, P], F32R),
        "val_w": sb("val_w", [P, E1 * DC]),
        "proj_w": sb("proj_w", [P, 2, DC]),
        "out_w": sb("out_w", [P, 2, D]),
        "same_graph": sb("same_graph", [P, P]),
        "node": sb("node", [P, NODES]),
        "spread": sb("spread", [48, 2, EH, NODES], BF16),
    }
    setup = {
        "gat_a": sb("s_gat_a", [P, 2, 2, D]),
        "att": sb("s_att", [P, EH, DC]),
        "loaded": raw1.loaded, "LOADS": raw1.LOADS,
        "made": sem("s_made"), "turned": sem("s_turned"), "step": sem("s_step"), "weights": sem("s_weights"),
    }
    return w, setup


MADE = 8


def make_constants(pool, c, w, setup):
    n = 0

    def link(ins):
        nonlocal n
        n += 1
        ins.then_inc(setup["made"], 1)
        pool.wait_ge(setup["made"], n)

    link(pool.memset(w["same_graph"][:], 0.0))
    for g in range(2):
        r = slice(64 * g, 64 * g + 64)
        link(pool.memset(w["same_graph"][r, r], 1.0))
    link(pool.tensor_tensor(w["node"][:], c["ident"][:, 0:64], c["ident"][:, 64:128], ALU.add))
    link(pool.memset(w["spread"][:], 0.0))
    for part in range(3):
        v = w["spread"][:].rearrange("r c e s -> r (c e) s")
        link(pool.affine_select(out=v, in_=v, compare_op=ALU.not_equal, fill=1.0, base=-16 * part,
                                pattern=[[-1, 16], [0, NODES]], channel_multiplier=1))
    assert n == MADE


def turn_weights(pe, c, raw1, banks, setup):
    qk, val, proj, outw = raw1.qk, raw1.val, raw1.proj, raw1.outw
    pe.wait_ge(setup["loaded"], 16 * setup["LOADS"])
    for e in range(E1):
        for h in range(2):
            pe.matmul(banks[0][:, (2 * e + h) * DC:(2 * e + h + 1) * DC],
                      qk[:, 1, e, h, :, :].rearrange("r a d -> r (a d)"), qk[:, 0, e, h, 0, :],
                      start=True, stop=True)
    for e in range(E1):
        pe.transpose(banks[1][:, e * DC:(e + 1) * DC], val[:, e, :, :].rearrange("r a d -> r (a d)"),
                     c["ident"][0:DC, 0:DC])
    for b in range(2):
        pe.transpose(banks[2][:, b * DC:(b + 1) * DC],
                     proj[:, 2 * b:2 * b + 2, :].rearrange("o e d -> o (e d)"), c["ident"][0:DC, 0:DC])
    for b in range(2):
        for k in range(2):
            ins = pe.transpose(banks[3 + k][:, b * P:(b + 1) * P], outw[:, b, k * P:(k + 1) * P], c["ident"][:])
    ins.then_inc(setup["turned"], 1)


def finish_weights(dve, w, raw1, banks, setup):
    gat_a, att, a_bc = setup["gat_a"], setup["att"], raw1.a_bc
    st = Steps(dve, setup["step"], 0)
    dve.wait_ge(setup["loaded"], 16 * setup["LOADS"])
    for k in range(2):
        for ic in range(2):
            ins = dve.tensor_tensor(gat_a[:, k, ic, :], w["gat_w"][:, ic, 0:D],
                                    a_bc[:, k].rearrange("p h d -> p (h d)"), ALU.mult)
    st.link(ins)
    for k in range(2):
        for ic in range(2):
            dve.tensor_reduce(w["gat_w"][:, ic, D + HEADS * k:D + HEADS * k + HEADS],
                              gat_a[:, k, ic, :].rearrange("p (h d) -> p h d", h=HEADS), AX.X, ALU.add)
    dve.memset(w["att_h"][:].bitcast(F32), 0.0)
    st.link(dve.memset(w["att_l"][:].bitcast(F32), 0.0))
    dve.wait_ge(setup["turned"], 1)
    st.link(dve.tensor_scalar(att[:], banks[0].rearrange("p (e d) -> p e d", e=EH), SCALE, None, ALU.mult))
    for g in range(2):
        r = slice(64 * g, 64 * g + 64)
        ins = dve.tensor_copy(w["att_h"][r, :, r], att[r])
    st.link(ins)
    for g in range(2):
        r = slice(64 * g, 64 * g + 64)
        dve.tensor_tensor(w["att_l"][r, :, r], att[r], w["att_h"][r, :, r].bitcast(F32), ALU.subtract)
    dve.tensor_copy(w["val_w"][:], banks[1][:, 0:E1 * DC])
    dve.tensor_copy(w["proj_w"][:], banks[2][:, 0:2 * DC].rearrange("p (b o) -> p b o", b=2))
    for k in range(2):
        ins = dve.tensor_copy(w["out_w"][:, k, :], banks[3 + k][:, 0:D])
    ins.then_inc(setup["weights"], 1)


def layer1(nc, c, w, setup, raw1, A):
    x1_t = A["x1"].rearrange("(t p) d -> p t d", p=P)
    out_t = A["out"].rearrange("(t g) m d -> (g m) t d", g=2)
    adj_t = A["adj"].rearrange("(t g) n m -> (g n) t m", g=2)
    with ExitStack() as ctx:
        def sb(name, shape, dt=F32):
            return ctx.enter_context(nc.sbuf_tensor("l_" + name, shape, dt))

        def ps(name, shape, dt=F32):
            return ctx.enter_context(nc.psum_tensor("l_" + name, shape, dt))

        def sem(name):
            return ctx.enter_context(nc.semaphore("l_" + name))

        ident, ident_bf = c["ident"], c["ident_bf"]
        yrow = [sb(f"yrow{u}", [P, 1], I32) for u in range(2)]
        prob = [sb(f"prob{u}", [P, 1]) for u in range(2)]
        pool_pad = sb("pool_pad", [P, 3])
        dve_pad = sb("dve_pad", [P, 1])
        x1 = [sb(f"x1{u}", [P, D]) for u in range(2)]
        yin = [sb(f"yin{u}", [P, D]) for u in range(2)]
        adj = [sb(f"adj{u}", [P, NODES]) for u in range(2)]
        x2 = [sb(f"x2{i}", [P, D]) for i in range(4)]
        stats = sb("stats", [P, 2, 6])
        mv = sb("mv", [P, 2, 2])
        factor = sb("factor", [P, 3], I32)
        rs_tmp = sb("rs_tmp", [P, 3])
        rs_var = sb("rs_var", [P, 3])
        res_scale = sb("res_scale", [P, 2])
        x3n = sb("x3n", [P, D])
        xa = [sb(f"xa{u}", [P, D]) for u in range(2)]
        xaT = sb("xaT", [P, 2, P])
        hx = sb("hx", [P, HEADS, DC + 2])
        e8 = sb("e8", [P, 2, HEADS])
        ediag = sb("ediag", [P, HEADS, NODES])
        edge = sb("edge", [P, NODES])
        noedge = sb("noedge", [P, NODES])
        score = sb("score", [P, HEADS, NODES])
        leaky = sb("leaky", [P, HEADS, NODES])
        masked = sb("masked", [P, HEADS, NODES])
        masked2 = sb("masked2", [P, HEADS, NODES])
        gmax = sb("gmax", [P, HEADS])
        gshift = sb("gshift", [P, HEADS, NODES])
        gprob = sb("gprob", [P, HEADS, P])
        gprobT = sb("gprobT", [P, HEADS, P])
        gsum = sb("gsum", [P, HEADS])
        gout = sb("gout", [P, HEADS, DC])
        x3 = [sb(f"x3{i}", [P, D]) for i in range(4)]
        xpad = sb("xpad", [P, C1, P])
        xbd = [sb(f"xbd{u}", [P, C1, P]) for u in range(2)]
        xmh = sb("xmh", [P, C1, NODES], F32R)
        xml = sb("xml", [P, C1, NODES], F32R)
        wk = sb("wk", [P, C1, EH, NODES])
        vd = [sb(f"vd{u}", [P, 2, C1, E1, 2 * V1]) for u in range(2)]
        rlog = sb("rlog", [P, E1])
        rmax = sb("rmax", [P, 1])
        rexp = sb("rexp", [P, E1])
        rsum = sb("rsum", [P, 1])
        gate = [sb(f"gate{u}", [P, E1]) for u in range(2)]
        nmax = sb("nmax", [P, 2 * EH])
        nrest = sb("nrest", [P, 2 * EH])
        nparts = sb("nparts", [P, 8, 2 * EH], BF16)
        nmaxT = sb("nmaxT", [48, P], BF16)
        pex = [sb(f"pex{i}", [P, E1, P]) for i in range(2)]
        pT = [sb(f"pT{i}", [P, E1, P]) for i in range(2)]
        den = sb("den", [P, 2, EH])
        fac = sb("fac", [P, 2, E1, 2])
        yh = sb("yh", [P, C1, E1, 2, DH])
        bias_e = sb("bias_e", [P, E1, DC])
        bias_2 = sb("bias_2", [P, 2, DC])
        gbias = sb("gbias", [P, DC])
        yT = sb("yT", [P, 2, 512])
        oc = sb("oc", [P, C1, DC])
        oT = sb("oT", [P, 2, P])
        final = [sb(f"final{u}", [P, D]) for u in range(2)]

        W0 = ps("W0", [P, 512])
        W1 = ps("W1", [P, 512])
        W2 = ps("W2", [P, 512])
        S = ps("S", [P, 3, 512])
        Y = ps("Y", [P, 2, 512])
        SBANK = [0, 1, 2, 0]
        setup_banks = [W0[:], W1[:], W2[:], S[:, 0, :], S[:, 1, :]]
        ZEROED = 11

        names = """zeroed picked gather_turn x2_ready xa_ready edges_ready gT_done xaT_ready gH_done
            hx_ready ediag_ready gB_done score_ready leaky_ready masked_ready gshift_ready gexp_done gP_done
            gprobT_ready gV_done gout_ready xpad_ready res_ready T4_done xbd_ready xmh_ready xml_ready V_done vd_ready
            yT_done yT_ready w_done wk_ready proj_done oc_ready router_done rlog_read rshift_ready rexp_done
            gate_ready gbias_ready S_done oT_done oT_ready nparts_ready nT_done nmaxT_ready A_done exp_done
            out_done final_ready PT_done pT_ready PV_done yh_ready bias_step first_step r_step m_step max_step
            gmax_step y_step x_step""".split()
        s_ = {n: sem(n) for n in names}
        x1_in = [sem(f"x1_in{u}") for u in range(2)]
        adj_in = [sem(f"adj_in{u}") for u in range(2)]
        y_in = [sem(f"y_in{u}") for u in range(2)]
        out_out = [sem(f"out_out{u}") for u in range(2)]
        block = ctx.enter_context(nc.Block())

        def upto(tile, per=1, part=None):
            part = per if part is None else part
            if isinstance(tile, int):
                return 0 if tile < 0 else per * TILES if tile >= TILES else per * tile + part
            return per * tile + part

        def schedule(eng, step):
            for s in range(5):
                step(s, s // 4, s % 4)
            with eng.Fori(1, 15) as j:
                for q in range(1, 5):
                    step(4 * j + q, j, q)
            for s in range(61, TILES + 3):
                step(s, s // 4, s % 4)

        def runs(s, lag):
            return not isinstance(s, int) or 0 <= s - lag < TILES

        def half(j, q, lag):
            return 2 * j + (q - lag) // 2

        @block.sync
        def _(sp):
            def load_x1(n, u):
                wait(sp, s_["x2_ready"], upto(n - 2))
                sp.dma_start(x1[u][:], x1_t[:, bass.ds(n, 1), :]).then_inc(x1_in[u], 16)

            def load_adj(n, u):
                wait(sp, s_["edges_ready"], upto(n - 2))
                sp.dma_start(adj[u][:], adj_t[:, bass.ds(n, 1), :]).then_inc(adj_in[u], 16)

            def step(s, j, q):
                if runs(s, -3):
                    load_x1(s + 3, (q + 3) % 2)
                if runs(s, -2):
                    load_adj(s + 2, q % 2)
                if runs(s, 3):
                    sp.wait_ge(s_["final_ready"], upto(s - 3))
                    u = (q - 3) % 2
                    sp.dma_start(out_t[:, bass.ds(s - 3, 1), :], final[u][:]).then_inc(out_out[u], 16)

            for n in range(2):
                load_x1(n, n)
                load_adj(n, n)
            load_x1(2, 0)
            schedule(sp, step)
            for u in range(2):
                sp.wait_ge(out_out[u], 16 * (TILES // 2))

        @block.gpsimd
        def _(pool):
            def gather(n, h, u):
                wait(pool, s_["picked"], upto(n))
                pool_turn(pool, pool_pad, 1 + u).then_inc(s_["gather_turn"], 1)
                pool.indirect_dma_start(yin[u][:], None, A["y"],
                                        bass.IndirectOffsetOnAxis(ap=yrow[u][:], axis=0)).then_inc(y_in[u], 16)
                pool.wait_ge(y_in[u], 16 * (h + 1))

            def spread_ej(g):
                pool.wait_ge(s_["hx_ready"], upto(g, 2))
                wait(pool, s_["gB_done"], upto(g - 1))
                pool.tensor_tensor(ediag[:], e8[:, 1, :].unsqueeze(2).to_broadcast([P, HEADS, NODES]),
                                   w["node"][:].unsqueeze(1).to_broadcast([P, HEADS, NODES]),
                                   ALU.mult).then_inc(s_["ediag_ready"], 1)
                pool.wait_ge(s_["ediag_ready"], upto(g))

            def moving_x(a, u):
                pool.wait_ge(s_["xmh_ready"], upto(a))
                wait(pool, s_["w_done"], upto(a - 1, 4))
                for g in range(2):
                    r = slice(64 * g, 64 * g + 64)
                    ins = pool.tensor_tensor(xml[r], xbd[u][r, :, 64 * g:64 * g + 64], xmh[r].bitcast(F32), ALU.subtract)
                    ins.then_inc(s_["xml_ready"], 1)
                    pool.wait_ge(s_["xml_ready"], upto(a, 2, g + 1))

            def mask(g):
                pool.wait_ge(s_["leaky_ready"], upto(g))
                pool.wait_ge(s_["edges_ready"], upto(g))
                wait(pool, s_["gshift_ready"], upto(g - 1))
                pool.tensor_tensor(masked[:], leaky[:], edge[:].unsqueeze(1).to_broadcast([P, HEADS, NODES]),
                                   ALU.mult).then_inc(s_["m_step"], 1)
                pool.wait_ge(s_["m_step"], upto(g))
                pool.tensor_tensor(masked2[:], masked[:], noedge[:].unsqueeze(1).to_broadcast([P, HEADS, NODES]),
                                   ALU.add).then_inc(s_["masked_ready"], 1)
                pool.wait_ge(s_["masked_ready"], upto(g))

            def gate_biases(b, u):
                pool.wait_ge(s_["gate_ready"], upto(b))
                pool.tensor_tensor(bias_e[:], w["proj_b"][:], gate[u][:].unsqueeze(2).to_broadcast([P, E1, DC]),
                                   ALU.mult).then_inc(s_["bias_step"], 1)
                pool.wait_ge(s_["bias_step"], upto(b, 2, 1))
                pool.tensor_tensor(bias_2[:], bias_e[:, 0:2, :], bias_e[:, 2:4, :], ALU.add).then_inc(s_["bias_step"], 1)
                pool.wait_ge(s_["bias_step"], upto(b, 2))
                wait(pool, s_["oc_ready"], upto(b - 1))
                pool.tensor_tensor(gbias[:], bias_2[:, 0, :], bias_2[:, 1, :], ALU.add).then_inc(s_["gbias_ready"], 1)
                pool.wait_ge(s_["gbias_ready"], upto(b))

            def step(s, j, q):
                if runs(s, -2):
                    gather(s + 2, half(j, q, -2), q % 2)
                if runs(s, 0):
                    spread_ej(s)
                if runs(s, 1):
                    moving_x(s - 1, (q - 1) % 2)
                if runs(s, 0):
                    mask(s)
                if runs(s, 2):
                    gate_biases(s - 2, q % 2)

            vds = [vd[u][:].rearrange("p g c e k -> p (g c e) k") for u in range(2)]
            pool.memset(pool_pad[:], 0.0).then_inc(s_["zeroed"], 1)
            pool.wait_ge(s_["zeroed"], 1)
            gather(0, 0, 0)
            gather(1, 0, 1)
            for buf in (gprob, xpad, vd[0], vd[1], nparts):
                pool.memset(buf[:], 0.0).then_inc(s_["zeroed"], 1)
            pool.memset(hx[:], 1.0).then_inc(s_["zeroed"], 1)
            pool.wait_ge(s_["zeroed"], 7)
            for u in range(2):
                for h in range(2):
                    r = slice(64 * h, 64 * h + 64)
                    pool.memset(vds[u][r, :, V1 * h + DH:V1 * h + DH + 1], 1.0).then_inc(s_["zeroed"], 1)
            pool.wait_ge(s_["zeroed"], ZEROED)
            make_constants(pool, c, w, setup)
            schedule(pool, step)


        @block.tensor
        def _(pe):
            def free(name, tile, per=1, part=None):
                wait(pe, s_[name], upto(tile, per, part))

            def need(name, tile, per=1, part=None):
                wait(pe, s_[name], upto(tile, per, part))

            turn_weights(pe, c, raw1, setup_banks, setup)
            pe.wait_ge(s_["zeroed"], ZEROED)
            pe.wait_ge(setup["made"], MADE)
            pe.wait_ge(setup["weights"], 1)

            def turn_xa(g, u):
                need("xa_ready", g)
                free("gout_ready", g - 1)
                for ic in range(2):
                    ins = pe.transpose(W2[:, ic * P:(ic + 1) * P], xa[u][:, ic * P:(ic + 1) * P], ident[:])
                ins.then_inc(s_["gT_done"], 1)

            def turn_xpad(a):
                need("xpad_ready", a)
                free("yT_ready", a - 2, 2, 1)
                free("pT_ready", a - 2, 4)
                for ch in range(C1):
                    ins = pe.transpose(W0[:, ch * P:(ch + 1) * P], xpad[:, ch, :], ident[:])
                ins.then_inc(s_["T4_done"], 1)

            def values(a, part, u):
                bank = (W0, W1)[part]
                if part == 0:
                    need("xbd_ready", a)
                else:
                    free("nmaxT_ready", a - 1, 2, 1)
                    free("yT_ready", a - 2, 2)
                for q in range(2):
                    ins = pe.matmul(bank[:, q * D:q * D + D], xbd[u][:, 2 * part + q, :], w["val_w"][:],
                                    start=True, stop=True)
                ins.then_inc(s_["V_done"], 1)

            def turn_y(r, part):
                need("yh_ready", r, 2)
                if part == 0:
                    free("pT_ready", r, 4)
                    bank = W0
                else:
                    free("pT_ready", r, 4, 3)
                    bank = W1
                for q in range(4):
                    ch, k = 2 * part + q // 2, q % 2
                    ins = pe.transpose(bank[:, q * P:(q + 1) * P],
                                       yh[:, ch, 2 * k:2 * k + 2].rearrange("p e h d -> p (e h d)"), ident[:])
                ins.then_inc(s_["yT_done"], 1)

            def att_keys(a, k):
                if k == 0:
                    need("xml_ready", a, 2)
                    free("score_ready", a + 1)
                elif k == 1:
                    free("pT_ready", a - 1, 4, 1)
                    free("vd_ready", a, 2, 1)
                elif k == 2:
                    free("pT_ready", a - 1, 4, 2)
                    free("vd_ready", a, 2)
                else:
                    free("wk_ready", a, 4, 2)
                bank = (W2, W0, W1, W0)[k]
                for e in range(2):
                    ins = mm3(pe, bank[:, e * 256:(e + 1) * 256],
                              (w["att_h"][:, 2 * k + e, :], w["att_l"][:, 2 * k + e, :]),
                              (xmh[:].rearrange("p c m -> p (c m)"), xml[:].rearrange("p c m -> p (c m)")))
                ins.then_inc(s_["w_done"], 1)

            def project(r):
                need("yT_ready", r, 2)
                free("yh_ready", r, 2)
                for ch in range(C1):
                    for k in range(2):
                        q = 2 * (ch % 2) + k
                        ins = pe.matmul(Y[:, 1, ch * DC:(ch + 1) * DC], yT[:, ch // 2, q * P:(q + 1) * P],
                                        w["proj_w"][:, k, :], start=(k == 0), stop=(k == 1))
                ins.then_inc(s_["proj_done"], 1)

            def route(a, u):
                free("final_ready", a - 2)
                for ch in range(C1):
                    ins = pe.matmul(Y[:, 1, 0:E1], xbd[u][:, ch, :], w["router_w"][:, ch, :], start=(ch == 0),
                                    stop=(ch == C1 - 1))
                ins.then_inc(s_["router_done"], 1)

            def scores(b, ch, u):
                if ch == 0:
                    need("wk_ready", b, 4)
                    free("exp_done", b - 1, 4)
                elif ch < 3:
                    free("exp_done", b - 1, 4, ch + 1)
                else:
                    free("exp_done", b, 4, 1)
                pe.matmul(S[:, SBANK[ch], :], xbd[u][:, ch, :], wk[:, ch].rearrange("p e m -> p (e m)"),
                          start=True, stop=False, skip_group_check=True).then_inc(s_["S_done"], 1)

            def turn_oc(r):
                need("oc_ready", r)
                free("yh_ready", r, 2)
                for k in range(2):
                    ins = pe.transpose(Y[:, 0, k * P:(k + 1) * P],
                                       oc[:].rearrange("p c o -> p (c o)")[:, k * P:(k + 1) * P], ident[:])
                ins.then_inc(s_["oT_done"], 1)

            def graph_h(g):
                need("xaT_ready", g)
                for ic in range(2):
                    ins = pe.matmul(W2[:, 0:D + 2 * HEADS], xaT[:, ic, :], w["gat_w"][:, ic, :], start=(ic == 0),
                                    stop=(ic == 1))
                ins.then_inc(s_["gH_done"], 1)

            def turn_max(b, part):
                need("nparts_ready", b, 2, part + 1)
                if part == 0:
                    free("yT_ready", b - 1, 2)
                    free("pT_ready", b - 1, 4, 3)
                    out = W1[:, 0:64]
                else:
                    free("oT_ready", b - 1)
                    out = Y[:, 0, 0:64]
                pe.transpose(out.bitcast(BF16), nparts[:].rearrange("p k m -> p (k m)"),
                             ident_bf[:]).then_inc(s_["nT_done"], 1)

            def subtract_max(b, part):
                need("nmaxT_ready", b, 2, part + 1)
                for k in range(2):
                    pe.matmul(S[:, SBANK[2 * part + k], :], nmaxT[:], w["spread"][:, k].rearrange("r e m -> r (e m)"),
                              start=False, stop=True, skip_group_check=True).then_inc(s_["A_done"], 1)

            def out_project(r):
                need("oT_ready", r)
                free("oc_ready", r)
                for k in range(2):
                    ins = pe.matmul(Y[:, 1, 0:D], oT[:, k, :], w["out_w"][:, k, :], start=(k == 0), stop=(k == 1))
                ins.then_inc(s_["out_done"], 1)

            def graph_ej(g):
                need("ediag_ready", g)
                free("hx_ready", g, 2)
                pe.matmul(W2[:, 0:HEADS * NODES], w["same_graph"][:], ediag[:].rearrange("p h m -> p (h m)"),
                          start=True, stop=True).then_inc(s_["gB_done"], 1)

            def turn_probs(b, ch):
                need("exp_done", b, 4, ch + 1)
                if ch == 0:
                    free("vd_ready", b + 1, 2, 1)
                    bank = W0
                elif ch == 1:
                    free("vd_ready", b + 1, 2)
                    bank = W1
                elif ch == 2:
                    free("wk_ready", b + 1, 4, 3)
                    free("pT_ready", b, 4, 2)
                    bank = W1
                else:
                    free("wk_ready", b + 1, 4)
                    free("pT_ready", b, 4, 1)
                    bank = W0
                for e in range(E1):
                    ins = pe.transpose(bank[:, e * P:(e + 1) * P], pex[ch % 2][:, e, :], ident[:])
                ins.then_inc(s_["PT_done"], 1)

            def head_out(b, ch, u):
                need("pT_ready", b, 4, ch + 1)
                if ch == 0:
                    need("vd_ready", b, 2)
                    free("nmaxT_ready", b, 2)
                    free("yh_ready", b - 1, 2)
                elif ch == 1:
                    free("rlog_read", b + 1)
                    free("final_ready", b - 1)
                    free("yh_ready", b - 1, 2)
                else:
                    free("yh_ready", b, 2, 1)
                for e in range(E1):
                    for g in range(2):
                        r = slice(64 * g, 64 * g + 64)
                        ins = pe.matmul(Y[r, ch % 2, e * 2 * V1:(e + 1) * 2 * V1], pT[ch % 2][:, e, r],
                                        vd[u][:, g, ch, e, :], start=True, stop=True)
                ins.then_inc(s_["PV_done"], 1)

            def turn_graph_prob(g):
                need("gexp_done", g)
                free("wk_ready", g - 1, 4, 1)
                free("score_ready", g)
                for h in range(HEADS):
                    ins = pe.transpose(W2[:, h * P:(h + 1) * P], gprob[:, h, :], ident[:])
                ins.then_inc(s_["gP_done"], 1)

            def graph_out(g):
                need("gprobT_ready", g)
                for h in range(HEADS):
                    ins = pe.matmul(W2[:, h * (DC + 2):(h + 1) * (DC + 2)], gprobT[:, h, :], hx[:, h, :],
                                    start=True, stop=True)
                ins.then_inc(s_["gV_done"], 1)

            def step(s, j, q):
                graph, prep, head, out = runs(s, 0), runs(s, 1), runs(s, 2), runs(s, 3)
                g, a, b, r = s, s - 1, s - 2, s - 3
                u, v = q % 2, (q - 1) % 2
                if head:
                    scores(b, 0, u)
                    scores(b, 1, u)
                if graph:
                    turn_xa(g, u)
                if head:
                    scores(b, 2, u)
                if graph:
                    graph_h(g)
                if out:
                    turn_y(r, 0)
                    turn_y(r, 1)
                if prep:
                    turn_xpad(a)
                if out:
                    project(r)
                if head:
                    turn_max(b, 0)
                if prep:
                    values(a, 0, v)
                if head:
                    subtract_max(b, 0)
                if out:
                    turn_oc(r)
                if graph:
                    graph_ej(g)
                if prep:
                    values(a, 1, v)
                if head:
                    scores(b, 3, u)
                    turn_probs(b, 0)
                if prep:
                    att_keys(a, 0)
                if out:
                    out_project(r)
                if head:
                    turn_max(b, 1)
                    turn_probs(b, 1)
                    head_out(b, 0, u)
                if prep:
                    route(a, v)
                    att_keys(a, 1)
                if graph:
                    turn_graph_prob(g)
                if head:
                    head_out(b, 1, u)
                    subtract_max(b, 1)
                if graph:
                    graph_out(g)
                if prep:
                    att_keys(a, 2)
                    att_keys(a, 3)
                if head:
                    turn_probs(b, 2)
                    turn_probs(b, 3)
                    head_out(b, 2, u)
                    head_out(b, 3, u)

            schedule(pe, step)

        @block.scalar
        def _(act):
            def need(name, tile, per=1, part=None):
                wait(act, s_[name], upto(tile, per, part))

            free = need
            act.wait_ge(s_["zeroed"], ZEROED)

            def copy_xaT(g):
                need("gT_done", g)
                free("gH_done", g - 1)
                act.activation(xaT[:], W2[:, 0:D].rearrange("p (c m) -> p c m", c=2), ACT.Copy).then_inc(s_["xaT_ready"], 1)

            def copy_yT(r, part):
                need("yT_done", r, 2, part + 1)
                free("proj_done", r - 1)
                act.activation(yT[:, part, :], (W0, W1)[part][:], ACT.Copy).then_inc(s_["yT_ready"], 1)

            def split_x(a, u):
                need("xbd_ready", a)
                free("w_done", a - 1, 4)
                free("xml_ready", a - 1, 2)
                for g in range(2):
                    r = slice(64 * g, 64 * g + 64)
                    ins = act.activation(xmh[r], xbd[u][r, :, 64 * g:64 * g + 64], ACT.Copy)
                ins.then_inc(s_["xmh_ready"], 1)

            def place_values(a, part, u):
                need("V_done", a, 2, part + 1)
                free("PV_done", a - 2, 4)
                src = (W0, W1)[part][:].rearrange("p (c e h k) -> p (c e) h k", c=2, e=E1, h=2)
                for g in range(2):
                    for h in range(2):
                        dst = vd[u][64 * h:64 * h + 64, g, 2 * part:2 * part + 2].rearrange("p c e k -> p (c e) k")
                        ins = act.activation(dst[:, :, V1 * h:V1 * h + DH], src[64 * g:64 * g + 64, :, h, :], ACT.Copy)
                ins.then_inc(s_["vd_ready"], 1)

            def copy_keys(a, k):
                need("w_done", a, 4, k + 1)
                if k == 0:
                    free("S_done", a - 1, 4)
                act.activation(wk[:, :, 2 * k:2 * k + 2, :].rearrange("p c e m -> p e c m"),
                               (W2, W0, W1, W0)[k][:].rearrange("p (e c m) -> p e c m", e=2, c=C1), ACT.Copy)\
                   .then_inc(s_["wk_ready"], 1)

            def route_exp(a):
                need("rshift_ready", a)
                free("gate_ready", a - 1)
                act.activation(rexp[:], rlog[:], ACT.Exp).then_inc(s_["rexp_done"], 1)

            def copy_oT(r):
                need("oT_done", r)
                free("out_done", r - 1)
                act.activation(oT[:], Y[:, 0, 0:D].rearrange("p (c m) -> p c m", c=2), ACT.Copy).then_inc(s_["oT_ready"], 1)

            def copy_h(g):
                need("gH_done", g)
                free("gV_done", g - 1)
                free("ediag_ready", g - 1)
                free("score_ready", g - 1)
                act.activation(hx[:, :, 0:DC], W2[:, 0:D].rearrange("p (h d) -> p h d", h=HEADS), ACT.Copy).then_inc(s_["hx_ready"], 1)
                act.activation(e8[:], W2[:, D:D + 2 * HEADS].rearrange("p (k h) -> p k h", k=2), ACT.Copy).then_inc(s_["hx_ready"], 1)

            def copy_max(b, part):
                need("nT_done", b, 2, part + 1)
                if part:
                    free("A_done", b, 4, 2)
                    src = Y[0:48, 0, 0:64]
                else:
                    free("A_done", b - 1, 4)
                    src = W1[0:48, 0:64]
                act.activation(nmaxT[:], src.bitcast(BF16), ACT.Copy).then_inc(s_["nmaxT_ready"], 1)

            def head_exp(b, ch):
                need("A_done", b, 4, ch + 1)
                if ch < 2:
                    free("PT_done", b - 1, 4, ch + 3)
                else:
                    free("PT_done", b, 4, ch - 1)
                act.activation(pex[ch % 2][:], S[:, SBANK[ch], :].rearrange("p (e m) -> p e m", e=E1), ACT.Exp)\
                   .then_inc(s_["exp_done"], 1)

            def copy_pT(b, ch):
                need("PT_done", b, 4, ch + 1)
                if ch < 2:
                    free("PV_done", b - 1, 4, ch + 3)
                else:
                    free("PV_done", b, 4, ch - 1)
                act.activation(pT[ch % 2][:], (W0, W1, W1, W0)[ch][:].rearrange("p (e m) -> p e m", e=E1), ACT.Copy)\
                   .then_inc(s_["pT_ready"], 1)

            def graph_exp(g):
                need("gshift_ready", g)
                free("gP_done", g - 1)
                for k in range(2):
                    r = slice(64 * k, 64 * k + 64)
                    ins = act.activation(gprob[r, :, r], gshift[r], ACT.Exp)
                ins.then_inc(s_["gexp_done"], 1)

            def copy_graph_probT(g):
                need("gP_done", g)
                free("gV_done", g - 1)
                act.activation(gprobT[:], W2[:].rearrange("p (h m) -> p h m", h=HEADS), ACT.Copy).then_inc(s_["gprobT_ready"], 1)

            def step(s, j, q):
                graph, prep, head, out = runs(s, 0), runs(s, 1), runs(s, 2), runs(s, 3)
                g, a, b, r = s, s - 1, s - 2, s - 3
                v = (q - 1) % 2
                if graph:
                    copy_xaT(g)
                    copy_h(g)
                if out:
                    copy_yT(r, 0)
                    copy_yT(r, 1)
                if head:
                    copy_max(b, 0)
                if prep:
                    split_x(a, v)
                if head:
                    head_exp(b, 0)
                    head_exp(b, 1)
                if prep:
                    place_values(a, 0, v)
                if out:
                    copy_oT(r)
                if prep:
                    place_values(a, 1, v)
                if head:
                    copy_pT(b, 0)
                if prep:
                    copy_keys(a, 0)
                if head:
                    copy_max(b, 1)
                    copy_pT(b, 1)
                if graph:
                    graph_exp(g)
                if prep:
                    route_exp(a)
                if graph:
                    copy_graph_probT(g)
                if prep:
                    copy_keys(a, 1)
                if head:
                    head_exp(b, 2)
                    head_exp(b, 3)
                if prep:
                    copy_keys(a, 2)
                    copy_keys(a, 3)
                if head:
                    copy_pT(b, 2)
                    copy_pT(b, 3)

            schedule(act, step)

        @block.vector
        def _(dve):
            def need(name, tile, per=1, part=None):
                wait(dve, s_[name], upto(tile, per, part))

            free = need

            def pick(n, u):
                free("x2_ready", n - 2)
                free("gather_turn", n - 2)
                dve.tensor_copy(prob[u][:], c["prob"][:, bass.ds(n, 1)])
                dve.tensor_copy(yrow[u][:], c["yrow"][:, bass.ds(n, 1)]).then_inc(s_["picked"], 1)

            def add_expert(n, h, i):
                u = i % 2
                dve.wait_ge(x1_in[u], 16 * (h + 1))
                dve.wait_ge(y_in[u], 16 * (h + 1))
                free("xpad_ready", n - 4)
                return dve.scalar_tensor_tensor(x2[i][:], yin[u][:], prob[u][:], x1[u][:], ALU.mult, ALU.add)\
                          .then_inc(s_["x2_ready"], 1)

            def norm_expert(n, i):
                free("gT_done", n - 2)
                dve.tensor_scalar(xa[i % 2][:], x2[i][:], mv[:, 0, 0:1], factor[:, 0:1].bitcast(F32),
                                  ALU.subtract, ALU.mult).then_inc(s_["xa_ready"], 1)

            def first_norms():
                st = Steps(dve, s_["first_step"], 0)
                for n in range(2):
                    add_expert(n, 0, n)
                    need("x2_ready", n)
                    st.link(dve.bn_stats(stats[:, 0, :], x2[n][:]))
                    dve.memset(dve_pad[:], 0.0)
                    st.link(dve.bn_aggr(mv[:, 0, :], stats[:, 0, :]))
                    st.link(dve.tensor_scalar(rs_var[:, 0:1], mv[:, 0, 1:2], EPS, None, ALU.add))
                    rsqrt(dve, st, rs_var[:, 0:1], factor[:, 0:1], rs_tmp[:, 0:1])
                    norm_expert(n, n)
                    need("xa_ready", n)

            def copy_x(a, u):
                need("T4_done", a)
                free("S_done", a - 2, 4)
                dve.tensor_tensor(xbd[u][:], W0[:].rearrange("p (c m) -> p c m", c=C1),
                                  w["norm_w"][:].unsqueeze(2).to_broadcast([P, C1, P]), ALU.mult).then_inc(s_["xbd_ready"], 1)

            def add_bias(r):
                need("proj_done", r)
                need("gbias_ready", r)
                free("oT_done", r - 1)
                dve.tensor_tensor(oc[:], Y[:, 1, 0:D].rearrange("p (c o) -> p c o", c=C1),
                                  gbias[:].unsqueeze(1).to_broadcast([P, C1, DC]), ALU.add).then_inc(s_["oc_ready"], 1)

            R_LINKS = 3

            def route_shift(a):
                st = Steps(dve, s_["r_step"], R_LINKS * a)
                need("router_done", a)
                dve.tensor_tensor(rlog[:], Y[:, 1, 0:E1], w["router_b"][:], ALU.add).then_inc(s_["rlog_read"], 1)
                need("rlog_read", a)
                st.link(dve.tensor_reduce(rmax[:], rlog[:], AX.X, ALU.max))
                dve.tensor_scalar(rlog[:], rlog[:], rmax[:], None, ALU.subtract).then_inc(s_["rshift_ready"], 1)
                return st

            def route_gate(a, st, u):
                need("rexp_done", a)
                st.link(dve.tensor_reduce(rsum[:], rexp[:], AX.X, ALU.add))
                st.link(dve.reciprocal(rsum[:], rsum[:]))
                free("bias_step", a - 2, 2, 1)
                dve.tensor_scalar(gate[u][:], rexp[:], rsum[:], None, ALU.mult).then_inc(s_["gate_ready"], 1)
                assert st.n == R_LINKS

            def head_max(b, ch):
                need("S_done", b, 4, ch + 1)
                return dve.tensor_reduce(nmax[:, (ch % 2) * EH:(ch % 2) * EH + EH],
                                         S[:, SBANK[ch], :].rearrange("p (e m) -> p e m", e=EH), AX.X, ALU.max)

            MAX_LINKS = 3

            def max_parts(b, part):
                st = Steps(dve, s_["max_step"], 2 * MAX_LINKS * b + MAX_LINKS * part)
                head_max(b, 2 * part)
                st.link(head_max(b, 2 * part + 1))
                if part:
                    free("nT_done", b, 2, 1)
                else:
                    free("nT_done", b - 1, 2)
                st.link(dve.tensor_scalar(nparts[:, 0, :], nmax[:], -1.0, None, ALU.mult))
                dve.scalar_tensor_tensor(nrest[:], nmax[:], -1.0, nparts[:, 0, :], ALU.mult, ALU.subtract)
                st.link(dve.scalar_tensor_tensor(nparts[:, 1, :], nmax[:], -1.0, nparts[:, 0, :], ALU.mult, ALU.subtract))
                dve.tensor_tensor(nparts[:, 2, :], nrest[:], nparts[:, 1, :], ALU.subtract).then_inc(s_["nparts_ready"], 1)
                need("nparts_ready", b, 2, part + 1)
                assert st.n == MAX_LINKS

            def finish(r, h, u, i):
                need("out_done", r)
                wait(dve, out_out[u], 16 * h)
                dve.tensor_tensor(final[u][:], Y[:, 1, 0:D], x3[i][:], ALU.add).then_inc(s_["final_ready"], 1)

            def edges(g, h, u):
                dve.wait_ge(adj_in[u], 16 * (h + 1))
                free("masked_ready", g - 1)
                dve.tensor_scalar(edge[:], adj[u][:], 0.0, None, ALU.is_gt)
                dve.tensor_scalar(noedge[:], adj[u][:], 0.0, NEG, ALU.is_le, ALU.mult).then_inc(s_["edges_ready"], 1)

            def graph_scores(g):
                need("gB_done", g)
                dve.tensor_tensor(score[:], W2[:, 0:HEADS * NODES].rearrange("p (h m) -> p h m", h=HEADS),
                                  e8[:, 0, :].unsqueeze(2).to_broadcast([P, HEADS, NODES]), ALU.add).then_inc(s_["score_ready"], 1)
                need("score_ready", g)
                free("m_step", g - 1)
                dve.scalar_tensor_tensor(leaky[:], score[:], SLOPE, score[:], ALU.mult, ALU.max).then_inc(s_["leaky_ready"], 1)

            def graph_shift(g):
                need("masked_ready", g)
                dve.tensor_reduce(gmax[:], masked2[:], AX.X, ALU.max).then_inc(s_["gmax_step"], 1)
                need("gmax_step", g)
                free("gexp_done", g - 1)
                dve.tensor_tensor(gshift[:], masked2[:], gmax[:].unsqueeze(2).to_broadcast([P, HEADS, NODES]),
                                  ALU.subtract).then_inc(s_["gshift_ready"], 1)

            def head_rows(b, part):
                need("PV_done", b, 4, 2 * part + 2)
                v = Y[:, :, 0:E1 * 2 * V1].rearrange("p c (e k) -> p c e k", k=V1)
                dve.reciprocal(den[:].unsqueeze(3), v[:, :, :, DH:V1]).then_inc(s_["y_step"], 1)

            def head_factors(b, part, u):
                if part == 0:
                    need("gate_ready", b)
                need("y_step", b, 4, 2 * part + 1)
                dve.tensor_tensor(fac[:], den[:].rearrange("p c (e h) -> p c e h", h=2),
                                  gate[u][:].unsqueeze(1).unsqueeze(3).to_broadcast([P, 2, E1, 2]),
                                  ALU.mult).then_inc(s_["y_step"], 1)

            def scale_heads(b, part):
                if part == 0:
                    free("yT_done", b - 1, 2)
                need("y_step", b, 4, 2 * part + 2)
                v = Y[:, :, 0:E1 * 2 * V1].rearrange("p c (e k) -> p c e k", k=V1)
                dve.tensor_tensor(yh[:, 2 * part:2 * part + 2].rearrange("p c e h d -> p c (e h) d"), v[:, :, :, 0:DH],
                                  fac[:].rearrange("p c e h -> p c (e h)").unsqueeze(3).to_broadcast([P, 2, EH, DH]),
                                  ALU.mult).then_inc(s_["yh_ready"], 1)

            X_LINKS = 6 + RSQRT_LINKS

            def graph_sum(s, j, q):
                g, b, i, ahead, head = s, s - 2, q % 4, runs(s, -2), runs(s, 2)
                k = (q + 2) % 4
                st = Steps(dve, s_["x_step"], X_LINKS * g)
                if ahead:
                    add_expert(s + 2, half(j, q, -2), k)
                need("gV_done", g)
                v = W2[:, 0:HEADS * (DC + 2)].rearrange("p (h k) -> p h k", h=HEADS)
                st.link(dve.reciprocal(gsum[:].unsqueeze(2), v[:, :, DC:DC + 1]))
                if ahead:
                    dve.bn_stats(stats[:, 0, :], x2[k][:])
                dve.tensor_tensor(gout[:], v[:, :, 0:DC], gsum[:].unsqueeze(2).to_broadcast([P, HEADS, DC]),
                                  ALU.mult).then_inc(s_["gout_ready"], 1)
                need("gout_ready", g)
                st.link(dve.tensor_tensor(x3n[:], gout[:].rearrange("p h d -> p (h d)"), x2[i][:], ALU.add))
                st.link(dve.bn_stats(stats[:, 1, :], x3n[:]))
                dve.memset(dve_pad[:], 0.0)
                if ahead:
                    dve.bn_aggr(mv[:, 0, :], stats[:, 0, :])
                st.link(dve.bn_aggr(mv[:, 1, :], stats[:, 1, :]))
                if ahead:
                    dve.tensor_scalar(rs_var[:, 0:2], mv[:, :, 1], EPS, None, ALU.add)
                else:
                    dve.tensor_scalar(rs_var[:, 1:2], mv[:, 1, 1:2], EPS, None, ALU.add)
                st.link(dve.tensor_scalar(rs_var[:, 2:3], mv[:, 1, 1:2], 1.0 + EPS, EPS * EPS, ALU.mult, ALU.add))
                cols = slice(0 if ahead else 1, 3)
                newton = (dve, st, rs_var[:, cols], factor[:, cols], rs_tmp[:, cols])
                rsqrt_seed(dve, st, rs_var[:, cols], factor[:, cols])
                rsqrt_newton(*newton)
                if head:
                    head_rows(b, 1)
                rsqrt_newton(*newton)
                if head:
                    head_factors(b, 1, q % 2)
                    scale_heads(b, 1)
                rsqrt_newton(*newton)
                free("T4_done", g - 1)
                for m in range(2):
                    r = slice(64 * m, 64 * m + 64)
                    ins = dve.tensor_scalar(xpad[r, :, r], x3n[r, :].rearrange("p (c d) -> p c d", c=C1),
                                            mv[r, 1, 0:1], factor[r, 2:3].bitcast(F32), ALU.subtract, ALU.mult)
                ins.then_inc(s_["xpad_ready"], 1)
                dve.tensor_scalar(res_scale[:, 0:1], factor[:, 1:2].bitcast(F32), 1.0, None, ALU.add)
                st.link(dve.tensor_tensor(res_scale[:, 1:2], factor[:, 1:2].bitcast(F32), mv[:, 1, 0:1], ALU.mult))
                if ahead:
                    norm_expert(s + 2, k)
                free("final_ready", g - 4)
                dve.tensor_scalar(x3[i][:], x3n[:], res_scale[:, 0:1], res_scale[:, 1:2], ALU.mult, ALU.subtract).then_inc(s_["res_ready"], 1)
                assert st.n == X_LINKS

            def step(s, j, q):
                graph, prep, head, out = runs(s, 0), runs(s, 1), runs(s, 2), runs(s, 3)
                g, a, b, r = s, s - 1, s - 2, s - 3
                u, v = q % 2, (q - 1) % 2
                if runs(s, -3):
                    pick(s + 3, (q + 3) % 2)
                if head:
                    max_parts(b, 0)
                if prep:
                    copy_x(a, v)
                if out:
                    add_bias(r)
                if graph:
                    edges(g, half(j, q, 0), u)
                    graph_scores(g)
                if head:
                    max_parts(b, 1)
                if graph:
                    graph_shift(g)
                if out:
                    finish(r, half(j, q, 3), v, (q - 3) % 4)
                if prep:
                    st = route_shift(a)
                    route_gate(a, st, v)
                if head:
                    head_rows(b, 0)
                    head_factors(b, 0, u)
                    scale_heads(b, 0)
                if graph:
                    graph_sum(s, j, q)
                elif head:
                    head_rows(b, 1)
                    head_factors(b, 1, u)
                    scale_heads(b, 1)

            pick(0, 0)
            pick(1, 1)
            finish_weights(dve, w, raw1, setup_banks, setup)
            first_norms()
            pick(2, 0)
            dve.wait_ge(s_["zeroed"], ZEROED)
            schedule(dve, step)


_INS = ["x", "adj", "L0_gnn_weight", "L0_gnn_bias", "L0_ffn_W1", "L0_ffn_b1", "L0_ffn_Wg", "L0_ffn_bg", "L0_ffn_Wd",
        "L0_ffn_bd", "L1_gnn_W", "L1_gnn_a", "L1_ffn_norm_w", "L1_ffn_router_w", "L1_ffn_router_b", "L1_ffn_qkv_w",
        "L1_ffn_proj_w", "L1_ffn_proj_b", "L1_ffn_out_w"]
_SHORT = ["x", "adj", "w0", "bias0", "w1", "b1", "wg", "bg", "wd", "bd", "gat_w", "gat_a", "norm_w", "router_w",
          "router_b", "qkv_w", "proj_w", "proj_b", "out_w"]


def program(nc, A):
    with ExitStack() as ctx:
        def sb(name, shape, dt=F32):
            return ctx.enter_context(nc.sbuf_tensor(name, shape, dt))

        def sem(name):
            return ctx.enter_context(nc.semaphore(name))

        with ExitStack() as layer0:
            c = place_shared(sb)
            wd_offset = (nc.sbuf_base + 31) // 32 * 32
            wd_raw = layer0.enter_context(nc.sbuf_tensor("wd_raw", [P, KH, E0 * D], F32))
            c["wd_offset"] = wd_offset
            layer0a(nc, c, A, wd_raw)
            plan_slots(nc, c)
            raw1 = RawWeights(nc, sem("raw1_loaded"))
            layer0b(nc, c, A, wd_raw, raw1)
        w, setup = place_layer1(raw1, sb, sem)
        layer1(nc, c, w, setup, raw1, A)


def kernel(**inputs):
    import numpy as _np
    import concourse.bacc as _bacc
    from concourse import mybir as _mybir
    from concourse.bass_utils import run_bass_kernel_spmd as _run

    nc = _bacc.Bacc("TRN2", target_bir_lowering=False, num_devices=1)
    arrays, A = {}, {}
    for name, short in zip(_INS, _SHORT):
        a = _np.ascontiguousarray(inputs[name])
        arrays[f"in_{name}"] = a
        A[short] = nc.dram_tensor(f"in_{name}", a.shape, _mybir.dt.from_np(a.dtype), kind="ExternalInput").ap()
    A["out"] = nc.dram_tensor("out_0", (2 * TILES, NODES, D), F32, kind="ExternalOutput").ap()
    for name, shape, dt in (("x1", (TOKENS, D), F32), ("xn", (TOKENS, D), F32), ("table", (E0 * TOKENS, 1), I32),
                            ("y", (SLOTS * P, D), F32)):
        A[name] = nc.dram_tensor("scratch_" + name, shape, dt, kind="Internal").ap()
    program(nc, A)
    r = _run(nc, [arrays], core_ids=[0])
    return r.results[0]["out_0"]
```
